# Optimizing a Trainium2 kernel written in Bass

```python
import numpy as np
import jax
import jax.numpy as jnp

def _softmax(x, axis=-1):
    return jax.nn.softmax(x, axis=axis)

def _gelu(x):
    return jax.nn.gelu(x, approximate=True)

def _silu(x):
    return jax.nn.silu(x)

def _sigmoid(x):
    return jax.nn.sigmoid(x)

def _layernorm(x, axis=-1, eps=1e-05):
    m = jnp.mean(x, axis=axis, keepdims=True)
    v = jnp.var(x, axis=axis, keepdims=True)
    return (x - m) / jnp.sqrt(v + eps)

def _scatter_add(tgt, idx, src, axis=0):
    return tgt.at[idx].add(src)

def _segment_sum(src, seg, n):
    return jax.ops.segment_sum(src, seg, n)
kernel_name = 'mk_seq_postln_d2_jaxref_r8_158de6'

def setup_inputs(seed: int=0):
    np.random.seed(seed)
    _w = jnp.asarray

    def _L0_attn_setup():
        import jax, jax.numpy as jnp
        import numpy as np
        N_HEAD = 16
        POWER = 4
        key = jax.random.key(seed)
        k0, k1, k2 = jax.random.split(key, 3)
        B, T, C = (2, 256, 128)
        x = jax.random.normal(k0, (B, T, C), dtype=jnp.float32)
        W_attn = jax.random.normal(k1, (C, 3 * C), dtype=jnp.float32) * 0.02
        b_attn = jnp.zeros((3 * C,), dtype=jnp.float32)
        W_proj = jax.random.normal(k2, (C, C), dtype=jnp.float32) * 0.02
        b_proj = jnp.zeros((C,), dtype=jnp.float32)
        score_gain = jnp.asarray(4.0, dtype=jnp.float32)
        return {'x': x, 'W_attn': W_attn, 'b_attn': b_attn, 'W_proj': W_proj, 'b_proj': b_proj, 'score_gain': score_gain}
    _L0_attn_in = _L0_attn_setup()

    def _L0_ffn_setup():
        import jax, jax.numpy as jnp
        import numpy as np
        E = 16
        F_C = 2.0
        D = 128
        I = 4 * D
        IS = 2 * D
        B, S = (4, 128)
        key = jax.random.key(seed)
        ks = jax.random.split(key, 8)
        w = 0.02
        return {'hidden_states': jax.random.normal(ks[0], (B, S, D), dtype=jnp.float32), 'gate_w': jax.random.normal(ks[1], (E, D), dtype=jnp.float32) * w, 'Wg': jax.random.normal(ks[2], (E, I, D), dtype=jnp.float32) * w, 'Wu': jax.random.normal(ks[3], (E, I, D), dtype=jnp.float32) * w, 'Wd': jax.random.normal(ks[4], (E, D, I), dtype=jnp.float32) * w, 'Sg': jax.random.normal(ks[5], (IS, D), dtype=jnp.float32) * w, 'Su': jax.random.normal(ks[6], (IS, D), dtype=jnp.float32) * w, 'Sd': jax.random.normal(ks[7], (D, IS), dtype=jnp.float32) * w}
    _L0_ffn_in = _L0_ffn_setup()

    def _L1_attn_setup():
        import math
        import jax, jax.numpy as jnp
        import numpy as np
        D_MODEL = 128
        N_HEADS = 16
        D_K = D_MODEL // N_HEADS
        D_C = 32
        B, S = (2, 256)
        key = jax.random.key(seed)
        ks = jax.random.split(key, 7)
        sd = lambda fan_in: 1.0 / math.sqrt(fan_in)
        return {'x': jax.random.normal(ks[0], (B, S, D_MODEL), dtype=jnp.float32), 'W_dq': jax.random.uniform(ks[1], (D_MODEL, D_C), minval=-sd(D_MODEL), maxval=sd(D_MODEL), dtype=jnp.float32), 'W_uq': jax.random.uniform(ks[2], (D_C, N_HEADS * D_K), minval=-sd(D_C), maxval=sd(D_C), dtype=jnp.float32), 'W_dkv': jax.random.uniform(ks[3], (D_MODEL, D_C), minval=-sd(D_MODEL), maxval=sd(D_MODEL), dtype=jnp.float32), 'W_uk': jax.random.uniform(ks[4], (D_C, N_HEADS * D_K), minval=-sd(D_C), maxval=sd(D_C), dtype=jnp.float32), 'W_uv': jax.random.uniform(ks[5], (D_C, N_HEADS * D_K), minval=-sd(D_C), maxval=sd(D_C), dtype=jnp.float32), 'W_o': jax.random.uniform(ks[6], (N_HEADS * D_K, D_MODEL), minval=-sd(N_HEADS * D_K), maxval=sd(N_HEADS * D_K), dtype=jnp.float32)}
    _L1_attn_in = _L1_attn_setup()

    def _L1_ffn_setup():
        import jax, jax.numpy as jnp
        import numpy as np
        B, S, D, F, E, K = (4, 256, 128, 256, 8, 2)
        key = jax.random.key(seed)
        k0, k1, k2, k3, k4 = jax.random.split(key, 5)
        sD = 1.0 / np.sqrt(D).astype(np.float32)
        sF = 1.0 / np.sqrt(F).astype(np.float32)
        return {'hidden_states': jax.random.normal(k0, (B, S, D), jnp.float32), 'Wg': jax.random.normal(k1, (D, E), jnp.float32) * sD, 'W1': jax.random.normal(k2, (E, D, F), jnp.float32) * sD, 'W3': jax.random.normal(k3, (E, D, F), jnp.float32) * sD, 'W2': jax.random.normal(k4, (E, F, D), jnp.float32) * sF}
    _L1_ffn_in = _L1_ffn_setup()
    _d = {'L0_attn_x': _L0_attn_in['x'], 'L0_attn_W_attn': _L0_attn_in['W_attn'], 'L0_attn_b_attn': _L0_attn_in['b_attn'], 'L0_attn_W_proj': _L0_attn_in['W_proj'], 'L0_attn_b_proj': _L0_attn_in['b_proj'], 'L0_attn_score_gain': _L0_attn_in['score_gain'], 'L0_ffn_gate_w': _L0_ffn_in['gate_w'], 'L0_ffn_Wg': _L0_ffn_in['Wg'], 'L0_ffn_Wu': _L0_ffn_in['Wu'], 'L0_ffn_Wd': _L0_ffn_in['Wd'], 'L0_ffn_Sg': _L0_ffn_in['Sg'], 'L0_ffn_Su': _L0_ffn_in['Su'], 'L0_ffn_Sd': _L0_ffn_in['Sd'], 'L1_attn_W_dq': _L1_attn_in['W_dq'], 'L1_attn_W_uq': _L1_attn_in['W_uq'], 'L1_attn_W_dkv': _L1_attn_in['W_dkv'], 'L1_attn_W_uk': _L1_attn_in['W_uk'], 'L1_attn_W_uv': _L1_attn_in['W_uv'], 'L1_attn_W_o': _L1_attn_in['W_o'], 'L1_ffn_Wg': _L1_ffn_in['Wg'], 'L1_ffn_W1': _L1_ffn_in['W1'], 'L1_ffn_W3': _L1_ffn_in['W3'], 'L1_ffn_W2': _L1_ffn_in['W2']}
    _x0 = _d['L0_attn_x']
    _d['L0_attn_x'] = jax.random.normal(jax.random.fold_in(jax.random.key(seed), 1), (2, 1024, 128), dtype=_x0.dtype)
    del _x0
    return _d

def reference(L0_attn_x, L0_attn_W_attn, L0_attn_b_attn, L0_attn_W_proj, L0_attn_b_proj, L0_attn_score_gain, L0_ffn_gate_w, L0_ffn_Wg, L0_ffn_Wu, L0_ffn_Wd, L0_ffn_Sg, L0_ffn_Su, L0_ffn_Sd, L1_attn_W_dq, L1_attn_W_uq, L1_attn_W_dkv, L1_attn_W_uk, L1_attn_W_uv, L1_attn_W_o, L1_ffn_Wg, L1_ffn_W1, L1_ffn_W3, L1_ffn_W2):

    def _L0_attn_ref(x, W_attn, b_attn, W_proj, b_proj, score_gain):
        import jax, jax.numpy as jnp
        import numpy as np
        N_HEAD = 16
        POWER = 4
        B, T, C = x.shape
        H = N_HEAD
        D = C // H
        qkv = x @ W_attn + b_attn
        q, k, v = jnp.split(qkv, 3, axis=-1)
        to_heads = lambda t: t.reshape(B, T, H, D).transpose(0, 2, 1, 3)
        q, k, v = (to_heads(q), to_heads(k), to_heads(v))
        s = jnp.einsum('bhtd,bhsd->bhts', q, k)
        s = s - s.mean(axis=-1, keepdims=True)
        mad = jnp.abs(s).mean(axis=-1, keepdims=True) + 1e-06
        s = s / mad * score_gain
        causal = jnp.tril(jnp.ones((T, T), dtype=bool))
        s = jnp.where(causal[None, None], s, jnp.asarray(-1000.0, s.dtype))
        r = jnp.maximum(s, 0.0) ** POWER
        att = r / (r.sum(axis=-1, keepdims=True) + 1e-06)
        y = jnp.einsum('bhts,bhsd->bhtd', att, v)
        y = y.transpose(0, 2, 1, 3).reshape(B, T, C)
        return y @ W_proj + b_proj

    def _L0_ffn_ref(hidden_states, gate_w, Wg, Wu, Wd, Sg, Su, Sd):
        import jax, jax.numpy as jnp
        import numpy as np
        E = 16
        F_C = 2.0
        D = 128
        I = 4 * D
        IS = 2 * D
        B, S = (4, 128)
        b, s, d = hidden_states.shape
        T = b * s
        C = int(T * F_C / E)
        flat_x = hidden_states.reshape(T, d)
        logits = flat_x @ gate_w.T
        scores = jax.nn.softmax(logits, axis=-1).T
        topk_weight, topk_idx = jax.lax.top_k(scores, C)
        xg = flat_x[topk_idx]
        g = jnp.einsum('ecd,eid->eci', xg, Wg)
        u = jnp.einsum('ecd,eid->eci', xg, Wu)
        h = jax.nn.gelu(g, approximate=False) * u
        eo = jnp.einsum('eci,edi->ecd', h, Wd)
        eo = eo * topk_weight[..., None]
        flat_out = jnp.zeros_like(flat_x).at[topk_idx.reshape(-1)].add(eo.reshape(-1, d))
        out = flat_out.reshape(b, s, d)
        sg = hidden_states @ Sg.T
        su = hidden_states @ Su.T
        shared = jax.nn.gelu(sg, approximate=False) * su @ Sd.T
        return out + shared

    def _L1_attn_ref(x, W_dq, W_uq, W_dkv, W_uk, W_uv, W_o):
        import math
        import jax, jax.numpy as jnp
        import numpy as np
        D_MODEL = 128
        N_HEADS = 16
        D_K = D_MODEL // N_HEADS
        D_C = 32
        B, S = (2, 256)
        Bx, Sx, _ = x.shape
        c_q = x @ W_dq
        Q = (c_q @ W_uq).reshape(Bx, Sx, N_HEADS, D_K)
        c_kv = x @ W_dkv
        K = (c_kv @ W_uk).reshape(Bx, Sx, N_HEADS, D_K)
        V = (c_kv @ W_uv).reshape(Bx, Sx, N_HEADS, D_K)
        scores = jnp.einsum('bqhd,bkhd->bhqk', Q, K) / math.sqrt(D_K)
        causal = jnp.tril(jnp.ones((Sx, Sx), dtype=bool))
        scores = jnp.where(causal, scores, -jnp.inf)
        attn = jax.nn.softmax(scores, axis=-1)
        out = jnp.einsum('bhqk,bkhd->bqhd', attn, V).reshape(Bx, Sx, N_HEADS * D_K)
        return out @ W_o

    def _L1_ffn_ref(hidden_states, Wg, W1, W3, W2):
        import jax, jax.numpy as jnp
        import numpy as np
        B, S, D, F, E, K = (4, 256, 128, 256, 8, 2)
        b, s, d = hidden_states.shape
        e = Wg.shape[1]
        x = hidden_states.reshape(-1, d)
        t = x.shape[0]
        gates = jax.nn.softmax(x @ Wg, axis=-1)
        top_g, top_i = jax.lax.top_k(gates, K)
        top_g = top_g / top_g.sum(axis=-1, keepdims=True)
        w = jnp.zeros((t, e), x.dtype).at[jnp.arange(t)[:, None], top_i].add(top_g)
        gate_h = jax.nn.silu(jnp.einsum('td,edf->etf', x, W1))
        up = jnp.einsum('td,edf->etf', x, W3)
        y = jnp.einsum('etf,efd->etd', gate_h * up, W2)
        out = jnp.einsum('te,etd->td', w, y)
        return out.reshape(b, s, d)
    x = L0_attn_x
    x = _layernorm(x + _L0_attn_ref(x, L0_attn_W_attn, L0_attn_b_attn, L0_attn_W_proj, L0_attn_b_proj, L0_attn_score_gain), axis=-1)
    x = _layernorm(x + _L0_ffn_ref(x, L0_ffn_gate_w, L0_ffn_Wg, L0_ffn_Wu, L0_ffn_Wd, L0_ffn_Sg, L0_ffn_Su, L0_ffn_Sd), axis=-1)
    x = _layernorm(x + _L1_attn_ref(x, L1_attn_W_dq, L1_attn_W_uq, L1_attn_W_dkv, L1_attn_W_uk, L1_attn_W_uv, L1_attn_W_o), axis=-1)
    x = _layernorm(x + _L1_ffn_ref(x, L1_ffn_Wg, L1_ffn_W1, L1_ffn_W3, L1_ffn_W2), axis=-1)
    return x

_drawn_inputs = setup_inputs


def setup_inputs(seed=0):
    import zlib

    import numpy as np

    out = dict(_drawn_inputs(seed))
    spreads = {'L0_attn_b_attn': (0.0, 0.1), 'L0_attn_b_proj': (0.0, 0.1)}
    factors = {'L0_ffn_gate_w': 5.746,
     'L0_ffn_Wg': 7.765,
     'L0_ffn_Wu': 4.384,
     'L0_ffn_Wd': 4.185,
     'L1_attn_W_dq': 3.147,
     'L1_attn_W_uq': 3.197,
     'L1_attn_W_uk': 3.568}
    for name, (base, spread) in spreads.items():
        noise = np.random.default_rng([zlib.crc32(name.encode()), seed]).standard_normal(out[name].shape)
        drawn = base * np.exp(spread * noise) if base else spread * noise
        out[name] = jnp.asarray(drawn.astype(out[name].dtype))
    for name, factor in factors.items():
        out[name] = (out[name] * factor).astype(out[name].dtype)
    return out
```

```python
from contextlib import ExitStack

import concourse.bass as bass
from concourse import mybir

F32 = mybir.dt.float32
BF16 = mybir.dt.bfloat16
F16 = mybir.dt.float16
I32 = mybir.dt.int32
U32 = mybir.dt.uint32
ALU = mybir.AluOpType
ACT = mybir.ActivationFunctionType
AX = mybir.AxisListType

P = 128
B = 2
T = 1024
NT = B * T // P
KT = T // P
H = 16
D = P // H
HQ = 4
NQ = B * H // HQ
BANK = 512
REP = 3
ROWS = REP * REP * D
VW = 32
EPS_LN = 1e-5

STEPS = [(0,)] + [(kt, KT - kt) for kt in range(1, KT // 2)] + [(KT // 2,)]
NS = len(STEPS)
POOL_HEADS = [3, 2, 3, 2, 3]


def pieces(s):
    out, at = [], 0
    for kt in STEPS[s]:
        out.append((kt, at, T - kt * P))
        at += T - kt * P
    return out, at


def cut(lo, hi, edges):
    out, at = [], lo
    while at < hi:
        nxt = min(hi, ((at - edges) // BANK + 1) * BANK + edges)
        out.append((at, nxt))
        at = nxt
    return out


def score_cuts(s):
    return [(kt, a, b, kt * P + a - at) for kt, at, n in pieces(s)[0] for a, b in cut(at, at + n, 0)]


def value_cuts(s):
    return [(kt, at + qa - kt * P, qa, qb) for kt, at, n in pieces(s)[0] for qa, qb in cut(kt * P, T, 0)]


def spread(main, extra):
    out, done = [], 0
    for n, item in enumerate(main):
        out.append(item)
        upto = len(extra) * (n + 1) // len(main)
        out += extra[done:upto]
        done = upto
    return out + extra[done:]


TAIL = [(i, hh) for i in range(KT - 1) for hh in range(HQ)]
TAIL_AT = [len(TAIL) * s // NS for s in range(NS + 1)]


def step_jobs(s):
    return spread([("c", hh) for hh in range(HQ)], [("u", n) for n in range(TAIL_AT[s], TAIL_AT[s + 1])])


JOBS = [(s, kind, n) for s in range(NS) for kind, n in step_jobs(s)]
NJ = len(JOBS)
STEP_AT = [[job[0] for job in JOBS].index(s) for s in range(NS)] + [NJ]
RELU_AT = {(s, n): j for j, (s, kind, n) in enumerate(JOBS) if kind == "c"}
NORM_AT = 2
TAIL_JOB = [j for j in range(NJ) if JOBS[j][1] == "u"]
TURN_AT, HELD, EVAC_AT = STEP_AT[2] + (2 - STEP_AT[2]) % 3, 6, STEP_AT[1] + 4
SLOT = [n % 3 if n < TURN_AT else (n - TURN_AT) % 2 if n < TURN_AT + HELD else (n - TURN_AT - HELD + 2) % 3
        for n in range(NJ)]
PREV = [max(m for m in range(-NJ, n) if SLOT[m % NJ] == SLOT[n]) for n in range(NJ)]


E0 = 16
I0 = 4 * P
CAP = 2 * B * T // E0
NH = CAP // P
IS = 2 * P
EB = P // E0
XW = P + E0
E1 = 8
TOP = 2
F1 = 2 * P
DC = 32
MROWS = ROWS + REP
NEG = -1e30
CH = B * T // BANK
CT = BANK // P
SCORE_BITS = 30

MAX_JOBS = [((0, CT * 2, 2), [(0, 0, P), (4, BANK, P)]), ((1, CT * 2, 2), [(1, 0, 2 * P), (5, BANK, 2 * P)]),
            ((2, 1, 1), [(2, 0, 3 * P)]), ((10, 1, 1), [(6, BANK, 3 * P)]), ((3, 1, 1), [(3, 0, BANK)]),
            ((4, 1, 1), [(4, 0, BANK)]), ((5, 1, 1), [(5, 0, BANK)]), ((6, 1, 1), [(6, 0, BANK)]),
            ((7, 1, 1), [(7, 0, BANK)]), ((11, 1, 1), [(7, BANK, BANK)])]
MAX = [(hh, n) for hh in range(HQ) for n in range(len(MAX_JOBS))]
MAX_AT = [len(MAX) * s // NS for s in range(NS + 1)]


def build(nc, a, out):
    with ExitStack() as whole:
        def sem(name):
            return whole.enter_context(nc.semaphore(name))

        def dram(name, shape, dt):
            return nc.dram_tensor(name, shape, dt, kind="Internal").ap()

        def sb(name, shape, dt, scope=whole):
            return scope.enter_context(nc.sbuf_tensor(name, shape, dt))

        q_rows = dram("q_rows", [B * P, REP, REP, T], BF16)
        k_rows = dram("k_rows", [B * P, REP, REP, T], BF16)
        q_quads = q_rows.rearrange("(g h d) m n t -> g (h d m n) t", g=NQ, h=HQ)
        k_quads = k_rows.rearrange("(g h d) m n t -> g (h d m n) t", g=NQ, h=HQ)
        v_ext_d = dram("v_ext_d", [NQ, P, KT * HQ * VW], F32)

        xs_rows = dram("xs_rows", [B * T, XW], F32)
        moe_rows = dram("moe_rows", [B * T, P], F32)
        m_rows = dram("m_rows", [NQ, REP, HQ * T], BF16)

        causal_ps = [whole.enter_context(nc.psum_tensor(f"causal_ps{i}", [P, T], F32)) for i in range(2)]
        tail_ps = whole.enter_context(nc.psum_tensor("tail_ps", [P, T], F32))
        acc_ps = whole.enter_context(nc.psum_tensor("acc_ps", [P, T], F32))

        slots = [*causal_ps, tail_ps]
        banks = [t[:, h * BANK:(h + 1) * BANK] for t in (causal_ps[0], causal_ps[1], tail_ps, acc_ps)
                 for h in range(2)]

        X = sb("X", [P, NT, P], F32)
        XT = sb("XT", [P, NT * P], F32)
        Y = sb("Y", [P, B, KT, P], F32)
        ident = sb("ident", [P, P], F32)
        Z = sb("Z", [P, NT, P], F32)
        stats = sb("stats", [P, NT, 6], F32)
        mean_var = sb("mean_var", [P, NT, 2], F32)
        spread_sb = sb("spread_sb", [P, 2, NT], F32)
        eps_ln = sb("eps_ln", [P, 1], F32)
        w_proj = sb("w_proj", [P, P], F32)
        YT = sb("YT", [P, 2, BANK], F32)

        A = ExitStack()
        w_attn = sb("w_attn", [P, 3 * P], F32, A)
        b_cols = sb("b_cols", [P, 3], F32, A)
        b_v = sb("b_v", [P, P], F32, A)
        gain = sb("gain", [P, 1], F32, A)
        gain_sign = sb("gain_sign", [P, 1], F32, A)
        gain_inv = sb("gain_inv", [P, 1], F32, A)
        gain_tmp = sb("gain_tmp", [P, 1], F32, A)
        upto = sb("upto", [P, P], F32, A)
        sum_sel = sb("sum_sel", [P, VW], F32, A)
        QS = sb("QS", [P, 2, HQ, T], BF16, A)
        KS = sb("KS", [P, 2, HQ, T], BF16, A)
        VS = sb("VS", [P, 2, KT, HQ * VW], F32, A)
        R1 = sb("R1", [P, 2, HQ, T], F32, A)
        R4 = sb("R4", [P, 2, HQ, T], F32, A)
        tails = sb("tails", [P, 2, KT, HQ], F32, A)
        junk = sb("junk", [P, 3, T], BF16, A)
        Ysb = sb("Ysb", [P, T], F32, A)
        nrm = sb("nrm", [P, 6, KT * HQ], F32, A)
        proj = R1[:, :, :, :].rearrange("p a h t -> p (a h t)").rearrange("p (m t) -> p m t", t=T)
        vx = R4[:, :, :, :].rearrange("p a h t -> p (a h t)")[:, 0:KT * H * VW].rearrange(
            "p (i h w) -> p i h w", i=KT, w=VW)

        xT_in = [sem(f"xT_in{b}") for b in range(B)]
        x_in = sem("x_in")
        w_in = sem("w_in")
        consts = sem("consts")
        dve_chain = sem("dve_chain")
        act_chain = sem("act_chain")
        pool_chain = sem("pool_chain")
        proj_full = sem("proj_full")
        proj_sb = sem("proj_sb")
        part_done = sem("part_done")
        rest_done = sem("rest_done")
        part_out = [sem(f"part_out{n}") for n in range(REP)]
        v_full = sem("v_full")
        v_sb = sem("v_sb")
        v_zero = sem("v_zero")
        v_out = sem("v_out")
        gains = sem("gains")
        stack_in = [sem(f"stack_in{i}") for i in range(2)]
        stack_used = sem("stack_used")
        filled = sem("filled")
        drained = sem("drained")
        square_done = sem("square_done")
        mask_done = sem("mask_done")
        fourth_pool = sem("fourth_pool")
        fourth_dve = sem("fourth_dve")
        step_summed = sem("step_summed")
        relu_summed = sem("relu_summed")
        acc_out = sem("acc_out")
        turned = sem("turned")
        normed = sem("normed")
        finish = sem("finish")
        upto_ready = sem("upto_ready")

        pt = [sb(f"pt{n}", [P, T], BF16, A) for n in range(REP)]

        A.close()

        M = ExitStack()
        gate_t = sb("gate_t", [P, E0], F32, M)
        sg_t = sb("sg_t", [P, IS], F32, M)
        su_t = sb("su_t", [P, IS], F32, M)
        sd_t = sb("sd_t", [P, IS // P, P], F32, M)
        act_s = sb("act_s", [P, 2, BANK], F32, M)
        hid_s = sb("hid_s", [P, IS // P, BANK], F32, M)
        S = sb("S", [P, NT, E0], F32, M)
        row1 = sb("row1", [P, NT], F32, M)
        row2 = sb("row2", [P, NT], F32, M)
        row3 = sb("row3", [P, NT], F32, M)
        SC = sb("SC", [P, 2, P], F32, M)
        thr = sb("thr", [P, 1], I32, M)
        thr_next = sb("thr_next", [P, 1], I32, M)
        cand = sb("cand", [P, 1], I32, M)
        bit = sb("bit", [P, 2], I32, M)
        keep = sb("keep", [P, 1], I32, M)
        over = sb("over", [P, 4 * P], BF16, M)
        count = sb("count", [P, 1], F32, M)
        tile_counts = sb("tile_counts", [P, 2, 2], F32, M)
        same_e = sb("same_e", [P, P], F32, M)
        before_e = sb("before_e", [P, P], F32, M)
        before_t = sb("before_t", [P, P], BF16, M)
        thr_t = sb("thr_t", [P, E0], F32, M)
        above = sb("above", [P, NT, E0], BF16, M)
        equal = sb("equal", [P, NT, E0], BF16, M)
        rank_a = sb("rank_a", [P, NT * E0], F32, M)
        rank_b = sb("rank_b", [P, NT * E0], F32, M)
        slot = sb("slot", [P, NT * E0], I32, M)
        slot_hi = sb("slot_hi", [P, NT * E0], I32, M)
        slot_lo = sb("slot_lo", [P, NT * E0], I32, M)
        hi_f = sb("hi_f", [P, NT * E0], F16, M)
        lo_f = sb("lo_f", [P, NT * E0], F16, M)
        iota16 = sb("iota16", [P, 16], F16, M)
        iota_i = sb("iota_i", [P, P], I32, M)
        token = sb("token", [P, NT], F16, M)
        hot_hi = sb("hot_hi", [P, NT, E0 * 16], F16, M)
        hot_lo = sb("hot_lo", [P, NT, E0 * 16], F16, M)
        own_e = sb("own_e", [P, 8, 16], F32, M)
        own_hi = sb("own_hi", [P, 16, 8], F32, M)
        is_e = sb("is_e", [P, 8], F32, M)
        picked = sb("picked", [P, 2, 8, 16], F32, M)
        lists = sb("lists", [P, 2, 16], F32, M)
        turned_l = sb("turned_l", [P, 2, 2, 16, 8], F32, M)
        idx = sb("idx", [P, E0, NH], I32, M)
        carrier = sb("carrier", [P, 1], F32, M)
        idx_in = sb("idx_in", [P, 4, NH], I32, M)
        idx_out = sb("idx_out", [P, 4, NH], I32, M)
        G = sb("G", [P, 4, NH, XW], F32, M)
        w_tok = sb("w_tok", [P, 4, NH], F32, M)
        GT = sb("GT", [P, 2, CAP], F32, M)
        wg = sb("wg", [P, 4, I0], F32, M)
        wu = sb("wu", [P, 4, I0], F32, M)
        wd = sb("wd", [P, 4, I0], F32, M)
        act_e = sb("act_e", [P, 4, CAP], F32, M)
        hid_e = sb("hid_e", [P, 2, 4, CAP], F32, M)
        out_e = sb("out_e", [P, 2, NH, P], F32, M)
        M.close()

        N = ExitStack()
        w_down = sb("w_down", [P, 2 * DC], F32, N)
        w_up = sb("w_up", [2 * DC, 2, P], F32, N)
        latent = sb("latent", [2 * DC, B * T], F32, N)
        QM = sb("QM", [P, 2, HQ, T], BF16, N)
        KM = sb("KM", [P, 2, HQ, T], BF16, N)
        QE = sb("QE", [P, 2, HQ, T], BF16, N)
        KE = sb("KE", [P, 2, HQ, T], BF16, N)
        VE = sb("VE", [P, 2, KT, HQ * VW], F32, N)
        EX = sb("EX", [P, 2, HQ, T], F32, N)
        Esb = sb("Esb", [P, T], F32, N)
        projE = EX[:, :, :, :].rearrange("p a h t -> p (a h t)").rearrange("p (m t) -> p m t", t=T)
        vxE = VE[:, :, :, :].rearrange("p a i w -> p (a i w)")
        vx2 = sb("vx2", [P, KT, H, VW], F32, N)
        ptE = [sb(f"ptE{n}", [P, T], BF16, N) for n in range(REP)]
        mx = sb("mx", [P, 2, HQ, 12], F32, N)
        mxt = sb("mxt", [P, HQ, KT], F32, N)
        mparts = sb("mparts", [HQ * KT, REP, P], BF16, N)
        mrest = sb("mrest", [HQ * KT, P], F32, N)
        mask = sb("mask", [P, P], BF16, N)
        identb = sb("identb", [P, P], BF16, N)
        mask_f = sb("mask_f", [P, P], F32, N)
        den = sb("den", [P, KT * HQ], F32, N)
        N.close()

        F = ExitStack()
        gate1 = sb("gate1", [P, E1], F32, F)
        GG = sb("GG", [P, NT, E1], F32, F)
        rowF = sb("rowF", [P, 3, NT], F32, F)
        cmp_a = sb("cmp_a", [P, NT, E1, E1], F32, F)
        cmp_b = sb("cmp_b", [P, NT, E1, E1], F32, F)
        lower = sb("lower", [P, E1, E1], F32, F)
        rankF = sb("rankF", [P, NT, E1], F32, F)
        GW = sb("GW", [P, NT, E1], F32, F)
        WT = sb("WT", [P, E1, NT], F32, F)
        w1 = sb("w1", [P, 2, F1], F32, F)
        w3 = sb("w3", [P, 2, F1], F32, F)
        w2 = sb("w2", [P, 2, F1 // P, P], F32, F)
        act_f = sb("act_f", [P, 3, BANK], F32, F)
        hid_f = sb("hid_f", [P, 2, F1 // P, BANK], F32, F)
        F.close()

        ln_var = sem("ln_var")
        ln_std = sem("ln_std")
        ln_rec = sem("ln_rec")
        ln_stat = sem("ln_stat")
        ln_x = sem("ln_x")
        res_in = sem("res_in")
        yt_full = sem("yt_full")
        yt_sb = sem("yt_sb")
        out_full = sem("out_full")
        z_sb = sem("z_sb")
        xt_full = sem("xt_full")
        xt_sb = sem("xt_sb")
        moe_w_in = sem("moe_w_in")
        sh_up = sem("sh_up")
        sh_act = sem("sh_act")
        sh_hid = sem("sh_hid")
        sh_down = sem("sh_down")
        sh_sum = sem("sh_sum")
        sh_out = sem("sh_out")
        logits = sem("logits")
        row_max = sem("row_max")
        exps = sem("exps")
        probs = sem("probs")
        xs_out = sem("xs_out")
        sc_full = sem("sc_full")
        counted = sem("counted")
        totalled = sem("totalled")
        search = sem("search")
        found = sem("found")
        thr_full = sem("thr_full")
        marked = sem("marked")
        ranked = sem("ranked")
        hot = sem("hot")
        listed = sem("listed")
        list_sb = sem("list_sb")
        idx_full = sem("idx_full")
        idx_sb = sem("idx_sb")
        masks0 = sem("masks0")
        gathered = [sem(f"gathered{k}") for k in range(4)]
        weights = [sem(f"weights{k}") for k in range(4)]
        g_turned = sem("g_turned")
        g_sb = sem("g_sb")
        up_full = sem("up_full")
        gelu_done = sem("gelu_done")
        hid_done = sem("hid_done")
        down_full = sem("down_full")
        out_sb = sem("out_sb")
        idx_ready = sem("idx_ready")
        scattered = sem("scattered")
        z_in = sem("z_in")
        w2_in = sem("w2_in")
        lat_full = sem("lat_full")
        lat_sb = sem("lat_sb")
        max_in = [sem(f"max_in{i}") for i in range(2)]
        exp_in = [sem(f"exp_in{i}") for i in range(2)]
        ones_set = sem("ones_set")
        max_full = sem("max_full")
        max_done = sem("max_done")
        mx_ready = sem("mx_ready")
        mx_full = sem("mx_full")
        m_sb = sem("m_sb")
        m_chain = sem("m_chain")
        m_out = sem("m_out")
        exp_full = sem("exp_full")
        exp_done = sem("exp_done")
        exp_summed = sem("exp_summed")
        e_out = sem("e_out")
        e_turned = sem("e_turned")
        e_normed = sem("e_normed")
        e_chain = sem("e_chain")
        projE_full = sem("projE_full")
        projE_sb = sem("projE_sb")
        partE = sem("partE")
        restE = sem("restE")
        partE_out = [sem(f"partE_out{n}") for n in range(REP)]
        vE_full = sem("vE_full")
        vE_sb = sem("vE_sb")
        vE_out = sem("vE_out")
        f_gate_in = sem("f_gate_in")
        f_logits = sem("f_logits")
        f_max = sem("f_max")
        f_exp = sem("f_exp")
        f_w = sem("f_w")
        f_win = [sem(f"f_win{i}") for i in range(2)]
        f_up = sem("f_up")
        f_act = sem("f_act")
        f_hid = sem("f_hid")
        f_y = sem("f_y")
        f_acc = sem("f_acc")
        block = whole.enter_context(nc.Block())

        def at_least(eng, s, value):
            if not isinstance(value, int) or value > 0:
                eng.wait_ge(s, value)

        @block.sync
        def _(sp):
            sp.dma_start(w_attn[:, :], a["w_attn"]).then_inc(w_in, 16)
            sp.dma_start(XT[:, 0:T], a["xT"][:, 0:T]).then_inc(xT_in[0], 16)
            sp.dma_start(b_cols[:, :], a["b_cols"]).then_inc(w_in, 16)
            sp.dma_start(b_v[:, :], a["b_attn"][2 * P:3 * P].unsqueeze(0).broadcast_to([P, P])).then_inc(w_in, 16)
            sp.dma_start(w_proj[:, :], a["w_proj"]).then_inc(w_in, 16)
            sp.dma_start(YT[:, 0, 0:P], a["b_proj"].unsqueeze(0).broadcast_to([P, P])).then_inc(w_in, 16)
            sp.dma_start(gain[:, :], a["gain"].broadcast_to([P, 1])).then_inc(w_in, 16)
            sp.dma_start(XT[:, T:2 * T], a["xT"][:, T:2 * T]).then_inc(xT_in[1], 16)
            sp.dma_start(X[:, :, :], a["x"].rearrange("(i p) c -> p i c", p=P)).then_inc(x_in, 16)

            for m in range(2 * B):
                b = m // 2
                for n in range(REP):
                    sp.wait_ge(part_done, REP * m + n + 1)
                    dst = k_rows[b * P:(b + 1) * P, :, n, :] if m % 2 else q_rows[b * P:(b + 1) * P, n, :, :]
                    sp.dma_start(dst, pt[n][:, :].unsqueeze(1).broadcast_to([P, REP, T])).then_inc(part_out[n], 16)
                if m % 2:
                    sp.wait_ge(v_sb, b + 1)
                    for g in range(NQ // B):
                        sp.dma_start(v_ext_d[b * NQ // B + g].rearrange("p (i w) -> p i w", i=KT),
                                     vx[:, :, HQ * g:HQ * (g + 1), :].rearrange("p i h w -> p i (h w)")
                                     ).then_inc(v_out, 16)
            for n in range(REP):
                sp.wait_ge(part_out[n], 16 * 2 * B)
            sp.wait_ge(v_out, 16 * NQ)

            def quad_of(dram_ap, g):
                return dram_ap[g] if isinstance(g, int) else dram_ap[bass.ds(g, 1), :, :].rearrange("o a b -> (o a) b")

            def load_quad(k, par):
                g = par * (NQ // B) + k
                for rows, stack in ((q_quads, QS), (k_quads, KS)):
                    sp.dma_start(stack[0:ROWS, par, :, :], quad_of(rows, g).rearrange("(h r) t -> r h t", h=HQ)
                                 ).then_inc(stack_in[par], 16)
                sp.dma_start(VS[:, par, :, :].rearrange("p i w -> p (i w)"), quad_of(v_ext_d, g)).then_inc(stack_in[par], 16)

            load_quad(0, 0)
            load_quad(0, 1)
            with sp.Fori(0, NQ // 2 - 1) as j:
                sp.wait_ge(step_summed, (2 * j + 1) * NS)
                load_quad(j + 1, 0)
                sp.wait_ge(step_summed, (2 * j + 2) * NS)
                load_quad(j + 1, 1)

            sp.wait_ge(normed, NQ)
            for dst, src in ((gate_t[:, :], a["gate_t"]), (sg_t[:, :], a["sg_t"]), (su_t[:, :], a["su_t"]),
                             (sd_t[:, :, :], a["sd_t"].rearrange("(k p) d -> p k d", p=P))):
                sp.dma_start(dst, src).then_inc(moe_w_in, 16)

            def load_expert(e, k):
                for dst, name in ((wg, "wg_t"), (wu, "wu_t")):
                    sp.dma_start(dst[:, k, :], one_of(a[name], e)).then_inc(weights[k], 16)
                sp.dma_start(wd[:, k, :].rearrange("p (m d) -> p m d", d=P),
                             one_of(a["wd_t"], e).rearrange("(m p) d -> p m d", p=P)).then_inc(weights[k], 16)

            def one_of(ap, e):
                return ap[e] if isinstance(e, int) else ap[bass.ds(e, 1), :, :].rearrange("o a b -> (o a) b")

            for k in range(4):
                load_expert(k, k)
            for n in range(CH):
                sp.wait_ge(sh_sum, n + 1)
                sp.dma_start(moe_rows[n * BANK:(n + 1) * BANK, :].rearrange("(i p) d -> p i d", p=P),
                             Z[:, n * CT:(n + 1) * CT, :]).then_inc(sh_out, 16)
            sp.wait_ge(probs, 1)
            xs = xs_rows.rearrange("(i p) w -> p i w", p=P)
            sp.dma_start(xs[:, :, 0:P], X[:, :, :]).then_inc(xs_out, 16)
            sp.dma_start(xs[:, :, P:XW], S[:, :, :]).then_inc(xs_out, 16)
            with sp.Fori(0, E0 // 4 - 1) as j:
                for k in range(4):
                    sp.wait_ge(down_full, 4 * j + k + 1)
                    load_expert(4 * j + 4 + k, k)
            sp.wait_ge(scattered, 16 * NH * E0)
            sp.dma_start(Z[:, :, :], moe_rows.rearrange("(i p) d -> p i d", p=P)).then_inc(z_in, 16)

            for dst, src in ((w_down[:, 0:DC], a["w_dq"]), (w_down[:, DC:2 * DC], a["w_dkv"]),
                             (w_up[0:DC, 0, :], a["w_uq"]), (w_up[DC:2 * DC, 0, :], a["w_uk"]),
                             (w_up[DC:2 * DC, 1, :], a["w_uv"]), (w_proj[:, :], a["w_o"])):
                sp.dma_start(dst, src).then_inc(w2_in, 16)
            for m in range(2 * B):
                b = m // 2
                for n in range(REP):
                    sp.wait_ge(partE, REP * m + n + 1)
                    dst = k_rows[b * P:(b + 1) * P, :, n, :] if m % 2 else q_rows[b * P:(b + 1) * P, n, :, :]
                    sp.dma_start(dst, ptE[n][:, :].unsqueeze(1).broadcast_to([P, REP, T])).then_inc(partE_out[n], 16)
                if m % 2:
                    sp.wait_ge(vE_sb, b + 1)
                    for g in range(NQ // B):
                        sp.dma_start(v_ext_d[b * NQ // B + g].rearrange("p (i w) -> p i w", i=KT),
                                     vx2[:, :, HQ * g:HQ * (g + 1), :].rearrange("p i h w -> p i (h w)")
                                     ).then_inc(vE_out, 16)
            for n in range(REP):
                sp.wait_ge(partE_out[n], 16 * 2 * B)
            sp.wait_ge(vE_out, 16 * NQ)
            sp.wait_ge(ones_set, 1)

            def load_max(k, par):
                g = par * (NQ // B) + k
                for rows, stack in ((q_quads, QM), (k_quads, KM)):
                    sp.dma_start(stack[0:ROWS, par, :, :], quad_of(rows, g).rearrange("(h r) t -> r h t", h=HQ)
                                 ).then_inc(max_in[par], 16)

            def store_max(g):
                sp.wait_ge(m_sb, g + 1)
                sp.dma_start(quad_of(m_rows, g).rearrange("r (h t) -> h r t", t=P), mparts[:, :, :]).then_inc(m_out, 16)

            def load_exp(k, par):
                sp.wait_ge(m_out, 16 * (2 * k + par + 1))
                g = par * (NQ // B) + k
                for rows, stack in ((q_quads, QE), (k_quads, KE)):
                    sp.dma_start(stack[0:ROWS, par, :, :], quad_of(rows, g).rearrange("(h r) t -> r h t", h=HQ)
                                 ).then_inc(exp_in[par], 16)
                sp.dma_start(QE[ROWS:MROWS, par, :, :].rearrange("r h t -> r (h t)"), quad_of(m_rows, 2 * k + par)
                             ).then_inc(exp_in[par], 16)
                sp.dma_start(VE[:, par, :, :].rearrange("p i w -> p (i w)"), quad_of(v_ext_d, g)
                             ).then_inc(exp_in[par], 16)

            load_max(0, 0)
            load_max(0, 1)
            for par in range(2):
                sp.wait_ge(max_full, len(MAX) * (par + 1))
                load_max(1, par)
                store_max(par)
                load_exp(0, par)
            with sp.Fori(0, NQ // 2 - 2) as j:
                for par in range(2):
                    sp.wait_ge(max_full, len(MAX) * (2 * j + 3 + par))
                    load_max(j + 2, par)
                    store_max(2 * j + 2 + par)
                    sp.wait_ge(exp_summed, NS * (2 * j + 1 + par))
                    load_exp(j + 1, par)
            for par in range(2):
                store_max(NQ - 2 + par)
                sp.wait_ge(exp_summed, NS * (NQ - 3 + par))
                load_exp(NQ // 2 - 1, par)

            sp.wait_ge(e_normed, NQ)
            sp.dma_start(gate1[:, :], a["gate1"]).then_inc(f_gate_in, 16)

            def load_ffn(e, k):
                for dst, name in ((w1, "w1"), (w3, "w3")):
                    sp.dma_start(dst[:, k, :], one_of(a[name], e)).then_inc(f_win[k], 16)
                sp.dma_start(w2[:, k, :, :], one_of(a["w2"], e).rearrange("(m p) d -> p m d", p=P)
                             ).then_inc(f_win[k], 16)

            load_ffn(0, 0)
            load_ffn(1, 1)
            with sp.Fori(0, E1 // 2 - 1) as j:
                for k in range(2):
                    sp.wait_ge(f_y, CH * (2 * j + k + 1))
                    load_ffn(2 * j + 2 + k, k)
            sp.wait_ge(ln_x, 4)
            sp.dma_start(out.rearrange("(i p) d -> p i d", p=P), X[:, :, :]).then_inc(finish, 16)
            sp.wait_ge(finish, 16)

        @block.tensor
        def _(pe):
            pe.wait_ge(w_in, 16 * 6)
            for m in range(2 * B):
                b = m // 2
                pe.wait_ge(xT_in[b], 16)
                at_least(pe, proj_sb, m - 1)
                for n in range(T // BANK):
                    mm = pe.matmul(causal_ps[m % 2][:, n * BANK:(n + 1) * BANK],
                                   w_attn[:, (m % 2) * P:(m % 2 + 1) * P],
                                   XT[:, b * T + n * BANK:b * T + (n + 1) * BANK], start=True, stop=True)
                mm.then_inc(proj_full, 1)
                if m % 2:
                    at_least(pe, v_sb, b)
                    for i in range(KT):
                        mm = pe.matmul(tail_ps[:, i * P:(i + 1) * P], XT[:, b * T + i * P:b * T + (i + 1) * P],
                                       w_attn[:, 2 * P:3 * P], start=True, stop=True)
                    mm.then_inc(v_full, 1)
            pe.wait_ge(proj_sb, 2 * B)
            pe.wait_ge(v_sb, B)
            pe.wait_ge(consts, 2)

            def fill(g, par, j):
                s, kind, n = JOBS[j]
                at_least(pe, drained, NJ * g + PREV[j] + 1)
                if j == TURN_AT + HELD:
                    at_least(pe, normed, g)
                (causal if kind == "c" else tail)(slots[SLOT[j]], par, s, n).then_inc(filled, 1)

            def causal(slot, par, s, hh):
                for kt, c0, c1, q0 in score_cuts(s):
                    mm = pe.matmul(slot[:, c0:c1], KS[0:ROWS, par, hh, kt * P:(kt + 1) * P],
                                   QS[0:ROWS, par, hh, q0:q0 + c1 - c0], start=True, stop=True)
                return mm

            def tail(slot, par, s, n):
                i, hh = TAIL[n]
                w = T - (i + 1) * P
                for c0, c1 in cut(0, w, 0):
                    mm = pe.matmul(slot[:, c0:c1], QS[0:ROWS, par, hh, i * P:(i + 1) * P],
                                   KS[0:ROWS, par, hh, (i + 1) * P + c0:(i + 1) * P + c1], start=True, stop=True)
                return mm

            def sums(g, par, s, powered):
                rp, cuts = (par + s) % 2, value_cuts(s)

                def group(k):
                    kt, c0, qa, qb = cuts[k]
                    if k == 0 and powered:
                        pe.wait_ge(fourth_pool, NS * g + s + 1)
                        pe.wait_ge(fourth_dve, NS * g + s + 1)
                    if k == 0 and not powered:
                        pe.wait_ge(drained, NJ * g + RELU_AT[s, HQ - 1] + 1)
                        if s == 0:
                            at_least(pe, acc_out, g)
                    for hh in range(HQ):
                        src, w = (R4, VS[:, par, kt, hh * VW:(hh + 1) * VW]) if powered else (R1, sum_sel[:, :])
                        last = powered and kt == STEPS[-2 if qb <= BANK else -1][0]
                        mm = pe.matmul(acc_ps[hh * VW:(hh + 1) * VW, qa:qb], w,
                                       src[:, rp, hh, c0:c0 + qb - qa],
                                       start=(kt == 0 and not powered), stop=last, tile_position=(0, hh * VW))
                    if k == len(cuts) - 1:
                        mm.then_inc(step_summed if powered else relu_summed, 1)
                return [lambda k=k: group(k) for k in range(len(cuts))]

            def turn(g, last=False):
                pe.wait_ge(acc_out, g + 1)
                pe.wait_ge(drained, NJ * (g + 1) + (PREV[TURN_AT + HELD] + 1 if not last else 0))
                for i in range(KT):
                    mm = pe.transpose(tail_ps[:, i * P:(i + 1) * P], Ysb[:, i * P:(i + 1) * P], ident[:, :])
                mm.then_inc(turned, 1)

            def quad(g, k, par, first=False):
                pe.wait_ge(stack_in[par], 16 * 3 * (k + 1))
                for s in range(NS):
                    early = [] if first and s < 2 else (
                        sums(g, par, s - 2, True) if s >= 2 else sums(g - 1, 1 - par, NS - 2 + s, True))
                    late = [] if s == 1 or (first and s == 0) else (
                        sums(g, par, s - 1, False) if s else sums(g - 1, 1 - par, NS - 1, False))
                    if s == 1:
                        late = sums(g, par, 0, False)
                    jobs = []
                    for j in range(STEP_AT[s], STEP_AT[s + 1]):
                        if j == TURN_AT and not first:
                            jobs.append(lambda: turn(g - 1))
                        jobs.append(lambda j=j: fill(g, par, j))
                    at = EVAC_AT - STEP_AT[s] + 2 if s == 1 else 4
                    for job in jobs[:4] + early + jobs[4:at] + spread(jobs[at:], late):
                        job()

            quad(0, 0, 0, first=True)
            with pe.Fori(0, NQ // 2 - 1) as j:
                quad(2 * j + 1, j, 1)
                quad(2 * j + 2, j + 1, 0)
            quad(NQ - 1, NQ // 2 - 1, 1)
            for job in (sums(NQ - 1, 1, NS - 1, False) + sums(NQ - 1, 1, NS - 2, True)
                        + sums(NQ - 1, 1, NS - 1, True)):
                job()
            turn(NQ - 1, last=True)

            def project(layer):
                pe.wait_ge(e_normed if layer else normed, NQ)
                for n in range(CH + 1):
                    if n < CH:
                        at_least(pe, yt_sb, CH * layer + n - 1)
                        for i in range(CT):
                            t = n * CT + i
                            mm = pe.transpose(banks[n % 2][:, i * P:(i + 1) * P],
                                              Y[:, t // KT, t % KT, :],
                                              ident[:, :])
                        mm.then_inc(yt_full, 1)
                    if n:
                        pe.wait_ge(yt_sb, CH * layer + n)
                        at_least(pe, z_sb, CH * layer + n - 2 if n > 2 else 0)
                        for i in range(CT):
                            mm = pe.matmul(banks[2 + (n - 1) % 2][:, i * P:(i + 1) * P],
                                           YT[:, (n - 1) % 2, i * P:(i + 1) * P], w_proj[:, :], start=True, stop=True)
                        mm.then_inc(out_full, 1)

            def turn_x(layer):
                pe.wait_ge(ln_x, layer + 1)
                for n in range(CH):
                    for i in range(CT):
                        mm = pe.transpose(banks[4 + n][:, i * P:(i + 1) * P], X[:, n * CT + i, :], ident[:, :])
                    mm.then_inc(xt_full, 1)

            project(0)
            turn_x(0)

            pe.wait_ge(moe_w_in, 16 * 4)
            pe.wait_ge(xt_sb, CH)
            for i in range(NT):
                mm = pe.matmul(banks[0][:, i * E0:(i + 1) * E0], XT[:, i * P:(i + 1) * P], gate_t[:, :],
                               start=True, stop=True)
            mm.then_inc(logits, 1)
            for n in range(CH):
                for k in range(IS // P):
                    m = n * (IS // P) + k
                    at_least(pe, sh_hid, m - 1)
                    for w, o in ((sg_t, 1), (su_t, 2)):
                        mm = pe.matmul(banks[o + 2 * (m % 2)], w[:, k * P:(k + 1) * P], XT[:, n * BANK:(n + 1) * BANK],
                                       start=True, stop=True)
                    mm.then_inc(sh_up, 1)
                pe.wait_ge(sh_hid, (n + 1) * (IS // P))
                at_least(pe, sh_sum, n - 1)
                for i in range(CT):
                    for k in range(IS // P):
                        mm = pe.matmul(banks[5 + n % 2][:, i * P:(i + 1) * P], hid_s[:, k, i * P:(i + 1) * P],
                                       sd_t[:, k, :], start=(k == 0), stop=(k == IS // P - 1))
                mm.then_inc(sh_down, 1)
            pe.wait_ge(probs, 1)
            pe.wait_ge(exps, 1)
            for h in range(2):
                mm = pe.transpose(banks[7][:, h * P:(h + 1) * P], S[:, 8 * h:8 * (h + 1), :], ident[:, :])
            mm.then_inc(sc_full, 1)
            pe.wait_ge(masks0, 3)
            with pe.Fori(0, SCORE_BITS) as j:
                pe.wait_ge(counted, j + 1)
                pe.matmul(banks[0][:, 0:1], same_e[:, :], count[:, :], start=True, stop=True).then_inc(totalled, 1)
            pe.wait_ge(found, 1)
            pe.transpose(banks[1][:, 0:P], thr[:, 0:1].bitcast(F32).broadcast_to([P, P]), ident[:, :]
                         ).then_inc(thr_full, 1)
            pe.wait_ge(marked, 2)
            for c, flag in ((0, above), (1, equal)):
                pe.matmul(banks[2][:, c * 2 * P:(c + 1) * 2 * P], before_t[:, :],
                          flag[:, :, :].rearrange("p i e -> p (i e)"), start=True, stop=False, skip_group_check=True)
                for h in range(2):
                    more = [(tile_counts[:, c, h:h + 1], before_e)]
                    if h:
                        more.append((tile_counts[:, c, 0:1], same_e))
                    if c:
                        more += [(tile_counts[:, 0, 0:1], same_e), (tile_counts[:, 0, 1:2], same_e)]
                    for n, (cnt, w) in enumerate(more):
                        mm = pe.matmul(banks[2][:, c * 2 * P + h * P:c * 2 * P + (h + 1) * P],
                                       cnt.broadcast_to([P, P]), w[:, :], start=False,
                                       stop=(h == 1 and n == len(more) - 1), skip_group_check=True)
            mm.then_inc(ranked, 1)
            pe.wait_ge(hot, 1)
            for q in range(2):
                for i in range(NT):
                    mm = pe.matmul(banks[3 + q][:, 0:P], hot_hi[:, i, q * P:(q + 1) * P], hot_lo[:, i, q * P:(q + 1) * P],
                                   start=(i == 0), stop=(i == NT - 1))
            mm.then_inc(listed, 1)
            pe.wait_ge(list_sb, 1)
            for q in range(2):
                for h in range(NH):
                    mm = pe.matmul(banks[5][:, (q * NH + h) * 8:(q * NH + h + 1) * 8],
                                   turned_l[:, q, h, :, :].rearrange("p a b -> p (a b)"), is_e[:, :],
                                   start=True, stop=True)
            mm.then_inc(idx_full, 1)
            pe.wait_ge(idx_sb, 1)

            def turn_tokens(j, k):
                pe.wait_ge(gathered[k], 16 * NH * (j + 1))
                if k >= 2:
                    at_least(pe, g_sb, 4 * j + k - 1)
                elif not isinstance(j, int) or j > 0:
                    pe.wait_ge(g_sb, 4 * j + k - 1)
                for h in range(NH):
                    mm = pe.transpose(banks[k % 2][:, h * P:(h + 1) * P], G[:, k, h, 0:P], ident[:, :])
                mm.then_inc(g_turned, 1)

            def expert_up(j, k):
                pe.wait_ge(weights[k], 16 * 3 * (j + 1))
                pe.wait_ge(g_sb, 4 * j + k + 1)
                for m in range(I0 // P):
                    if isinstance(j, int) and j == 0:
                        at_least(pe, hid_done, 4 * k + m - 3)
                    else:
                        pe.wait_ge(hid_done, 16 * j + 4 * k + m - 3)
                    for w, c in ((wg, 0), (wu, 1)):
                        mm = pe.matmul(banks[2 + m][:, c * CAP:(c + 1) * CAP], w[:, k, m * P:(m + 1) * P],
                                       GT[:, k % 2, :], start=True, stop=True)
                    mm.then_inc(up_full, 1)

            def expert_down(j, k):
                pe.wait_ge(hid_done, 16 * j + 4 * k + 4)
                if k >= 2 or not isinstance(j, int) or j > 0:
                    pe.wait_ge(out_sb, 4 * j + k - 1)
                for h in range(NH):
                    for m in range(I0 // P):
                        mm = pe.matmul(banks[6 + k % 2][:, h * P:(h + 1) * P], hid_e[:, k % 2, m, h * P:(h + 1) * P],
                                       wd[:, k, m * P:(m + 1) * P], start=(m == 0), stop=(m == I0 // P - 1))
                mm.then_inc(down_full, 1)

            def four_experts(j):
                turn_tokens(j, 0)
                turn_tokens(j, 1)
                expert_up(j, 0)
                for k in range(1, 4):
                    expert_up(j, k)
                    expert_down(j, k - 1)
                    if k < 3:
                        turn_tokens(j, k + 1)
                expert_down(j, 3)

            four_experts(0)
            with pe.Fori(1, E0 // 4) as j:
                four_experts(j)

            turn_x(1)
            pe.wait_ge(w2_in, 16 * 6)
            pe.wait_ge(xt_sb, 2 * CH)
            for n in range(CH):
                mm = pe.matmul(banks[n][0:2 * DC, :], w_down[:, :], XT[:, n * BANK:(n + 1) * BANK], start=True, stop=True)
                mm.then_inc(lat_full, 1)
            pe.wait_ge(lat_sb, CH)
            for m in range(2 * B):
                b, r0 = m // 2, DC * (m % 2)
                at_least(pe, projE_sb, m - 1)
                for n in range(T // BANK):
                    mm = pe.matmul(causal_ps[m % 2][:, n * BANK:(n + 1) * BANK], w_up[r0:r0 + DC, 0, :],
                                   latent[r0:r0 + DC, b * T + n * BANK:b * T + (n + 1) * BANK], start=True, stop=True)
                mm.then_inc(projE_full, 1)
                if m % 2:
                    at_least(pe, vE_sb, b)
                    for i in range(KT):
                        mm = pe.matmul(tail_ps[:, i * P:(i + 1) * P], latent[DC:2 * DC, b * T + i * P:b * T + (i + 1) * P],
                                       w_up[DC:2 * DC, 1, :], start=True, stop=True)
                    mm.then_inc(vE_full, 1)
            pe.wait_ge(projE_sb, 2 * B)
            pe.wait_ge(vE_sb, B)

            def row_scores(g, par, n):
                hh, c = MAX[n]
                half = n % 2
                at_least(pe, max_done, len(MAX) * g + n - 1)
                if n < 2:
                    at_least(pe, m_sb, g)
                    at_least(pe, e_normed, g - 3)
                at = half * BANK
                for i, k0, w in MAX_JOBS[c][1]:
                    diag = k0 + w == (i + 1) * P
                    mm = pe.matmul(tail_ps[:, at:at + w], QM[0:ROWS, par, hh, i * P:(i + 1) * P],
                                   KM[0:ROWS, par, hh, k0:k0 + w], start=True, stop=not diag, skip_group_check=True)
                    if diag:
                        mm = pe.matmul(tail_ps[:, at + w - P:at + w], mask[:, :], identb[:, :],
                                       start=False, stop=True, skip_group_check=True)
                    at += w
                mm.then_inc(max_full, 1)

            def turn_max(g):
                pe.wait_ge(mx_ready, g + 1)
                pe.transpose(tail_ps[0:HQ * KT, 0:P], mxt[:, :, :], ident[:, :]).then_inc(mx_full, 1)

            def exp_scores(g, par, s, hh):
                at_least(pe, exp_done, HQ * NS * g + HQ * s + hh - 1)
                cuts = score_cuts(s)
                for n, (kt, c0, c1, q0) in enumerate(cuts):
                    mm = pe.matmul(causal_ps[hh % 2][:, c0:c1], KE[0:MROWS, par, hh, kt * P:(kt + 1) * P],
                                   QE[0:MROWS, par, hh, q0:q0 + c1 - c0], start=True, stop=q0 != kt * P,
                                   skip_group_check=True)
                    if q0 == kt * P:
                        mm = pe.matmul(causal_ps[hh % 2][:, c0:c0 + P], identb[:, :], mask[:, :],
                                       start=False, stop=True, skip_group_check=True)
                mm.then_inc(exp_full, 1)

            def exp_sums(g, par, s):
                rp, cuts = (par + s) % 2, value_cuts(s)

                def group(k):
                    kt, c0, qa, qb = cuts[k]
                    if k == 0:
                        pe.wait_ge(exp_done, HQ * NS * g + HQ * (s + 1))
                        if s == 0:
                            at_least(pe, e_out, g)
                    for hh in range(HQ):
                        mm = pe.matmul(acc_ps[hh * VW:(hh + 1) * VW, qa:qb], VE[:, par, kt, hh * VW:(hh + 1) * VW],
                                       EX[:, rp, hh, c0:c0 + qb - qa], start=(kt == 0),
                                       stop=(kt == STEPS[-2 if qb <= BANK else -1][0]), tile_position=(0, hh * VW))
                    if k == len(cuts) - 1:
                        mm.then_inc(exp_summed, 1)
                return [lambda k=k: group(k) for k in range(len(cuts))]

            def turn_exp(g):
                pe.wait_ge(e_out, g + 1)
                for i in range(KT):
                    mm = pe.transpose(tail_ps[:, i * P:(i + 1) * P], Esb[:, i * P:(i + 1) * P], ident[:, :])
                mm.then_inc(e_turned, 1)

            def run_all(jobs):
                for job in jobs:
                    job()

            def max_part(g, par, s):
                return [lambda n=n: row_scores(g, par, n) for n in range(MAX_AT[s], MAX_AT[s + 1])]

            def exp_step(g, par, s):
                return [lambda hh=hh: exp_scores(g, par, s, hh) for hh in range(HQ)]

            pe.wait_ge(masks0, 5)
            for g in range(2):
                pe.wait_ge(max_in[g], 16 * 2)
                for s in range(NS):
                    run_all(max_part(g, g, s))
                pe.wait_ge(max_done, len(MAX) * (g + 1))
                turn_max(g)

            def exp_quad(g, k, par, with_max, first=False):
                pe.wait_ge(exp_in[par], 16 * 4 * (k + 1))
                if with_max:
                    pe.wait_ge(max_in[par], 16 * 2 * (k + 2))
                for s in range(NS):
                    back = [] if s == 0 and first else exp_sums(g, par, s - 1) if s else exp_sums(g - 1, 1 - par, NS - 1)
                    jobs = exp_step(g, par, s)
                    if with_max:
                        jobs = spread(max_part(g + 2, par, s), jobs)
                    run_all(spread(jobs, back))
                if with_max:
                    pe.wait_ge(max_done, len(MAX) * (g + 3))
                    turn_max(g + 2)
                if not first:
                    pe.wait_ge(m_sb, g + 3 if with_max else NQ)
                    at_least(pe, e_normed, g - 1)
                    turn_exp(g - 1)

            exp_quad(0, 0, 0, True, first=True)
            exp_quad(1, 0, 1, True)
            with pe.Fori(1, NQ // 2 - 1) as j:
                exp_quad(2 * j, j, 0, True)
                exp_quad(2 * j + 1, j, 1, True)
            exp_quad(NQ - 2, NQ // 2 - 1, 0, False)
            exp_quad(NQ - 1, NQ // 2 - 1, 1, False)
            run_all(exp_sums(NQ - 1, 1, NS - 1))
            pe.wait_ge(e_normed, NQ - 1)
            turn_exp(NQ - 1)
            project(1)
            turn_x(2)

            pe.wait_ge(f_gate_in, 16)
            pe.wait_ge(xt_sb, 3 * CH)
            for i in range(NT):
                mm = pe.matmul(banks[0][:, i * E1:(i + 1) * E1], XT[:, i * P:(i + 1) * P], gate1[:, :],
                               start=True, stop=True)
            mm.then_inc(f_logits, 1)
            pe.wait_ge(f_max, 2)

            KF = F1 // P

            def ffn_up(e, k, n, first):
                for m in range(KF):
                    c = CH * KF * e + KF * n + m
                    ring = (KF * n + m) % 2
                    if not (first and n == 0):
                        pe.wait_ge(f_hid, c - 1)
                    for w, o in ((w1, 0), (w3, 1)):
                        mm = pe.matmul(banks[2 * ring + o], w[:, k, m * P:(m + 1) * P],
                                       XT[:, n * BANK:(n + 1) * BANK], start=True, stop=True)
                    mm.then_inc(f_up, 1)

            def ffn_down(e, k, n, first):
                pe.wait_ge(f_hid, CH * KF * e + KF * (n + 1))
                if not (first and n < 2):
                    pe.wait_ge(f_acc, CH * e + n - 1)
                for i in range(CT):
                    for m in range(KF):
                        mm = pe.matmul(banks[4 + n % 2][:, i * P:(i + 1) * P], hid_f[:, n % 2, m, i * P:(i + 1) * P],
                                       w2[:, k, m, :], start=(m == 0), stop=(m == KF - 1))
                mm.then_inc(f_y, 1)

            def ffn_two(e, kk, first):
                for k in range(2):
                    pe.wait_ge(f_win[k], 16 * 3 * (kk + 1))
                    first_k = first and k == 0
                    ffn_up(e + k, k, 0, first_k)
                    for n in range(CH):
                        if n + 1 < CH:
                            ffn_up(e + k, k, n + 1, False)
                        ffn_down(e + k, k, n, first_k)

            ffn_two(0, 0, True)
            with pe.Fori(1, E1 // 2) as j:
                ffn_two(2 * j, j, False)

        @block.scalar
        def _(act):
            for m in range(2 * B):
                for n in range(REP):
                    act.wait_ge(rest_done, REP * m + n + 1)
                    if m > 0:
                        act.wait_ge(part_out[n], 16 * m)
                    act.activation(pt[n][:, :], proj[:, m, :], ACT.Copy).then_inc(part_done, 1)

            def drain(g, par, j):
                s, kind, n = JOBS[j]
                if j == 0:
                    at_least(act, normed, g - 1)
                if (kind, n) == ("c", 0):
                    at_least(act, relu_summed, NS * g + s - 1)
                    at_least(act, square_done, 2 * (NS * g + s - 1))
                if kind == "u":
                    at_least(act, drained, NJ * g + (TAIL_JOB[n - 3] + 1 if n >= 3 else 0))
                act.wait_ge(filled, NJ * g + j + 1)
                (keep if kind == "c" else add_up)(slots[SLOT[j]], par, s, n).then_inc(drained, 1)

            def keep(slot, par, s, hh):
                rp, width = (par + s) % 2, pieces(s)[1]
                return act.activation(R1[:, rp, hh, 0:width], slot[:, 0:width], ACT.Relu)

            def add_up(slot, par, s, n):
                i, hh = TAIL[n]
                return act.activation(junk[:, n % 3, 0:T - (i + 1) * P], slot[:, 0:T - (i + 1) * P], ACT.Relu,
                                      accum_out=tails[:, par, i, hh:hh + 1])

            def evacuate(g):
                act.wait_ge(step_summed, NS * (g + 1))
                at_least(act, turned, g)
                act.activation(Ysb[:, :], acc_ps[:, :], ACT.Copy).then_inc(acc_out, 1)

            def quad(g, par, first=False):
                for j in range(NJ):
                    if j == EVAC_AT and not first:
                        evacuate(g - 1)
                    drain(g, par, j)

            for n in range(REP):
                act.wait_ge(part_out[n], 16 * 2 * B)
            quad(0, 0, first=True)
            with act.Fori(0, NQ // 2 - 1) as j:
                quad(2 * j + 1, 1)
                quad(2 * j + 2, 0)
            quad(NQ - 1, 1)
            evacuate(NQ - 1)

            def project(layer):
                for n in range(CH):
                    act.wait_ge(yt_full, CH * layer + n + 1)
                    at_least(act, out_full, CH * layer + n - 1 if n > 1 else 0)
                    act.activation(YT[:, n % 2, :], banks[n % 2], ACT.Copy).then_inc(yt_sb, 1)

            def deviation(layer):
                act.wait_ge(ln_var, layer + 1)
                act.activation(spread_sb[:, 0, :], mean_var[:, :, 1], ACT.Sqrt, bias=eps_ln[:, 0:1]).then_inc(ln_std, 1)

            def copy_xt(layer):
                for n in range(CH):
                    act.wait_ge(xt_full, CH * layer + n + 1)
                    act.activation(XT[:, n * BANK:(n + 1) * BANK], banks[4 + n], ACT.Copy).then_inc(xt_sb, 1)

            project(0)
            deviation(0)
            copy_xt(0)

            act.wait_ge(row_max, 1)
            act.activation(S[:, :, :], S[:, :, :], ACT.Exp).then_inc(exps, 1)
            for n in range(CH):
                for k in range(IS // P):
                    m = n * (IS // P) + k
                    act.wait_ge(sh_up, m + 1)
                    at_least(act, sh_hid, m - 1)
                    act.activation(act_s[:, m % 2, :], banks[1 + 2 * (m % 2)], ACT.Gelu).then_inc(sh_act, 1)

            def gelu_expert(j, k):
                for m in range(I0 // P):
                    act.wait_ge(up_full, 16 * j + 4 * k + m + 1)
                    if k > 0 or not isinstance(j, int) or j > 0:
                        act.wait_ge(hid_done, 16 * j + 4 * k + m - 3)
                    act.activation(act_e[:, m, :], banks[2 + m][:, 0:CAP], ACT.Gelu).then_inc(gelu_done, 1)

            for k in range(4):
                gelu_expert(0, k)
            with act.Fori(1, E0 // 4) as j:
                for k in range(4):
                    gelu_expert(j, k)
            deviation(1)
            copy_xt(1)

            for n in range(CH):
                act.wait_ge(lat_full, n + 1)
                act.activation(latent[:, n * BANK:(n + 1) * BANK], banks[n][0:2 * DC, :], ACT.Copy).then_inc(lat_sb, 1)
            for m in range(2 * B):
                for n in range(REP):
                    act.wait_ge(restE, REP * m + n + 1)
                    if m > 0:
                        act.wait_ge(partE_out[n], 16 * m)
                    act.activation(ptE[n][:, :], projE[:, m, :], ACT.Copy).then_inc(partE, 1)

            def exps_of(g, par, s, hh):
                rp, width = (par + s) % 2, pieces(s)[1]
                act.wait_ge(exp_full, HQ * NS * g + HQ * s + hh + 1)
                if hh == 0:
                    at_least(act, exp_summed, NS * g + s - 1)
                act.activation(EX[:, rp, hh, 0:width], causal_ps[hh % 2][:, 0:width], ACT.Exp,
                               scale=float(D) ** -0.5).then_inc(exp_done, 1)

            def exp_evacuate(g):
                act.wait_ge(exp_summed, NS * (g + 1))
                at_least(act, e_turned, g)
                act.activation(Esb[:, :], acc_ps[:, :], ACT.Copy).then_inc(e_out, 1)

            def exp_quad(g, par, first=False):
                for s in range(NS):
                    for hh in range(HQ):
                        exps_of(g, par, s, hh)
                    if s == 0 and not first:
                        exp_evacuate(g - 1)

            for n in range(REP):
                act.wait_ge(partE_out[n], 16 * 2 * B)
            exp_quad(0, 0, first=True)
            exp_quad(1, 1)
            with act.Fori(1, NQ // 2 - 1) as j:
                exp_quad(2 * j, 0)
                exp_quad(2 * j + 1, 1)
            exp_quad(NQ - 2, 0)
            exp_quad(NQ - 1, 1)
            exp_evacuate(NQ - 1)
            project(1)
            deviation(2)
            copy_xt(2)

            act.wait_ge(f_max, 1)
            act.activation(GG[:, :, :], GG[:, :, :], ACT.Exp).then_inc(f_exp, 1)
            KF = F1 // P

            def silus(e, first):
                for c in range(CH * KF):
                    act.wait_ge(f_up, CH * KF * e + c + 1)
                    if not (first and c < 2):
                        act.wait_ge(f_hid, CH * KF * e + c - 1)
                    act.activation(act_f[:, c % 2, :], banks[2 * (c % 2)], ACT.Silu).then_inc(f_act, 1)

            silus(0, True)
            with act.Fori(1, E1) as e:
                silus(e, False)
            deviation(3)

        @block.vector
        def _(dve):
            chained = [0]

            def link(ins):
                ins.then_inc(dve_chain, 1)
                chained[0] += 1
                dve.wait_ge(dve_chain, chained[0])

            dve.memset(eps_ln[:, :], EPS_LN)
            dve.memset(vx, 0.0).then_inc(v_zero, 1)
            dve.memset(tails[:, :, :, :], 0.0)
            dve.memset(ident[:, :], 1.0)
            dve.memset(sum_sel[:, :], 0.0).then_inc(consts, 1)
            dve.wait_ge(consts, 1)
            dve.memset(sum_sel[:, D + 1:D + 2], 1.0)
            dve.wait_ge(v_zero, 1)
            dve.memset(vx[:, :, :, D:D + 1], 1.0).then_inc(v_zero, 1)
            dve.wait_ge(w_in, 16 * 6)
            link(dve.tensor_scalar(gain_tmp[:, :], gain[:, :], 0.0, 2.0, ALU.is_ge, ALU.mult))
            dve.tensor_scalar(gain_sign[:, :], gain_tmp[:, :], -1.0, None, ALU.add)
            link(dve.reciprocal(gain_inv[:, :], gain[:, :]))
            dve.wait_ge(v_zero, 2)
            for m in range(2 * B):
                f = proj[:, m, :]
                dve.wait_ge(proj_full, m + 1)
                if m % 2 == 0:
                    dve.tensor_scalar(f, causal_ps[0][:, :], b_cols[:, 0:1], gain_sign[:, :],
                                      ALU.add, ALU.mult).then_inc(proj_sb, 1)
                    dve.wait_ge(proj_sb, m + 1)
                    dve.tensor_scalar(f, f, 1.0, None, ALU.mult).then_inc(rest_done, 1)
                else:
                    dve.tensor_scalar(f, causal_ps[1][:, :], b_cols[:, 1:2], 0.0, ALU.add, ALU.add,
                                      accum_out=gain_tmp[:, :]).then_inc(proj_sb, 1)
                    dve.wait_ge(proj_sb, m + 1)
                    link(dve.tensor_scalar(nrm[:, 0, 0:1], gain_tmp[:, :], -1.0 / T, None, ALU.mult))
                    dve.tensor_scalar(f, f, nrm[:, 0, 0:1], None, ALU.add).then_inc(rest_done, 1)
                for n in range(REP - 1):
                    dve.wait_ge(part_done, REP * m + n + 1)
                    dve.tensor_tensor(f, f, pt[n][:, :], ALU.subtract).then_inc(rest_done, 1)
                if m % 2:
                    b = m // 2
                    dve.wait_ge(v_full, b + 1)
                    at_least(dve, v_out, 16 * (NQ // B) * b)
                    for i in range(KT):
                        ins = dve.tensor_tensor(vx[:, i, :, 0:D],
                                                tail_ps[:, i * P:(i + 1) * P].rearrange("p (h d) -> p h d", d=D),
                                                b_v[:, :].rearrange("p (h d) -> p h d", d=D), ALU.add)
                    ins.then_inc(v_sb, 1)
            dve.wait_ge(v_out, 16 * NQ)
            dve.wait_ge(v_sb, B)
            dve.wait_ge(upto_ready, 2)

            def square(g, par, s):
                rp, width = (par + s) % 2, pieces(s)[1]
                at_least(dve, step_summed, NS * g + s - 1)
                for h0 in (0, 2):
                    dve.wait_ge(drained, NJ * g + RELU_AT[s, h0 + 1] + 1)
                    dve.tensor_tensor(R4[:, rp, h0:h0 + 2, 0:width], R1[:, rp, h0:h0 + 2, 0:width],
                                      R1[:, rp, h0:h0 + 2, 0:width], ALU.mult).then_inc(square_done, 1)
                    dve.wait_ge(square_done, 2 * NS * g + 2 * s + h0 // 2 + 1)
                    for kt, at, _ in pieces(s)[0]:
                        ins = dve.tensor_tensor(R4[:, rp, h0:h0 + 2, at:at + P], R4[:, rp, h0:h0 + 2, at:at + P],
                                                upto[:, :].unsqueeze(1).broadcast_to([P, 2, P]), ALU.mult)
                    ins.then_inc(mask_done, 1)

            def fourth(g, par, s):
                rp, width, h0 = (par + s) % 2, pieces(s)[1], POOL_HEADS[s]
                dve.wait_ge(mask_done, 2 * NS * g + 2 * s + 2)
                dve.tensor_tensor(R4[:, rp, h0:HQ, 0:width], R4[:, rp, h0:HQ, 0:width],
                                  R4[:, rp, h0:HQ, 0:width], ALU.mult).then_inc(fourth_dve, 1)

            def y_of(k, par):
                heads = slice(HQ * D * k, HQ * D * (k + 1)) if isinstance(k, int) else bass.ds(k * (HQ * D), HQ * D)
                return Y[:, par, :, heads].rearrange("p i (h d) -> p i h d", d=D)

            def before(k, par):
                return (k, 0) if par else (k - 1, 1)

            def normalise(k, par):
                got = tail_ps[:, :].rearrange("p (i h w) -> p i h w", i=KT, w=VW)
                g = 2 * k + par
                sums, z, z2, z4, den, w = [nrm[:, n, :].rearrange("p (i h) -> p i h", h=HQ) for n in range(6)]
                dve.wait_ge(turned, g + 1)

                def then(ins):
                    ins.then_inc(dve_chain, 1)
                    step[0] += 1
                    dve.wait_ge(dve_chain, base + per * g + step[0])
                base, per, step = chained[0], 7, [0]
                then(dve.tensor_tensor(sums, got[:, :, :, D + 1], tails[:, par, :, :], ALU.add))
                then(dve.tensor_scalar(z, sums, 2.0 / T, 1e-6, ALU.mult, ALU.add))
                then(dve.tensor_scalar(z, z, gain_inv[:, 0:1], None, ALU.mult))
                then(dve.tensor_tensor(z2, z, z, ALU.mult))
                then(dve.tensor_tensor(z4, z2, z2, ALU.mult))
                then(dve.scalar_tensor_tensor(den, z4, 1e-6, got[:, :, :, D], ALU.mult, ALU.add))
                then(dve.reciprocal(w, den))
                dve.tensor_tensor(y_of(k, par), got[:, :, :, 0:D],
                                  w.unsqueeze(3).broadcast_to([P, KT, HQ, D]), ALU.mult).then_inc(normed, 1)

            def quad(k, par, first=False):
                g = 2 * k + par
                for s in range(NS):
                    if s == NORM_AT and not first:
                        normalise(*before(k, par))
                    square(g, par, s)
                    fourth(g, par, s)

            quad(0, 0, first=True)
            with dve.Fori(0, NQ // 2 - 1) as j:
                quad(j, 1)
                quad(j + 1, 0)
            quad(NQ // 2 - 1, 1)
            normalise(NQ // 2 - 1, 1)
            chained[0] += 7 * NQ

            def residual(layer):
                for n in range(CH):
                    dve.wait_ge(out_full, CH * layer + n + 1)
                    dve.tensor_tensor(Z[:, n * CT:(n + 1) * CT, :], X[:, n * CT:(n + 1) * CT, :],
                                      banks[2 + n % 2].rearrange("p (i d) -> p i d", d=P), ALU.add).then_inc(z_sb, 1)

            def layer_norm(layer):
                for i in range(NT):
                    dve.bn_stats(stats[:, i, :], Z[:, i, :]).then_inc(ln_stat, 1)
                for i in range(NT):
                    dve.wait_ge(ln_stat, NT * layer + i + 1)
                    ins = dve.bn_aggr(mean_var[:, i, :], stats[:, i, :])
                ins.then_inc(ln_var, 1)
                dve.wait_ge(ln_std, layer + 1)
                dve.reciprocal(spread_sb[:, 1, :], spread_sb[:, 0, :]).then_inc(ln_rec, 1)
                dve.wait_ge(ln_rec, layer + 1)
                dve.wait_ge(ln_var, layer + 1)
                for i in range(NT):
                    ins = dve.tensor_scalar(X[:, i, :], Z[:, i, :], mean_var[:, i, 0:1], spread_sb[:, 1, i:i + 1],
                                            ALU.subtract, ALU.mult)
                ins.then_inc(ln_x, 1)

            dve.wait_ge(res_in, 1)
            residual(0)
            dve.wait_ge(z_sb, CH)
            layer_norm(0)

            dve.wait_ge(logits, 1)
            got = banks[0][:, 0:NT * E0].rearrange("p (i e) -> p i e", e=E0)
            link(dve.tensor_reduce(row1[:, :], got, AX.X, ALU.max))
            dve.tensor_tensor(S[:, :, :], got, row1[:, :].unsqueeze(2).broadcast_to([P, NT, E0]),
                              ALU.subtract).then_inc(row_max, 1)
            dve.wait_ge(exps, 1)
            link(dve.tensor_reduce(row2[:, :], S[:, :, :], AX.X, ALU.add))
            link(dve.reciprocal(row3[:, :], row2[:, :]))
            dve.tensor_tensor(S[:, :, :], S[:, :, :], row3[:, :].unsqueeze(2).broadcast_to([P, NT, E0]),
                              ALU.mult).then_inc(probs, 1)
            for n in range(CH):
                for k in range(IS // P):
                    m = n * (IS // P) + k
                    dve.wait_ge(sh_act, m + 1)
                    if k == 0:
                        at_least(dve, sh_down, n)
                    dve.tensor_tensor(hid_s[:, k, :], act_s[:, m % 2, :], banks[2 + 2 * (m % 2)],
                                      ALU.mult).then_inc(sh_hid, 1)
                dve.wait_ge(sh_down, n + 1)
                dve.tensor_tensor(Z[:, n * CT:(n + 1) * CT, :], X[:, n * CT:(n + 1) * CT, :],
                                  banks[5 + n % 2].rearrange("p (i d) -> p i d", d=P), ALU.add).then_inc(sh_sum, 1)
            dve.wait_ge(sc_full, 1)
            link(dve.tensor_copy(SC[:, :, :].rearrange("p h t -> p (h t)"), banks[7][:, 0:2 * P]))
            dve.memset(thr[:, :], 0)
            dve.memset(bit[:, 0:1], 1 << (SCORE_BITS - 1))
            link(dve.memset(cand[:, :], 1 << (SCORE_BITS - 1)))
            sc_all = SC[:, :, :].rearrange("p h t -> p (h t)")
            base = chained[0]
            with dve.Fori(0, SCORE_BITS) as j:
                dve.tensor_scalar(over[:, 0:2 * P], sc_all, cand[:, 0:1].bitcast(F32), 0.0, ALU.is_ge, ALU.add,
                                  accum_out=count[:, :]).then_inc(counted, 1)
                dve.tensor_scalar(bit[:, 1:2], bit[:, 0:1], 1, None, ALU.logical_shift_right).then_inc(search, 1)
                dve.wait_ge(search, 4 * j + 1)
                dve.tensor_tensor(thr_next[:, :], thr[:, :], bit[:, 1:2], ALU.bitwise_or).then_inc(search, 1)
                dve.wait_ge(totalled, j + 1)
                dve.tensor_scalar(keep[:, :], banks[0][:, 0:1], CAP - 0.5, -1.0, ALU.is_ge, ALU.mult).then_inc(search, 1)
                dve.wait_ge(search, 4 * j + 3)
                dve.scalar_tensor_tensor(cand[:, :], keep[:, :], bit[:, 0:1], thr_next[:, :], ALU.bitwise_and,
                                         ALU.bitwise_or)
                dve.scalar_tensor_tensor(thr[:, :], keep[:, :], bit[:, 0:1], thr[:, :], ALU.bitwise_and,
                                         ALU.bitwise_or).then_inc(search, 1)
                dve.wait_ge(search, 4 * j + 4)
                dve.tensor_copy(bit[:, 0:1], bit[:, 1:2]).then_inc(dve_chain, 1)
                dve.wait_ge(dve_chain, base + 1 + j)
            chained[0] += SCORE_BITS
            dve.nop().then_inc(found, 1)
            for c, op in ((0, ALU.is_gt), (1, ALU.is_equal)):
                for h in range(2):
                    dve.tensor_scalar(over[:, (2 * c + h) * P:(2 * c + h + 1) * P], SC[:, h, :], thr[:, 0:1].bitcast(F32), 0.0, op,
                                      ALU.add, accum_out=tile_counts[:, c, h:h + 1])
            dve.wait_ge(thr_full, 1)
            link(dve.tensor_copy(thr_t[:, :], banks[1][:, 0:E0]))
            for flag, op in ((above, ALU.is_gt), (equal, ALU.is_equal)):
                dve.tensor_tensor(flag[:, :, :], S[:, :, :], thr_t[:, :].unsqueeze(1).broadcast_to([P, NT, E0]), op
                                  ).then_inc(marked, 1)
            dve.wait_ge(ranked, 1)
            dve.wait_ge(marked, 2)
            big = float(2 * B * T)
            dve.scalar_tensor_tensor(rank_a[:, :], banks[2][:, 0:2 * P], -big,
                                     above[:, :, :].rearrange("p i e -> p (i e)"), ALU.add, ALU.mult)
            link(dve.scalar_tensor_tensor(rank_b[:, :], banks[2][:, 2 * P:4 * P], -big,
                                          equal[:, :, :].rearrange("p i e -> p (i e)"), ALU.add, ALU.mult))
            link(dve.scalar_tensor_tensor(slot[:, :], rank_a[:, :], big, rank_b[:, :], ALU.add, ALU.add))
            link(dve.tensor_scalar(slot_hi[:, :], slot[:, :], 4, None, ALU.logical_shift_right))
            link(dve.tensor_scalar(slot_lo[:, :], slot[:, :], 15, None, ALU.bitwise_and))
            link(dve.tensor_copy(hi_f[:, :], slot_hi[:, :]))
            link(dve.tensor_copy(lo_f[:, :], slot_lo[:, :]))
            dve.wait_ge(masks0, 4)
            for hot_x, val in ((hot_hi, hi_f), (hot_lo, lo_f)):
                link(dve.tensor_tensor(hot_x[:, :, :].rearrange("p i (e s) -> p (i e) s", s=16),
                                       val[:, :].unsqueeze(2).broadcast_to([P, NT * E0, 16]),
                                       iota16[:, :].unsqueeze(1).broadcast_to([P, NT * E0, 16]), ALU.is_equal))
            dve.tensor_tensor(hot_hi[:, :, :], hot_hi[:, :, :], token[:, :].unsqueeze(2).broadcast_to([P, NT, E0 * 16]),
                              ALU.mult).then_inc(hot, 1)
            dve.wait_ge(listed, 1)
            for q in range(2):
                link(dve.tensor_tensor(picked[:, q, :, :], banks[3 + q][:, 0:P].rearrange("p (e b) -> p e b", b=16),
                                       own_e[:, :, :], ALU.mult))
                link(dve.tensor_reduce(lists[:, q, :], picked[:, q, :, :].rearrange("p e b -> p b e"), AX.X, ALU.add))
                for h in range(NH):
                    ins = dve.tensor_tensor(turned_l[:, q, h, :, :], own_hi[:, :, :],
                                            lists[:, q, h * 8:(h + 1) * 8].unsqueeze(1).broadcast_to([P, 16, 8]),
                                            ALU.mult)
            ins.then_inc(list_sb, 1)
            dve.wait_ge(idx_full, 1)
            dve.tensor_copy(idx[:, :, :].rearrange("p (q e) h -> p q h e", q=2),
                            banks[5][:, 0:2 * NH * 8].rearrange("p (q h e) -> p q h e", q=2, e=8)).then_inc(idx_sb, 1)

            def take_tokens(j, k):
                dve.wait_ge(g_turned, 4 * j + k + 1)
                if k >= 2 or not isinstance(j, int) or j > 0:
                    dve.wait_ge(up_full, 16 * j + 4 * (k - 1))
                col = P + 4 * j + k
                w_col = G[:, k, :, col:col + 1] if isinstance(j, int) else G[:, k, :, bass.ds(col, 1)]
                dve.tensor_copy(w_tok[:, k, :].unsqueeze(2), w_col)
                dve.tensor_copy(GT[:, k % 2, :], banks[k % 2][:, 0:CAP]).then_inc(g_sb, 1)

            def hidden(j, k):
                for m in range(I0 // P):
                    dve.wait_ge(gelu_done, 16 * j + 4 * k + m + 1)
                    if m == 0 and (k >= 2 or not isinstance(j, int) or j > 0):
                        dve.wait_ge(down_full, 4 * j + k - 1)
                    dve.tensor_tensor(hid_e[:, k % 2, m, :], act_e[:, m, :], banks[2 + m][:, CAP:2 * CAP],
                                      ALU.mult).then_inc(hid_done, 1)

            def weigh(j, k):
                dve.wait_ge(down_full, 4 * j + k + 1)
                if k >= 2 or not isinstance(j, int) or j > 0:
                    dve.wait_ge(scattered, 16 * NH * (4 * j + k - 1))
                for h in range(NH):
                    ins = dve.tensor_scalar(out_e[:, k % 2, h, :], banks[6 + k % 2][:, h * P:(h + 1) * P],
                                            w_tok[:, k, h:h + 1], None, ALU.mult)
                ins.then_inc(out_sb, 1)

            def four_experts(j):
                take_tokens(j, 0)
                take_tokens(j, 1)
                hidden(j, 0)
                for k in range(1, 4):
                    hidden(j, k)
                    weigh(j, k - 1)
                    if k < 3:
                        take_tokens(j, k + 1)
                weigh(j, 3)

            four_experts(0)
            with dve.Fori(1, E0 // 4) as j:
                four_experts(j)
            dve.wait_ge(z_in, 16)
            layer_norm(1)

            dve.wait_ge(w2_in, 16 * 6)
            dve.memset(KE[64:96, :, :, :], 1.0)
            dve.memset(vx2[:, :, :, :], 0.0).then_inc(v_zero, 1)
            dve.wait_ge(v_zero, 3)
            dve.memset(vx2[:, :, :, D:D + 1], 1.0).then_inc(ones_set, 1)
            dve.wait_ge(ones_set, 1)
            for m in range(2 * B):
                f = projE[:, m, :]
                dve.wait_ge(projE_full, m + 1)
                dve.tensor_copy(f, causal_ps[m % 2][:, :]).then_inc(projE_sb, 1)
                dve.wait_ge(projE_sb, m + 1)
                dve.nop().then_inc(restE, 1)
                for n in range(REP - 1):
                    dve.wait_ge(partE, REP * m + n + 1)
                    dve.tensor_tensor(f, f, ptE[n][:, :], ALU.subtract).then_inc(restE, 1)
                if m % 2:
                    b = m // 2
                    dve.wait_ge(vE_full, b + 1)
                    at_least(dve, vE_out, 16 * (NQ // B) * b)
                    dve.tensor_copy(vx2[:, :, :, 0:D], tail_ps[:, :].rearrange("p (i h d) -> p i h d", i=KT, d=D)
                                    ).then_inc(vE_sb, 1)

            def row_max_of(g, par, n):
                hh, c = MAX[n]
                (o0, step, cnt), groups = MAX_JOBS[c]
                w, half = groups[0][2], n % 2
                dve.wait_ge(max_full, len(MAX) * g + n + 1)
                dst = mx[:, par, hh, o0:o0 + step * (cnt - 1) + 1:step]
                dve.tensor_reduce(dst, tail_ps[:, half * BANK:half * BANK + cnt * w].rearrange("p (c w) -> p c w", w=w),
                                  AX.X, ALU.max, negate=True).then_inc(max_done, 1)

            def parts_of_max(g, par):
                dve.wait_ge(max_done, len(MAX) * (g + 1))
                at_least(dve, mx_full, g)
                dve.tensor_copy(mxt[:, :, 0:CT], mx[:, par, :, 0:CT])
                dve.tensor_tensor(mxt[:, :, CT:KT], mx[:, par, :, CT:KT], mx[:, par, :, KT:12], ALU.min
                                  ).then_inc(mx_ready, 1)
                dve.wait_ge(mx_full, g + 1)
                if not isinstance(g, int) or g > 0:
                    dve.wait_ge(m_out, 16 * g)
                src = tail_ps[0:HQ * KT, 0:P]

                def then(n, ins):
                    ins.then_inc(m_chain, 1)
                    dve.wait_ge(m_chain, 4 * g + n)
                then(1, dve.tensor_copy(mparts[:, 0, :], src))
                then(2, dve.tensor_tensor(mrest[:, :], src, mparts[:, 0, :], ALU.subtract))
                then(3, dve.tensor_copy(mparts[:, 1, :], mrest[:, :]))
                then(4, dve.tensor_tensor(mrest[:, :], mrest[:, :], mparts[:, 1, :], ALU.subtract))
                dve.tensor_copy(mparts[:, 2, :], mrest[:, :]).then_inc(m_sb, 1)

            def exp_normalise(k, par):
                g = 2 * k + par
                got = tail_ps[:, :].rearrange("p (i h w) -> p i h w", i=KT, w=VW)
                d3 = den[:, :].rearrange("p (i h) -> p i h", h=HQ)
                dve.wait_ge(e_turned, g + 1)
                dve.reciprocal(d3, got[:, :, :, D]).then_inc(e_chain, 1)
                dve.wait_ge(e_chain, g + 1)
                dve.tensor_tensor(y_of(k, par), got[:, :, :, 0:D],
                                  d3.unsqueeze(3).broadcast_to([P, KT, HQ, D]), ALU.mult).then_inc(e_normed, 1)

            for g in range(2):
                for n in range(len(MAX)):
                    row_max_of(g, g, n)
                parts_of_max(g, g)

            def max_quad(k, par, first=False):
                g = 2 * k + par
                for n in range(len(MAX)):
                    row_max_of(g + 2, par, n)
                parts_of_max(g + 2, par)
                if not first:
                    exp_normalise(*before(k, par))

            max_quad(0, 0, first=True)
            max_quad(0, 1)
            with dve.Fori(1, NQ // 2 - 1) as j:
                max_quad(j, 0)
                max_quad(j, 1)
            for g in range(NQ - 3, NQ):
                exp_normalise(g // 2, g % 2)
            residual(1)
            dve.wait_ge(z_sb, 2 * CH)
            layer_norm(2)

            dve.wait_ge(f_logits, 1)
            got1 = banks[0][:, 0:NT * E1].rearrange("p (i e) -> p i e", e=E1)
            link(dve.tensor_reduce(rowF[:, 0, :], got1, AX.X, ALU.max))
            dve.tensor_tensor(GG[:, :, :], got1, rowF[:, 0, :].unsqueeze(2).broadcast_to([P, NT, E1]),
                              ALU.subtract).then_inc(f_max, 1)
            dve.wait_ge(f_exp, 1)
            link(dve.tensor_reduce(rowF[:, 1, :], GG[:, :, :], AX.X, ALU.add))
            link(dve.reciprocal(rowF[:, 2, :], rowF[:, 1, :]))
            link(dve.tensor_tensor(GG[:, :, :], GG[:, :, :], rowF[:, 2, :].unsqueeze(2).broadcast_to([P, NT, E1]), ALU.mult))
            dve.wait_ge(masks0, 6)
            for i0 in range(0, NT, 4):
                mine = GG[:, i0:i0 + 4, :].unsqueeze(3).broadcast_to([P, 4, E1, E1])
                other = GG[:, i0:i0 + 4, :].unsqueeze(2).broadcast_to([P, 4, E1, E1])
                dve.tensor_tensor(cmp_a[:, i0:i0 + 4, :, :], other, mine, ALU.is_gt)
                link(dve.tensor_tensor(cmp_b[:, i0:i0 + 4, :, :], other, mine, ALU.is_equal))
            low = lower[:, :, :].unsqueeze(1).broadcast_to([P, NT, E1, E1])
            link(dve.tensor_tensor(cmp_b[:, :, :, :], cmp_b[:, :, :, :], low, ALU.mult))
            link(dve.tensor_tensor(cmp_a[:, :, :, :], cmp_a[:, :, :, :], cmp_b[:, :, :, :], ALU.add))
            link(dve.tensor_reduce(rankF[:, :, :], cmp_a[:, :, :, :], AX.X, ALU.add))
            link(dve.scalar_tensor_tensor(GW[:, :, :], rankF[:, :, :], TOP - 0.5, GG[:, :, :], ALU.is_lt, ALU.mult))
            link(dve.tensor_reduce(rowF[:, 0, :], GW[:, :, :], AX.X, ALU.add))
            link(dve.reciprocal(rowF[:, 1, :], rowF[:, 0, :]))
            link(dve.tensor_tensor(WT[:, :, :], GW[:, :, :].rearrange("p i e -> p e i"),
                                   rowF[:, 1, :].unsqueeze(1).broadcast_to([P, E1, NT]), ALU.mult))
            link(dve.tensor_copy(Z[:, :, :], X[:, :, :]))
            dve.nop().then_inc(f_max, 1)
            KF = F1 // P

            def hidden1(e, n, first):
                for m in range(KF):
                    c = KF * n + m
                    dve.wait_ge(f_act, CH * KF * e + c + 1)
                    if m == 0 and not (first and n < 2):
                        dve.wait_ge(f_y, CH * e + n - 1)
                    dve.tensor_tensor(hid_f[:, n % 2, m, :], act_f[:, c % 2, :], banks[2 * (c % 2) + 1],
                                      ALU.mult).then_inc(f_hid, 1)

            def add_up(e, n, first):
                dve.wait_ge(f_y, CH * e + n + 1)
                if not first:
                    dve.wait_ge(f_acc, CH * e + n - 3)
                for i in range(CT):
                    t = n * CT + i
                    w = WT[:, 0, t:t + 1] if isinstance(e, int) else WT[:, bass.ds(e, 1), t:t + 1].rearrange("p o t -> p (o t)")
                    ins = dve.scalar_tensor_tensor(Z[:, t, :], banks[4 + n % 2][:, i * P:(i + 1) * P], w, Z[:, t, :],
                                                   ALU.mult, ALU.add)
                ins.then_inc(f_acc, 1)

            def expert1(e, first):
                hidden1(e, 0, first)
                for n in range(CH):
                    if n + 1 < CH:
                        hidden1(e, n + 1, first)
                    add_up(e, n, first)

            expert1(0, True)
            with dve.Fori(1, E1) as e:
                expert1(e, False)
            dve.wait_ge(f_acc, CH * E1)
            layer_norm(3)

        @block.gpsimd
        def _(pool):
            pool.wait_ge(consts, 1)
            pool.affine_select(out=ident[:, :], in_=ident[:, :], compare_op=ALU.is_equal, fill=0.0, base=0,
                               pattern=[[-1, P]], channel_multiplier=1).then_inc(consts, 1)
            pool.memset(upto[:, :], 1.0).then_inc(upto_ready, 1)
            pool.wait_ge(upto_ready, 1)
            pool.affine_select(out=upto[:, :], in_=upto[:, :], compare_op=ALU.is_ge, fill=0.0, base=0,
                               pattern=[[1, P]], channel_multiplier=-1).then_inc(upto_ready, 1)

            def quad(g, par):
                for s in range(NS):
                    rp, width = (par + s) % 2, pieces(s)[1]
                    for h0, h1 in ((0, 2), (2, POOL_HEADS[s])):
                        if h0 < h1:
                            pool.wait_ge(mask_done, 2 * NS * g + 2 * s + h0 // 2 + 1)
                            ins = pool.tensor_tensor(R4[:, rp, h0:h1, 0:width], R4[:, rp, h0:h1, 0:width],
                                                     R4[:, rp, h0:h1, 0:width], ALU.mult)
                    ins.then_inc(fourth_pool, 1)

            pool.wait_ge(x_in, 16)
            pool.wait_ge(w_in, 16 * 6)
            pool.tensor_tensor(X[:, :, :], X[:, :, :], YT[:, 0, 0:P].unsqueeze(1).broadcast_to([P, NT, P]),
                               ALU.add).then_inc(res_in, 1)
            with pool.Fori(0, NQ // 2) as j:
                quad(2 * j, 0)
                quad(2 * j + 1, 1)

            pool.wait_ge(normed, NQ)

            def link(n, ins):
                ins.then_inc(pool_chain, 1)
                pool.wait_ge(pool_chain, n)
            pool.iota(iota_i[:, :], pattern=[[0, P // E0], [1, E0]], base=0, channel_multiplier=0)
            link(1, pool.memset(same_e[:, :], 0.0))
            for o in range(-(P // E0) + 1, P // E0):
                link(o + 8 + 1, pool.affine_select(out=same_e[:, :], in_=same_e[:, :], compare_op=ALU.not_equal, fill=1.0,
                                                   base=o * E0, pattern=[[-1, P]], channel_multiplier=1))
            link(17, pool.memset(own_e[:, :, :], 1.0))
            pool.affine_select(out=before_e[:, :], in_=same_e[:, :], compare_op=ALU.is_gt, fill=0.0, base=0,
                               pattern=[[1, P]], channel_multiplier=-1).then_inc(masks0, 1)
            link(18, pool.memset(rank_a[:, 0:P], 1.0))
            pool.affine_select(out=before_t[:, :], in_=rank_a[:, 0:P], compare_op=ALU.is_gt, fill=0.0, base=0,
                               pattern=[[1, P]], channel_multiplier=-1).then_inc(masks0, 1)
            link(19, pool.affine_select(out=own_e[:, :, :], in_=own_e[:, :, :], compare_op=ALU.is_ge, fill=0.0, base=0,
                                        pattern=[[-16, 8], [0, 16]], channel_multiplier=1))
            link(20, pool.affine_select(out=own_e[:, :, :], in_=own_e[:, :, :], compare_op=ALU.is_ge, fill=0.0, base=15,
                                        pattern=[[16, 8], [0, 16]], channel_multiplier=-1))
            link(21, pool.tensor_copy(is_e[:, :], own_e[:, :, 0]))
            link(22, pool.memset(own_hi[:, :, :], 0.0))
            for e in range(8):
                link(23 + e, pool.affine_select(out=own_hi[:, :, :], in_=own_hi[:, :, :], compare_op=ALU.not_equal,
                                                fill=1.0, base=-16 * e, pattern=[[-1, 16], [0, 8]],
                                                channel_multiplier=1))
            link(31, pool.tensor_copy(iota16[:, :], iota_i[:, 0:16]))
            link(32, pool.iota(iota_i[:, 0:NT], pattern=[[P, NT]], base=0, channel_multiplier=1))
            pool.tensor_copy(token[:, :], iota_i[:, 0:NT]).then_inc(masks0, 1)
            pool.wait_ge(masks0, 3)
            pool.nop().then_inc(masks0, 1)

            def carry_waits():
                pool.tensor_tensor(carrier[:, :], eps_ln[:, :], eps_ln[:, :], ALU.add)

            def gather(e, k):
                src = idx[:, e, :] if isinstance(e, int) else idx[:, bass.ds(e, 1), :].rearrange("p o h -> p (o h)")
                pool.tensor_copy(idx_in[:, k, :], src).then_inc(idx_ready, 1)
                return 1

            def fetch(k):
                for h in range(NH):
                    pool.indirect_dma_start(out=G[:, k, h, :], out_offset=None, in_=xs_rows,
                                            in_offset=bass.IndirectOffsetOnAxis(ap=idx_in[:, k, h:h + 1].bitcast(U32), axis=0)
                                            ).then_inc(gathered[k], 16)

            def scatter(j, k):
                e = 4 * j + k
                src = idx[:, e, :] if isinstance(e, int) else idx[:, bass.ds(e, 1), :].rearrange("p o h -> p (o h)")
                pool.tensor_copy(idx_out[:, k, :], src).then_inc(idx_ready, 1)
                pool.wait_ge(idx_ready, 4 + (8 * j if not isinstance(j, int) or j < 3 else 24) + scat_at(j, k))
                pool.wait_ge(out_sb, e + 1)
                if not (isinstance(e, int) and e == 0):
                    pool.wait_ge(scattered, 16 * NH * e)
                carry_waits()
                for h in range(NH):
                    pool.indirect_dma_start(out=moe_rows, in_=out_e[:, k % 2, h, :], in_offset=None,
                                            out_offset=bass.IndirectOffsetOnAxis(ap=idx_out[:, k, h:h + 1].bitcast(U32), axis=0),
                                            compute_op=ALU.add).then_inc(scattered, 16)

            ORDER = [("g", 0), ("g", 1), ("s", 0), ("g", 2), ("s", 1), ("g", 3), ("s", 2), ("s", 3)]

            def scat_at(j, k):
                order = ORDER if not isinstance(j, int) or j < 3 else [o for o in ORDER if o[0] == "s"]
                return order.index(("s", k)) + 1

            pool.wait_ge(idx_sb, 1)
            pool.wait_ge(xs_out, 16 * 2)
            for k in range(4):
                gather(k, k)
            pool.wait_ge(idx_ready, 4)
            for k in range(4):
                fetch(k)
            pool.wait_ge(sh_out, 16 * CH)

            def four_experts(j):
                for n, (kind, k) in enumerate(ORDER):
                    if kind == "g":
                        pool.wait_ge(g_sb, 4 * j + k + 1)
                        gather(4 * j + 4 + k, k)
                        pool.wait_ge(idx_ready, 4 + 8 * j + n + 1)
                        carry_waits()
                        fetch(k)
                    else:
                        scatter(j, k)

            four_experts(0)
            with pool.Fori(1, E0 // 4 - 1) as j:
                four_experts(j)
            for k in range(4):
                scatter(E0 // 4 - 1, k)

            pool.wait_ge(w2_in, 16 * 6)
            pool.tensor_copy(identb[:, :], ident[:, :])
            link(33, pool.memset(mask_f[:, :], 0.0))
            pool.affine_select(out=mask[:, :], in_=mask_f[:, :], compare_op=ALU.is_ge, fill=NEG, base=0,
                               pattern=[[1, P]], channel_multiplier=-1).then_inc(masks0, 1)
            pool.wait_ge(e_normed, NQ)
            link(34, pool.memset(lower[:, :, :], 1.0))
            pool.affine_select(out=lower[:, :, :], in_=lower[:, :, :], compare_op=ALU.is_gt, fill=0.0, base=0,
                               pattern=[[1, E1], [-1, E1]], channel_multiplier=0).then_inc(masks0, 1)


_INS = {
    "x": ("L0_attn_x", lambda a: a.reshape(B * T, P)),
    "xT": ("L0_attn_x", lambda a: a.reshape(B * T, P).T),
    "w_attn": ("L0_attn_W_attn", lambda a: a),
    "b_attn": ("L0_attn_b_attn", lambda a: a),
    "b_cols": ("L0_attn_b_attn", lambda a: a.reshape(3, P).T),
    "w_proj": ("L0_attn_W_proj", lambda a: a),
    "b_proj": ("L0_attn_b_proj", lambda a: a),
    "gain": ("L0_attn_score_gain", lambda a: a.reshape(1)),
    "gate_t": ("L0_ffn_gate_w", lambda a: a.T),
    "wg_t": ("L0_ffn_Wg", lambda a: a.transpose(0, 2, 1)),
    "wu_t": ("L0_ffn_Wu", lambda a: a.transpose(0, 2, 1)),
    "wd_t": ("L0_ffn_Wd", lambda a: a.transpose(0, 2, 1)),
    "sg_t": ("L0_ffn_Sg", lambda a: a.T),
    "su_t": ("L0_ffn_Su", lambda a: a.T),
    "sd_t": ("L0_ffn_Sd", lambda a: a.T),
    "w_dq": ("L1_attn_W_dq", lambda a: a),
    "w_uq": ("L1_attn_W_uq", lambda a: a),
    "w_dkv": ("L1_attn_W_dkv", lambda a: a),
    "w_uk": ("L1_attn_W_uk", lambda a: a),
    "w_uv": ("L1_attn_W_uv", lambda a: a),
    "w_o": ("L1_attn_W_o", lambda a: a),
    "gate1": ("L1_ffn_Wg", lambda a: a),
    "w1": ("L1_ffn_W1", lambda a: a),
    "w3": ("L1_ffn_W3", lambda a: a),
    "w2": ("L1_ffn_W2", lambda a: a),
}


def kernel(**inputs):
    import numpy as _np
    import concourse.bacc as _bacc
    from concourse.bass_utils import run_bass_kernel_spmd as _run

    nc = _bacc.Bacc("TRN2", target_bir_lowering=False, num_devices=1)
    arrays, aps = {}, {}
    for name, (source, lay) in _INS.items():
        arr = _np.ascontiguousarray(lay(_np.asarray(inputs[source])))
        arrays[f"in_{name}"] = arr
        aps[name] = nc.dram_tensor(f"in_{name}", arr.shape, mybir.dt.from_np(arr.dtype), kind="ExternalInput").ap()
    out = nc.dram_tensor("out_x", (B * T, P), F32, kind="ExternalOutput").ap()
    build(nc, aps, out)
    r = _run(nc, [arrays], core_ids=[0])
    return r.results[0]["out_x"].reshape(B, T, P)
```

```python
from contextlib import ExitStack

import concourse.bass as bass
from concourse import mybir

F32 = mybir.dt.float32
BF16 = mybir.dt.bfloat16
F16 = mybir.dt.float16
I32 = mybir.dt.int32
U32 = mybir.dt.uint32
ALU = mybir.AluOpType
ACT = mybir.ActivationFunctionType
AX = mybir.AxisListType

P = 128
B = 2
T = 1024
NT = B * T // P
KT = T // P
H = 16
D = P // H
HQ = 4
NQ = B * H // HQ
BANK = 512
REP = 3
ROWS = REP * REP * D
VW = 32
EPS_LN = 1e-5

STEPS = [(0,)] + [(kt, KT - kt) for kt in range(1, KT // 2)] + [(KT // 2,)]
NS = len(STEPS)
POOL_HEADS = [3, 2, 3, 2, 3]


def pieces(s):
    out, at = [], 0
    for kt in STEPS[s]:
        out.append((kt, at, T - kt * P))
        at += T - kt * P
    return out, at


def cut(lo, hi, edges):
    out, at = [], lo
    while at < hi:
        nxt = min(hi, ((at - edges) // BANK + 1) * BANK + edges)
        out.append((at, nxt))
        at = nxt
    return out


def score_cuts(s):
    return [(kt, a, b, kt * P + a - at) for kt, at, n in pieces(s)[0] for a, b in cut(at, at + n, 0)]


def value_cuts(s):
    return [(kt, at + qa - kt * P, qa, qb) for kt, at, n in pieces(s)[0] for qa, qb in cut(kt * P, T, 0)]


def spread(main, extra):
    out, done = [], 0
    for n, item in enumerate(main):
        out.append(item)
        upto = len(extra) * (n + 1) // len(main)
        out += extra[done:upto]
        done = upto
    return out + extra[done:]


TAIL = [(i, hh) for i in range(KT - 1) for hh in range(HQ)]
TAIL_AT = [len(TAIL) * s // NS for s in range(NS + 1)]


def step_jobs(s):
    return spread([("c", hh) for hh in range(HQ)], [("u", n) for n in range(TAIL_AT[s], TAIL_AT[s + 1])])


JOBS = [(s, kind, n) for s in range(NS) for kind, n in step_jobs(s)]
NJ = len(JOBS)
STEP_AT = [[job[0] for job in JOBS].index(s) for s in range(NS)] + [NJ]
RELU_AT = {(s, n): j for j, (s, kind, n) in enumerate(JOBS) if kind == "c"}
NORM_AT = 2
TAIL_JOB = [j for j in range(NJ) if JOBS[j][1] == "u"]
TURN_AT, HELD, EVAC_AT = STEP_AT[2] + (2 - STEP_AT[2]) % 3, 6, STEP_AT[1] + 4
SLOT = [n % 3 if n < TURN_AT else (n - TURN_AT) % 2 if n < TURN_AT + HELD else (n - TURN_AT - HELD + 2) % 3
        for n in range(NJ)]
PREV = [max(m for m in range(-NJ, n) if SLOT[m % NJ] == SLOT[n]) for n in range(NJ)]


E0 = 16
I0 = 4 * P
CAP = 2 * B * T // E0
NH = CAP // P
IS = 2 * P
EB = P // E0
XW = P + E0
E1 = 8
TOP = 2
F1 = 2 * P
DC = 32
MROWS = ROWS + REP
NEG = -1e30
CH = B * T // BANK
CT = BANK // P
STACK_DMAS = REP * REP + REP
PARTS_OUT = 16 * NQ // B
SCORE_BITS = 30
ROUNDS = SCORE_BITS // 2

MAX_JOBS = [((0, CT * 2, 2), [(0, 0, P), (4, BANK, P)]), ((1, CT * 2, 2), [(1, 0, 2 * P), (5, BANK, 2 * P)]),
            ((2, 1, 1), [(2, 0, 3 * P)]), ((10, 1, 1), [(6, BANK, 3 * P)]), ((3, 1, 1), [(3, 0, BANK)]),
            ((4, 1, 1), [(4, 0, BANK)]), ((5, 1, 1), [(5, 0, BANK)]), ((6, 1, 1), [(6, 0, BANK)]),
            ((7, 1, 1), [(7, 0, BANK)]), ((11, 1, 1), [(7, BANK, BANK)])]
MAX = [(hh, n) for hh in range(HQ) for n in range(len(MAX_JOBS))]
MAX_AT = [len(MAX) * s // NS for s in range(NS + 1)]


def build(nc, a, out):
    with ExitStack() as whole:
        def sem(name):
            return whole.enter_context(nc.semaphore(name))

        def dram(name, shape, dt):
            return nc.dram_tensor(name, shape, dt, kind="Internal").ap()

        def sb(name, shape, dt, scope=whole):
            return scope.enter_context(nc.sbuf_tensor(name, shape, dt))

        q_parts = dram("q_parts", [NQ, REP, D, HQ, T], BF16)
        k_parts = dram("k_parts", [NQ, REP, D, HQ, T], BF16)

        xs_rows = dram("xs_rows", [B * T, XW], F32)
        moe_rows = dram("moe_rows", [B * T, P], F32)
        m_rows = dram("m_rows", [NQ, REP, HQ * T], BF16)

        causal_ps = [whole.enter_context(nc.psum_tensor(f"causal_ps{i}", [P, T], F32)) for i in range(2)]
        tail_ps = whole.enter_context(nc.psum_tensor("tail_ps", [P, T], F32))
        acc_ps = whole.enter_context(nc.psum_tensor("acc_ps", [P, T], F32))

        slots = [*causal_ps, tail_ps]
        banks = [t[:, h * BANK:(h + 1) * BANK] for t in (causal_ps[0], causal_ps[1], tail_ps, acc_ps)
                 for h in range(2)]

        X = sb("X", [P, NT, P], F32)
        XT = sb("XT", [P, NT * P], F32)
        Y = sb("Y", [P, B, KT, P], F32)
        ident = sb("ident", [P, P], F32)
        Z = sb("Z", [P, NT, P], F32)
        stats = sb("stats", [P, NT, 6], F32)
        mean_var = sb("mean_var", [P, NT, 2], F32)
        spread_sb = sb("spread_sb", [P, 2, NT], F32)
        eps_ln = sb("eps_ln", [P, 1], F32)
        w_proj = sb("w_proj", [P, P], F32)
        YT = sb("YT", [P, 2, BANK], F32)
        pt = sb("pt", [P, 2, REP, T], BF16)
        VS = sb("VS", [P, 2, KT, HQ * VW], F32)

        A = ExitStack()
        w_attn = sb("w_attn", [P, 3 * P], F32, A)
        b_cols = sb("b_cols", [P, 3], F32, A)
        b_v = sb("b_v", [P, P], F32, A)
        gain = sb("gain", [P, 1], F32, A)
        gain_sign = sb("gain_sign", [P, 1], F32, A)
        gain_inv = sb("gain_inv", [P, 1], F32, A)
        gain_tmp = sb("gain_tmp", [P, 1], F32, A)
        k_sum = sb("k_sum", [P, 1], F32, A)
        k_mean = sb("k_mean", [P, 1], F32, A)
        upto = sb("upto", [P, P], F32, A)
        sum_sel = sb("sum_sel", [P, VW], F32, A)
        QS = sb("QS", [P, 2, HQ, T], BF16, A)
        KS = sb("KS", [P, 2, HQ, T], BF16, A)
        R1 = sb("R1", [P, 2, HQ, T], F32, A)
        R4 = sb("R4", [P, 2, HQ, T], F32, A)
        tails = sb("tails", [P, 2, KT, HQ], F32, A)
        junk = sb("junk", [P, 3, T], BF16, A)
        Ysb = sb("Ysb", [P, T], F32, A)
        nrm = sb("nrm", [P, 6, KT * HQ], F32, A)
        proj = R1[:, :, :, :].rearrange("p a h t -> p (a h t)").rearrange("p (m t) -> p m t", t=T)
        xT_in = [sem(f"xT_in{b}") for b in range(B)]
        x_in = sem("x_in")
        w_in = sem("w_in")
        consts = sem("consts")
        dve_chain = sem("dve_chain")
        act_chain = sem("act_chain")
        pool_chain = sem("pool_chain")
        proj_full = sem("proj_full")
        part_done = sem("part_done")
        rest_done = sem("rest_done")
        part_out = [[sem(f"part_out{m}{n}") for n in range(REP)] for m in range(2)]
        v_full = sem("v_full")
        v_sb = sem("v_sb")
        v_ready = sem("v_ready")
        stack_in = [sem(f"stack_in{i}") for i in range(2)]
        filled = sem("filled")
        drained = sem("drained")
        square_done = sem("square_done")
        mask_done = sem("mask_done")
        fourth_pool = sem("fourth_pool")
        fourth_dve = sem("fourth_dve")
        step_summed = sem("step_summed")
        relu_summed = sem("relu_summed")
        acc_out = sem("acc_out")
        turned = sem("turned")
        normed = sem("normed")
        finish = sem("finish")
        upto_ready = sem("upto_ready")

        A.close()

        M = ExitStack()
        gate_t = sb("gate_t", [P, E0], F32, M)
        sg_t = sb("sg_t", [P, IS], F32, M)
        su_t = sb("su_t", [P, IS], F32, M)
        sd_t = sb("sd_t", [P, IS // P, P], F32, M)
        act_s = sb("act_s", [P, 2, BANK], F32, M)
        hid_s = sb("hid_s", [P, IS // P, BANK], F32, M)
        S = sb("S", [P, NT, E0], F32, M)
        row1 = sb("row1", [P, NT], F32, M)
        row2 = sb("row2", [P, NT], F32, M)
        row3 = sb("row3", [P, NT], F32, M)
        SC = sb("SC", [P, 2, P], F32, M)
        thr = sb("thr", [P, 1], I32, M)
        two_bits = sb("two_bits", [P, 4], I32, M)
        cand = sb("cand", [P, 4], I32, M)
        reached = sb("reached", [P, 4], F32, M)
        over = sb("over", [P, 6 * P], BF16, M)
        count = sb("count", [P, 4], F32, M)
        tile_counts = sb("tile_counts", [P, 2, 2], F32, M)
        same_e = sb("same_e", [P, P], F32, M)
        before_e = sb("before_e", [P, P], F32, M)
        before_t = sb("before_t", [P, P], BF16, M)
        thr_t = sb("thr_t", [P, E0], F32, M)
        above = sb("above", [P, NT, E0], BF16, M)
        equal = sb("equal", [P, NT, E0], BF16, M)
        rank_a = sb("rank_a", [P, NT * E0], F32, M)
        rank_b = sb("rank_b", [P, NT * E0], F32, M)
        slot = sb("slot", [P, NT * E0], I32, M)
        slot_hi = sb("slot_hi", [P, NT * E0], I32, M)
        slot_lo = sb("slot_lo", [P, NT * E0], I32, M)
        hi_f = sb("hi_f", [P, NT * E0], F16, M)
        lo_f = sb("lo_f", [P, NT * E0], F16, M)
        iota16 = sb("iota16", [P, 16], F16, M)
        iota_i = sb("iota_i", [P, P], I32, M)
        token = sb("token", [P, NT], F16, M)
        hot_hi = sb("hot_hi", [P, NT, E0 * 16], F16, M)
        hot_lo = sb("hot_lo", [P, NT, E0 * 16], F16, M)
        own_e = sb("own_e", [P, 8, 16], F32, M)
        own_hi = sb("own_hi", [P, 16, 8], F32, M)
        is_e = sb("is_e", [P, 8], F32, M)
        picked = sb("picked", [P, 2, 8, 16], F32, M)
        lists = sb("lists", [P, 2, 16], F32, M)
        turned_l = sb("turned_l", [P, 2, 2, 16, 8], F32, M)
        idx = sb("idx", [P, E0, NH], I32, M)
        carrier = sb("carrier", [P, 1], F32, M)
        idx_in = sb("idx_in", [P, 4, NH], I32, M)
        idx_out = sb("idx_out", [P, 4, NH], I32, M)
        G = sb("G", [P, 4, NH, XW], F32, M)
        w_tok = sb("w_tok", [P, 4, NH], F32, M)
        GT = sb("GT", [P, 2, CAP], F32, M)
        wg = sb("wg", [P, 4, I0], F32, M)
        wu = sb("wu", [P, 4, I0], F32, M)
        wd = sb("wd", [P, 4, I0], F32, M)
        act_e = sb("act_e", [P, 4, CAP], F32, M)
        hid_e = sb("hid_e", [P, 2, 4, CAP], F32, M)
        out_e = sb("out_e", [P, 2, NH, P], F32, M)
        M.close()

        N = ExitStack()
        w_down = sb("w_down", [P, 2 * DC], F32, N)
        w_up = sb("w_up", [2 * DC, 2, P], F32, N)
        latent = sb("latent", [2 * DC, B * T], F32, N)
        QM = sb("QM", [P, 2, HQ, T], BF16, N)
        KM = sb("KM", [P, 2, HQ, T], BF16, N)
        QE = sb("QE", [P, 2, HQ, T], BF16, N)
        KE = sb("KE", [P, 2, HQ, T], BF16, N)
        EX = sb("EX", [P, 2, HQ, T], F32, N)
        Esb = sb("Esb", [P, T], F32, N)
        projE = EX[:, :, :, :].rearrange("p a h t -> p (a h t)").rearrange("p (m t) -> p m t", t=T)
        mx = sb("mx", [P, 2, HQ, 12], F32, N)
        mxt = sb("mxt", [P, HQ, KT], F32, N)
        mparts = sb("mparts", [HQ * KT, REP, P], BF16, N)
        mrest = sb("mrest", [HQ * KT, P], F32, N)
        mask = sb("mask", [P, P], BF16, N)
        identb = sb("identb", [P, P], BF16, N)
        mask_f = sb("mask_f", [P, P], F32, N)
        den = sb("den", [P, KT * HQ], F32, N)
        N.close()

        F = ExitStack()
        gate1 = sb("gate1", [P, E1], F32, F)
        GG = sb("GG", [P, NT, E1], F32, F)
        rowF = sb("rowF", [P, 3, NT], F32, F)
        cmp_a = sb("cmp_a", [P, NT, E1, E1], F32, F)
        cmp_b = sb("cmp_b", [P, NT, E1, E1], F32, F)
        lower = sb("lower", [P, E1, E1], F32, F)
        rankF = sb("rankF", [P, NT, E1], F32, F)
        GW = sb("GW", [P, NT, E1], F32, F)
        WT = sb("WT", [P, E1, NT], F32, F)
        w1 = sb("w1", [P, 2, F1], F32, F)
        w3 = sb("w3", [P, 2, F1], F32, F)
        w2 = sb("w2", [P, 2, F1 // P, P], F32, F)
        act_f = sb("act_f", [P, 3, BANK], F32, F)
        hid_f = sb("hid_f", [P, 2, F1 // P, BANK], F32, F)
        F.close()

        ln_var = sem("ln_var")
        ln_std = sem("ln_std")
        ln_rec = sem("ln_rec")
        ln_stat = sem("ln_stat")
        ln_x = sem("ln_x")
        res_in = sem("res_in")
        yt_full = sem("yt_full")
        yt_sb = sem("yt_sb")
        out_full = sem("out_full")
        z_sb = sem("z_sb")
        xt_full = sem("xt_full")
        xt_sb = sem("xt_sb")
        moe_w_in = sem("moe_w_in")
        sh_up = sem("sh_up")
        sh_act = sem("sh_act")
        sh_hid = sem("sh_hid")
        sh_down = sem("sh_down")
        sh_sum = sem("sh_sum")
        sh_out = sem("sh_out")
        logits = sem("logits")
        row_max = sem("row_max")
        exps = sem("exps")
        probs = sem("probs")
        xs_out = sem("xs_out")
        sc_full = sem("sc_full")
        counted = sem("counted")
        totalled = sem("totalled")
        search = sem("search")
        found = sem("found")
        thr_full = sem("thr_full")
        marked = sem("marked")
        ranked = sem("ranked")
        hot = sem("hot")
        listed = sem("listed")
        list_sb = sem("list_sb")
        idx_full = sem("idx_full")
        idx_sb = sem("idx_sb")
        masks0 = sem("masks0")
        gathered = [sem(f"gathered{k}") for k in range(4)]
        weights = [sem(f"weights{k}") for k in range(4)]
        g_turned = sem("g_turned")
        g_sb = sem("g_sb")
        up_full = sem("up_full")
        gelu_done = sem("gelu_done")
        hid_done = sem("hid_done")
        down_full = sem("down_full")
        out_sb = sem("out_sb")
        idx_ready = sem("idx_ready")
        scattered = sem("scattered")
        z_in = sem("z_in")
        w2_in = sem("w2_in")
        lat_full = sem("lat_full")
        lat_sb = sem("lat_sb")
        max_in = [sem(f"max_in{i}") for i in range(2)]
        exp_in = [sem(f"exp_in{i}") for i in range(2)]
        ones_set = sem("ones_set")
        max_full = sem("max_full")
        max_done = sem("max_done")
        mx_ready = sem("mx_ready")
        mx_full = sem("mx_full")
        m_sb = sem("m_sb")
        m_chain = sem("m_chain")
        m_out = sem("m_out")
        exp_full = sem("exp_full")
        exp_done = sem("exp_done")
        exp_summed = sem("exp_summed")
        e_out = sem("e_out")
        e_turned = sem("e_turned")
        e_normed = sem("e_normed")
        e_chain = sem("e_chain")
        f_gate_in = sem("f_gate_in")
        f_logits = sem("f_logits")
        f_max = sem("f_max")
        f_exp = sem("f_exp")
        f_w = sem("f_w")
        f_win = [sem(f"f_win{i}") for i in range(2)]
        f_up = sem("f_up")
        f_act = sem("f_act")
        f_hid = sem("f_hid")
        f_y = sem("f_y")
        f_acc = sem("f_acc")
        block = whole.enter_context(nc.Block())

        def at_least(eng, s, value):
            if not isinstance(value, int) or value > 0:
                eng.wait_ge(s, value)

        @block.sync
        def _(sp):
            sp.dma_start(w_attn[:, :], a["w_attn"]).then_inc(w_in, 16)
            sp.dma_start(XT[:, 0:T], a["xT"][:, 0:T]).then_inc(xT_in[0], 16)
            sp.dma_start(b_cols[:, :], a["b_cols"]).then_inc(w_in, 16)
            sp.dma_start(b_v[:, :], a["b_attn"][2 * P:3 * P].unsqueeze(0).broadcast_to([P, P])).then_inc(w_in, 16)
            sp.dma_start(w_proj[:, :], a["w_proj"]).then_inc(w_in, 16)
            sp.dma_start(YT[:, 0, 0:P], a["b_proj"].unsqueeze(0).broadcast_to([P, P])).then_inc(w_in, 16)
            sp.dma_start(gain[:, :], a["gain"].broadcast_to([P, 1])).then_inc(w_in, 16)
            sp.dma_start(XT[:, T:2 * T], a["xT"][:, T:2 * T]).then_inc(xT_in[1], 16)
            sp.dma_start(X[:, :, :], a["x"].rearrange("(i p) c -> p i c", p=P)).then_inc(x_in, 16)

            def store_parts(layer, b):
                for n in range(REP):
                    for m, parts in enumerate((q_parts, k_parts)):
                        sp.wait_ge(part_done, 2 * REP * (B * layer + b) + 2 * n + m + 1)
                        for k in range(NQ // B):
                            sp.dma_start(parts[b * (NQ // B) + k, n].rearrange("d h t -> h d t"),
                                         pt[k * HQ * D:(k + 1) * HQ * D, m, n, :]).then_inc(part_out[m][n], 16)

            def parts_stored(layer, b):
                for m in range(2):
                    for n in range(REP):
                        sp.wait_ge(part_out[m][n], PARTS_OUT * (B * layer + b + 1))

            def load_stack(q_stack, k_stack, g, done):
                q, k = [quad_of(parts, g).rearrange("r d h t -> r d (h t)") for parts in (q_parts, k_parts)]
                for m in range(REP):
                    rows = slice(m * REP * D, (m + 1) * REP * D)
                    for n in range(REP):
                        at = (m * REP + n) * D
                        sp.dma_start(q_stack[at:at + D, :, :].rearrange("p h t -> p (h t)"), q[m]).then_inc(done, 16)
                    sp.dma_start(k_stack[rows, :, :].rearrange("p h t -> p (h t)"),
                                 k.rearrange("r d x -> (r d) x")).then_inc(done, 16)

            def quad_of(dram_ap, g):
                if isinstance(g, int):
                    return dram_ap[g]
                if len(dram_ap.shape) == 3:
                    return dram_ap[bass.ds(g, 1), :, :].rearrange("o a b -> (o a) b")
                return dram_ap[bass.ds(g, 1), :, :, :, :].rearrange("o r d h t -> (o r) d h t")

            def load_quad(k, par):
                g = par * (NQ // B) + k
                load_stack(QS[:, par, :, :], KS[:, par, :, :], g, stack_in[par])

            for b in range(B):
                store_parts(0, b)
                parts_stored(0, b)
                load_quad(0, b)
            with sp.Fori(0, NQ // 2 - 1) as j:
                sp.wait_ge(step_summed, (2 * j + 1) * NS)
                load_quad(j + 1, 0)
                sp.wait_ge(step_summed, (2 * j + 2) * NS)
                load_quad(j + 1, 1)

            sp.wait_ge(normed, NQ)
            for dst, src in ((gate_t[:, :], a["gate_t"]), (sg_t[:, :], a["sg_t"]), (su_t[:, :], a["su_t"]),
                             (sd_t[:, :, :], a["sd_t"].rearrange("(k p) d -> p k d", p=P))):
                sp.dma_start(dst, src).then_inc(moe_w_in, 16)

            def load_expert(e, k):
                for dst, name in ((wg, "wg_t"), (wu, "wu_t")):
                    sp.dma_start(dst[:, k, :], one_of(a[name], e)).then_inc(weights[k], 16)
                sp.dma_start(wd[:, k, :].rearrange("p (m d) -> p m d", d=P),
                             one_of(a["wd_t"], e).rearrange("(m p) d -> p m d", p=P)).then_inc(weights[k], 16)

            def one_of(ap, e):
                return ap[e] if isinstance(e, int) else ap[bass.ds(e, 1), :, :].rearrange("o a b -> (o a) b")

            for k in range(4):
                load_expert(k, k)
            for n in range(CH):
                sp.wait_ge(sh_sum, n + 1)
                sp.dma_start(moe_rows[n * BANK:(n + 1) * BANK, :].rearrange("(i p) d -> p i d", p=P),
                             Z[:, n * CT:(n + 1) * CT, :]).then_inc(sh_out, 16)
            sp.wait_ge(probs, 1)
            xs = xs_rows.rearrange("(i p) w -> p i w", p=P)
            sp.dma_start(xs[:, :, 0:P], X[:, :, :]).then_inc(xs_out, 16)
            sp.dma_start(xs[:, :, P:XW], S[:, :, :]).then_inc(xs_out, 16)
            with sp.Fori(0, E0 // 4 - 1) as j:
                for k in range(4):
                    sp.wait_ge(down_full, 4 * j + k + 1)
                    load_expert(4 * j + 4 + k, k)
            sp.wait_ge(scattered, 16 * NH * E0)
            sp.dma_start(Z[:, :, :], moe_rows.rearrange("(i p) d -> p i d", p=P)).then_inc(z_in, 16)

            for dst, src in ((w_down[:, 0:DC], a["w_dq"]), (w_down[:, DC:2 * DC], a["w_dkv"]),
                             (w_up[0:DC, 0, :], a["w_uq"]), (w_up[DC:2 * DC, 0, :], a["w_uk"]),
                             (w_up[DC:2 * DC, 1, :], a["w_uv"]), (w_proj[:, :], a["w_o"])):
                sp.dma_start(dst, src).then_inc(w2_in, 16)
            def load_max(k, par):
                g = par * (NQ // B) + k
                load_stack(QM[:, par, :, :], KM[:, par, :, :], g, max_in[par])

            def store_max(g):
                sp.wait_ge(m_sb, g + 1)
                sp.dma_start(quad_of(m_rows, g).rearrange("r (h t) -> h r t", t=P), mparts[:, :, :]).then_inc(m_out, 16)

            def load_exp(k, par):
                sp.wait_ge(m_out, 16 * (2 * k + par + 1))
                g = par * (NQ // B) + k
                load_stack(QE[:, par, :, :], KE[:, par, :, :], g, exp_in[par])
                sp.dma_start(QE[ROWS:MROWS, par, :, :].rearrange("r h t -> r (h t)"), quad_of(m_rows, 2 * k + par)
                             ).then_inc(exp_in[par], 16)

            for b in range(B):
                store_parts(1, b)
                parts_stored(1, b)
                load_max(0, b)
            sp.wait_ge(ones_set, 1)
            for par in range(2):
                sp.wait_ge(max_full, len(MAX) * (par + 1))
                load_max(1, par)
                store_max(par)
                load_exp(0, par)
            with sp.Fori(0, NQ // 2 - 2) as j:
                for par in range(2):
                    sp.wait_ge(max_full, len(MAX) * (2 * j + 3 + par))
                    load_max(j + 2, par)
                    store_max(2 * j + 2 + par)
                    sp.wait_ge(exp_summed, NS * (2 * j + 1 + par))
                    load_exp(j + 1, par)
            for par in range(2):
                store_max(NQ - 2 + par)
                sp.wait_ge(exp_summed, NS * (NQ - 3 + par))
                load_exp(NQ // 2 - 1, par)

            sp.wait_ge(e_normed, NQ)
            sp.dma_start(gate1[:, :], a["gate1"]).then_inc(f_gate_in, 16)

            def load_ffn(e, k):
                for dst, name in ((w1, "w1"), (w3, "w3")):
                    sp.dma_start(dst[:, k, :], one_of(a[name], e)).then_inc(f_win[k], 16)
                sp.dma_start(w2[:, k, :, :], one_of(a["w2"], e).rearrange("(m p) d -> p m d", p=P)
                             ).then_inc(f_win[k], 16)

            load_ffn(0, 0)
            load_ffn(1, 1)
            with sp.Fori(0, E1 // 2 - 1) as j:
                for k in range(2):
                    sp.wait_ge(f_y, CH * (2 * j + k + 1))
                    load_ffn(2 * j + 2 + k, k)
            sp.wait_ge(ln_x, 4)
            sp.dma_start(out.rearrange("(i p) d -> p i d", p=P), X[:, :, :]).then_inc(finish, 16)
            sp.wait_ge(finish, 16)

        @block.tensor
        def _(pe):
            pe.wait_ge(w_in, 16 * 6)
            for m in range(2 * B):
                b = m // 2
                pe.wait_ge(xT_in[b], 16)
                if m > 1:
                    pe.wait_ge(rest_done, m - 1)
                for n in range(T // BANK):
                    mm = pe.matmul(causal_ps[m % 2][:, n * BANK:(n + 1) * BANK],
                                   w_attn[:, (m % 2) * P:(m % 2 + 1) * P],
                                   XT[:, b * T + n * BANK:b * T + (n + 1) * BANK], start=True, stop=True)
                mm.then_inc(proj_full, 1)
                if m % 2:
                    at_least(pe, v_sb, b)
                    for i in range(KT):
                        mm = pe.matmul(tail_ps[:, i * P:(i + 1) * P], XT[:, b * T + i * P:b * T + (i + 1) * P],
                                       w_attn[:, 2 * P:3 * P], start=True, stop=True)
                    mm.then_inc(v_full, 1)
            pe.wait_ge(rest_done, 2 * REP * (B - 1) + 2)
            pe.wait_ge(v_sb, B)
            pe.wait_ge(consts, 2)

            def fill(g, par, j):
                s, kind, n = JOBS[j]
                at_least(pe, drained, NJ * g + PREV[j] + 1)
                if j == TURN_AT + HELD:
                    at_least(pe, normed, g)
                (causal if kind == "c" else tail)(slots[SLOT[j]], par, s, n).then_inc(filled, 1)

            def causal(slot, par, s, hh):
                for kt, c0, c1, q0 in score_cuts(s):
                    mm = pe.matmul(slot[:, c0:c1], KS[0:ROWS, par, hh, kt * P:(kt + 1) * P],
                                   QS[0:ROWS, par, hh, q0:q0 + c1 - c0], start=True, stop=True)
                return mm

            def tail(slot, par, s, n):
                i, hh = TAIL[n]
                w = T - (i + 1) * P
                for c0, c1 in cut(0, w, 0):
                    mm = pe.matmul(slot[:, c0:c1], QS[0:ROWS, par, hh, i * P:(i + 1) * P],
                                   KS[0:ROWS, par, hh, (i + 1) * P + c0:(i + 1) * P + c1], start=True, stop=True)
                return mm

            def sums(g, par, s, powered):
                rp, cuts = (par + s) % 2, value_cuts(s)

                def group(k):
                    kt, c0, qa, qb = cuts[k]
                    if k == 0 and powered:
                        pe.wait_ge(fourth_pool, NS * g + s + 1)
                        pe.wait_ge(fourth_dve, NS * g + s + 1)
                        if s == 0:
                            pe.wait_ge(v_ready, g + 1)
                    if k == 0 and not powered:
                        pe.wait_ge(drained, NJ * g + RELU_AT[s, HQ - 1] + 1)
                        if s == 0:
                            at_least(pe, acc_out, g)
                    for hh in range(HQ):
                        src, w = (R4, VS[:, par, kt, hh * VW:(hh + 1) * VW]) if powered else (R1, sum_sel[:, :])
                        last = powered and kt == STEPS[-2 if qb <= BANK else -1][0]
                        mm = pe.matmul(acc_ps[hh * VW:(hh + 1) * VW, qa:qb], w,
                                       src[:, rp, hh, c0:c0 + qb - qa],
                                       start=(kt == 0 and not powered), stop=last, tile_position=(0, hh * VW))
                    if k == len(cuts) - 1:
                        mm.then_inc(step_summed if powered else relu_summed, 1)
                return [lambda k=k: group(k) for k in range(len(cuts))]

            def turn(g, last=False):
                pe.wait_ge(acc_out, g + 1)
                pe.wait_ge(drained, NJ * (g + 1) + (PREV[TURN_AT + HELD] + 1 if not last else 0))
                for i in range(KT):
                    mm = pe.transpose(tail_ps[:, i * P:(i + 1) * P], Ysb[:, i * P:(i + 1) * P], ident[:, :])
                mm.then_inc(turned, 1)

            def quad(g, k, par, first=False):
                pe.wait_ge(stack_in[par], 16 * STACK_DMAS * (k + 1))
                for s in range(NS):
                    early = [] if first and s < 2 else (
                        sums(g, par, s - 2, True) if s >= 2 else sums(g - 1, 1 - par, NS - 2 + s, True))
                    late = [] if s == 1 or (first and s == 0) else (
                        sums(g, par, s - 1, False) if s else sums(g - 1, 1 - par, NS - 1, False))
                    if s == 1:
                        late = sums(g, par, 0, False)
                    jobs = []
                    for j in range(STEP_AT[s], STEP_AT[s + 1]):
                        if j == TURN_AT and not first:
                            jobs.append(lambda: turn(g - 1))
                        jobs.append(lambda j=j: fill(g, par, j))
                    at = EVAC_AT - STEP_AT[s] + 2 if s == 1 else 4
                    for job in jobs[:4] + early + jobs[4:at] + spread(jobs[at:], late):
                        job()

            quad(0, 0, 0, first=True)
            with pe.Fori(0, NQ // 2 - 1) as j:
                quad(2 * j + 1, j, 1)
                quad(2 * j + 2, j + 1, 0)
            quad(NQ - 1, NQ // 2 - 1, 1)
            for job in (sums(NQ - 1, 1, NS - 1, False) + sums(NQ - 1, 1, NS - 2, True)
                        + sums(NQ - 1, 1, NS - 1, True)):
                job()
            turn(NQ - 1, last=True)

            def project(layer):
                pe.wait_ge(e_normed if layer else normed, NQ)
                for n in range(CH + 1):
                    if n < CH:
                        at_least(pe, yt_sb, CH * layer + n - 1)
                        for i in range(CT):
                            t = n * CT + i
                            mm = pe.transpose(banks[n % 2][:, i * P:(i + 1) * P],
                                              Y[:, t // KT, t % KT, :],
                                              ident[:, :])
                        mm.then_inc(yt_full, 1)
                    if n:
                        pe.wait_ge(yt_sb, CH * layer + n)
                        at_least(pe, z_sb, CH * layer + n - 2 if n > 2 else 0)
                        for i in range(CT):
                            mm = pe.matmul(banks[2 + (n - 1) % 2][:, i * P:(i + 1) * P],
                                           YT[:, (n - 1) % 2, i * P:(i + 1) * P], w_proj[:, :], start=True, stop=True)
                        mm.then_inc(out_full, 1)

            def turn_x(layer):
                pe.wait_ge(ln_x, layer + 1)
                for n in range(CH):
                    for i in range(CT):
                        mm = pe.transpose(banks[4 + n][:, i * P:(i + 1) * P], X[:, n * CT + i, :], ident[:, :])
                    mm.then_inc(xt_full, 1)

            project(0)
            turn_x(0)

            pe.wait_ge(moe_w_in, 16 * 4)
            pe.wait_ge(xt_sb, CH)
            for i in range(NT):
                mm = pe.matmul(banks[0][:, i * E0:(i + 1) * E0], XT[:, i * P:(i + 1) * P], gate_t[:, :],
                               start=True, stop=True)
            mm.then_inc(logits, 1)
            pe.wait_ge(probs, 1)
            for h in range(2):
                mm = pe.transpose(banks[7][:, h * P:(h + 1) * P], S[:, 8 * h:8 * (h + 1), :], ident[:, :])
            mm.then_inc(sc_full, 1)
            pe.wait_ge(masks0, 3)

            def total(r):
                pe.wait_ge(counted, r + 1)
                pe.matmul(banks[0][:, 0:4], same_e[:, :], count[:, :], start=True, stop=True).then_inc(totalled, 1)

            with pe.Fori(0, CH) as n:
                for k in range(IS // P):
                    total(3 * n + k)
                    for w, o in ((sg_t, 1), (su_t, 2)):
                        mm = pe.matmul(banks[o + 2 * k], w[:, k * P:(k + 1) * P], XT[:, bass.ds(n * BANK, BANK)],
                                       start=True, stop=True)
                    mm.then_inc(sh_up, 1)
                total(3 * n + 2)
                pe.wait_ge(sh_hid, (n + 1) * (IS // P))
                for i in range(CT):
                    for k in range(IS // P):
                        mm = pe.matmul(banks[5][:, i * P:(i + 1) * P], hid_s[:, k, i * P:(i + 1) * P],
                                       sd_t[:, k, :], start=(k == 0), stop=(k == IS // P - 1))
                mm.then_inc(sh_down, 1)
            with pe.Fori(3 * CH, ROUNDS) as r:
                total(r)
            pe.wait_ge(found, 1)
            pe.transpose(banks[1][:, 0:P], thr[:, 0:1].bitcast(F32).broadcast_to([P, P]), ident[:, :]
                         ).then_inc(thr_full, 1)
            pe.wait_ge(marked, 2)
            for c, flag in ((0, above), (1, equal)):
                pe.matmul(banks[2][:, c * 2 * P:(c + 1) * 2 * P], before_t[:, :],
                          flag[:, :, :].rearrange("p i e -> p (i e)"), start=True, stop=False, skip_group_check=True)
                for h in range(2):
                    more = [(tile_counts[:, c, h:h + 1], before_e)]
                    if h:
                        more.append((tile_counts[:, c, 0:1], same_e))
                    if c:
                        more += [(tile_counts[:, 0, 0:1], same_e), (tile_counts[:, 0, 1:2], same_e)]
                    for n, (cnt, w) in enumerate(more):
                        mm = pe.matmul(banks[2][:, c * 2 * P + h * P:c * 2 * P + (h + 1) * P],
                                       cnt.broadcast_to([P, P]), w[:, :], start=False,
                                       stop=(h == 1 and n == len(more) - 1), skip_group_check=True)
            mm.then_inc(ranked, 1)
            pe.wait_ge(hot, 1)
            for q in range(2):
                for i in range(NT):
                    mm = pe.matmul(banks[3 + q][:, 0:P], hot_hi[:, i, q * P:(q + 1) * P], hot_lo[:, i, q * P:(q + 1) * P],
                                   start=(i == 0), stop=(i == NT - 1))
            mm.then_inc(listed, 1)
            pe.wait_ge(list_sb, 1)
            for q in range(2):
                for h in range(NH):
                    mm = pe.matmul(banks[5][:, (q * NH + h) * 8:(q * NH + h + 1) * 8],
                                   turned_l[:, q, h, :, :].rearrange("p a b -> p (a b)"), is_e[:, :],
                                   start=True, stop=True)
            mm.then_inc(idx_full, 1)
            pe.wait_ge(idx_sb, 1)

            def turn_tokens(j, k):
                pe.wait_ge(gathered[k], 16 * NH * (j + 1))
                if k >= 2:
                    at_least(pe, g_sb, 4 * j + k - 1)
                elif not isinstance(j, int) or j > 0:
                    pe.wait_ge(g_sb, 4 * j + k - 1)
                for h in range(NH):
                    mm = pe.transpose(banks[k % 2][:, h * P:(h + 1) * P], G[:, k, h, 0:P], ident[:, :])
                mm.then_inc(g_turned, 1)

            def expert_up(j, k):
                pe.wait_ge(weights[k], 16 * 3 * (j + 1))
                pe.wait_ge(g_sb, 4 * j + k + 1)
                for m in range(I0 // P):
                    if isinstance(j, int) and j == 0:
                        at_least(pe, hid_done, 4 * k + m - 3)
                    else:
                        pe.wait_ge(hid_done, 16 * j + 4 * k + m - 3)
                    for w, c in ((wg, 0), (wu, 1)):
                        mm = pe.matmul(banks[2 + m][:, c * CAP:(c + 1) * CAP], w[:, k, m * P:(m + 1) * P],
                                       GT[:, k % 2, :], start=True, stop=True)
                    mm.then_inc(up_full, 1)

            def expert_down(j, k):
                pe.wait_ge(hid_done, 16 * j + 4 * k + 4)
                if k >= 2 or not isinstance(j, int) or j > 0:
                    pe.wait_ge(out_sb, 4 * j + k - 1)
                for h in range(NH):
                    for m in range(I0 // P):
                        mm = pe.matmul(banks[6 + k % 2][:, h * P:(h + 1) * P], hid_e[:, k % 2, m, h * P:(h + 1) * P],
                                       wd[:, k, m * P:(m + 1) * P], start=(m == 0), stop=(m == I0 // P - 1))
                mm.then_inc(down_full, 1)

            def four_experts(j):
                turn_tokens(j, 0)
                turn_tokens(j, 1)
                expert_up(j, 0)
                for k in range(1, 4):
                    expert_up(j, k)
                    expert_down(j, k - 1)
                    if k < 3:
                        turn_tokens(j, k + 1)
                expert_down(j, 3)

            four_experts(0)
            with pe.Fori(1, E0 // 4) as j:
                four_experts(j)

            turn_x(1)
            pe.wait_ge(w2_in, 16 * 6)
            pe.wait_ge(xt_sb, 2 * CH)
            for n in range(CH):
                mm = pe.matmul(banks[n][0:2 * DC, :], w_down[:, :], XT[:, n * BANK:(n + 1) * BANK], start=True, stop=True)
                mm.then_inc(lat_full, 1)
            pe.wait_ge(lat_sb, CH)
            for m in range(2 * B):
                b, r0 = m // 2, DC * (m % 2)
                if m > 1:
                    pe.wait_ge(rest_done, 2 * REP * B + m - 1)
                for n in range(T // BANK):
                    mm = pe.matmul(causal_ps[m % 2][:, n * BANK:(n + 1) * BANK], w_up[r0:r0 + DC, 0, :],
                                   latent[r0:r0 + DC, b * T + n * BANK:b * T + (n + 1) * BANK], start=True, stop=True)
                mm.then_inc(proj_full, 1)
                if m % 2:
                    at_least(pe, v_sb, B + b if b else 0)
                    for i in range(KT):
                        mm = pe.matmul(tail_ps[:, i * P:(i + 1) * P], latent[DC:2 * DC, b * T + i * P:b * T + (i + 1) * P],
                                       w_up[DC:2 * DC, 1, :], start=True, stop=True)
                    mm.then_inc(v_full, 1)
            pe.wait_ge(rest_done, 2 * REP * (2 * B - 1) + 2)
            pe.wait_ge(v_sb, 2 * B)

            def row_scores(g, par, n):
                hh, c = MAX[n]
                half = n % 2
                at_least(pe, max_done, len(MAX) * g + n - 1)
                if n < 2:
                    at_least(pe, m_sb, g)
                    at_least(pe, e_normed, g - 3)
                at = half * BANK
                for i, k0, w in MAX_JOBS[c][1]:
                    diag = k0 + w == (i + 1) * P
                    mm = pe.matmul(tail_ps[:, at:at + w], QM[0:ROWS, par, hh, i * P:(i + 1) * P],
                                   KM[0:ROWS, par, hh, k0:k0 + w], start=True, stop=not diag, skip_group_check=True)
                    if diag:
                        mm = pe.matmul(tail_ps[:, at + w - P:at + w], mask[:, :], identb[:, :],
                                       start=False, stop=True, skip_group_check=True)
                    at += w
                mm.then_inc(max_full, 1)

            def turn_max(g):
                pe.wait_ge(mx_ready, g + 1)
                pe.transpose(tail_ps[0:HQ * KT, 0:P], mxt[:, :, :], ident[:, :]).then_inc(mx_full, 1)

            def exp_scores(g, par, s, hh):
                at_least(pe, exp_done, HQ * NS * g + HQ * s + hh - 1)
                cuts = score_cuts(s)
                for n, (kt, c0, c1, q0) in enumerate(cuts):
                    mm = pe.matmul(causal_ps[hh % 2][:, c0:c1], KE[0:MROWS, par, hh, kt * P:(kt + 1) * P],
                                   QE[0:MROWS, par, hh, q0:q0 + c1 - c0], start=True, stop=q0 != kt * P,
                                   skip_group_check=True)
                    if q0 == kt * P:
                        mm = pe.matmul(causal_ps[hh % 2][:, c0:c0 + P], identb[:, :], mask[:, :],
                                       start=False, stop=True, skip_group_check=True)
                mm.then_inc(exp_full, 1)

            def exp_sums(g, par, s):
                rp, cuts = (par + s) % 2, value_cuts(s)

                def group(k):
                    kt, c0, qa, qb = cuts[k]
                    if k == 0:
                        pe.wait_ge(exp_done, HQ * NS * g + HQ * (s + 1))
                        if s == 0:
                            at_least(pe, e_out, g)
                            pe.wait_ge(v_ready, NQ + g + 1)
                    for hh in range(HQ):
                        mm = pe.matmul(acc_ps[hh * VW:(hh + 1) * VW, qa:qb], VS[:, par, kt, hh * VW:(hh + 1) * VW],
                                       EX[:, rp, hh, c0:c0 + qb - qa], start=(kt == 0),
                                       stop=(kt == STEPS[-2 if qb <= BANK else -1][0]), tile_position=(0, hh * VW))
                    if k == len(cuts) - 1:
                        mm.then_inc(exp_summed, 1)
                return [lambda k=k: group(k) for k in range(len(cuts))]

            def turn_exp(g):
                pe.wait_ge(e_out, g + 1)
                for i in range(KT):
                    mm = pe.transpose(tail_ps[:, i * P:(i + 1) * P], Esb[:, i * P:(i + 1) * P], ident[:, :])
                mm.then_inc(e_turned, 1)

            def run_all(jobs):
                for job in jobs:
                    job()

            def max_part(g, par, s):
                return [lambda n=n: row_scores(g, par, n) for n in range(MAX_AT[s], MAX_AT[s + 1])]

            def exp_step(g, par, s):
                return [lambda hh=hh: exp_scores(g, par, s, hh) for hh in range(HQ)]

            pe.wait_ge(masks0, 5)
            for g in range(2):
                pe.wait_ge(max_in[g], 16 * STACK_DMAS)
                for s in range(NS):
                    run_all(max_part(g, g, s))
                pe.wait_ge(max_done, len(MAX) * (g + 1))
                turn_max(g)

            def exp_quad(g, k, par, with_max, first=False):
                pe.wait_ge(exp_in[par], 16 * (STACK_DMAS + 1) * (k + 1))
                if with_max:
                    pe.wait_ge(max_in[par], 16 * STACK_DMAS * (k + 2))
                for s in range(NS):
                    back = [] if s == 0 and first else exp_sums(g, par, s - 1) if s else exp_sums(g - 1, 1 - par, NS - 1)
                    jobs = exp_step(g, par, s)
                    if with_max:
                        jobs = spread(max_part(g + 2, par, s), jobs)
                    run_all(spread(jobs, back))
                if with_max:
                    pe.wait_ge(max_done, len(MAX) * (g + 3))
                    turn_max(g + 2)
                if not first:
                    pe.wait_ge(m_sb, g + 3 if with_max else NQ)
                    at_least(pe, e_normed, g - 1)
                    turn_exp(g - 1)

            exp_quad(0, 0, 0, True, first=True)
            exp_quad(1, 0, 1, True)
            with pe.Fori(1, NQ // 2 - 1) as j:
                exp_quad(2 * j, j, 0, True)
                exp_quad(2 * j + 1, j, 1, True)
            exp_quad(NQ - 2, NQ // 2 - 1, 0, False)
            exp_quad(NQ - 1, NQ // 2 - 1, 1, False)
            run_all(exp_sums(NQ - 1, 1, NS - 1))
            pe.wait_ge(e_normed, NQ - 1)
            turn_exp(NQ - 1)
            project(1)
            turn_x(2)

            pe.wait_ge(f_gate_in, 16)
            pe.wait_ge(xt_sb, 3 * CH)
            for i in range(NT):
                mm = pe.matmul(banks[0][:, i * E1:(i + 1) * E1], XT[:, i * P:(i + 1) * P], gate1[:, :],
                               start=True, stop=True)
            mm.then_inc(f_logits, 1)
            pe.wait_ge(f_max, 2)

            KF = F1 // P

            def ffn_up(e, k, n, first):
                for m in range(KF):
                    c = CH * KF * e + KF * n + m
                    ring = (KF * n + m) % 2
                    if not (first and n == 0):
                        pe.wait_ge(f_hid, c - 1)
                    for w, o in ((w1, 0), (w3, 1)):
                        mm = pe.matmul(banks[2 * ring + o], w[:, k, m * P:(m + 1) * P],
                                       XT[:, n * BANK:(n + 1) * BANK], start=True, stop=True)
                    mm.then_inc(f_up, 1)

            def ffn_down(e, k, n, first):
                pe.wait_ge(f_hid, CH * KF * e + KF * (n + 1))
                if not (first and n < 2):
                    pe.wait_ge(f_acc, CH * e + n - 1)
                for i in range(CT):
                    for m in range(KF):
                        mm = pe.matmul(banks[4 + n % 2][:, i * P:(i + 1) * P], hid_f[:, n % 2, m, i * P:(i + 1) * P],
                                       w2[:, k, m, :], start=(m == 0), stop=(m == KF - 1))
                mm.then_inc(f_y, 1)

            def ffn_two(e, kk, first):
                for k in range(2):
                    pe.wait_ge(f_win[k], 16 * 3 * (kk + 1))
                    first_k = first and k == 0
                    ffn_up(e + k, k, 0, first_k)
                    for n in range(CH):
                        if n + 1 < CH:
                            ffn_up(e + k, k, n + 1, False)
                        ffn_down(e + k, k, n, first_k)

            ffn_two(0, 0, True)
            with pe.Fori(1, E1 // 2) as j:
                ffn_two(2 * j, j, False)

        @block.scalar
        def _(act):
            def cut_parts(layer, values):
                for b in range(B):
                    for n in range(REP):
                        for m in range(2):
                            act.wait_ge(rest_done, 2 * REP * (B * layer + b) + 2 * n + m + 1)
                            at_least(act, part_out[m][n], PARTS_OUT * (B * layer + b))
                            act.activation(pt[:, m, n, :], values[:, 2 * b + m, :], ACT.Copy).then_inc(part_done, 1)

            cut_parts(0, proj)

            def drain(g, par, j):
                s, kind, n = JOBS[j]
                if j == 0:
                    at_least(act, normed, g - 1)
                if (kind, n) == ("c", 0):
                    at_least(act, relu_summed, NS * g + s - 1)
                    at_least(act, square_done, 2 * (NS * g + s - 1))
                if kind == "u":
                    at_least(act, drained, NJ * g + (TAIL_JOB[n - 3] + 1 if n >= 3 else 0))
                act.wait_ge(filled, NJ * g + j + 1)
                (keep if kind == "c" else add_up)(slots[SLOT[j]], par, s, n).then_inc(drained, 1)

            def keep(slot, par, s, hh):
                rp, width = (par + s) % 2, pieces(s)[1]
                return act.activation(R1[:, rp, hh, 0:width], slot[:, 0:width], ACT.Relu)

            def add_up(slot, par, s, n):
                i, hh = TAIL[n]
                return act.activation(junk[:, n % 3, 0:T - (i + 1) * P], slot[:, 0:T - (i + 1) * P], ACT.Relu,
                                      accum_out=tails[:, par, i, hh:hh + 1])

            def evacuate(g):
                act.wait_ge(step_summed, NS * (g + 1))
                at_least(act, turned, g)
                act.activation(Ysb[:, :], acc_ps[:, :], ACT.Copy).then_inc(acc_out, 1)

            def quad(g, par, first=False):
                for j in range(NJ):
                    if j == EVAC_AT and not first:
                        evacuate(g - 1)
                    drain(g, par, j)

            quad(0, 0, first=True)
            quad(1, 1)
            with act.Fori(1, NQ // 2) as j:
                quad(2 * j, 0)
                quad(2 * j + 1, 1)
            evacuate(NQ - 1)

            def project(layer):
                for n in range(CH):
                    act.wait_ge(yt_full, CH * layer + n + 1)
                    at_least(act, out_full, CH * layer + n - 1 if n > 1 else 0)
                    act.activation(YT[:, n % 2, :], banks[n % 2], ACT.Copy).then_inc(yt_sb, 1)

            def deviation(layer):
                act.wait_ge(ln_var, layer + 1)
                act.activation(spread_sb[:, 0, :], mean_var[:, :, 1], ACT.Sqrt, bias=eps_ln[:, 0:1]).then_inc(ln_std, 1)

            def copy_xt(layer):
                for n in range(CH):
                    act.wait_ge(xt_full, CH * layer + n + 1)
                    act.activation(XT[:, n * BANK:(n + 1) * BANK], banks[4 + n], ACT.Copy).then_inc(xt_sb, 1)

            project(0)
            deviation(0)
            copy_xt(0)

            act.wait_ge(row_max, 1)
            act.activation(S[:, :, :], S[:, :, :], ACT.Exp).then_inc(exps, 1)
            with act.Fori(0, CH) as n:
                for k in range(IS // P):
                    act.wait_ge(sh_up, n * (IS // P) + k + 1)
                    act.activation(act_s[:, k, :], banks[1 + 2 * k], ACT.Gelu).then_inc(sh_act, 1)

            def gelu_expert(j, k):
                for m in range(I0 // P):
                    act.wait_ge(up_full, 16 * j + 4 * k + m + 1)
                    if k > 0 or not isinstance(j, int) or j > 0:
                        act.wait_ge(hid_done, 16 * j + 4 * k + m - 3)
                    act.activation(act_e[:, m, :], banks[2 + m][:, 0:CAP], ACT.Gelu).then_inc(gelu_done, 1)

            for k in range(4):
                gelu_expert(0, k)
            with act.Fori(1, E0 // 4) as j:
                for k in range(4):
                    gelu_expert(j, k)
            deviation(1)
            copy_xt(1)

            for n in range(CH):
                act.wait_ge(lat_full, n + 1)
                act.activation(latent[:, n * BANK:(n + 1) * BANK], banks[n][0:2 * DC, :], ACT.Copy).then_inc(lat_sb, 1)
            cut_parts(1, projE)

            def exps_of(g, par, s, hh):
                rp, width = (par + s) % 2, pieces(s)[1]
                act.wait_ge(exp_full, HQ * NS * g + HQ * s + hh + 1)
                if hh == 0:
                    at_least(act, exp_summed, NS * g + s - 1)
                act.activation(EX[:, rp, hh, 0:width], causal_ps[hh % 2][:, 0:width], ACT.Exp,
                               scale=float(D) ** -0.5).then_inc(exp_done, 1)

            def exp_evacuate(g):
                act.wait_ge(exp_summed, NS * (g + 1))
                at_least(act, e_turned, g)
                act.activation(Esb[:, :], acc_ps[:, :], ACT.Copy).then_inc(e_out, 1)

            def exp_quad(g, par, first=False):
                for s in range(NS):
                    for hh in range(HQ):
                        exps_of(g, par, s, hh)
                    if s == 0 and not first:
                        exp_evacuate(g - 1)

            exp_quad(0, 0, first=True)
            exp_quad(1, 1)
            with act.Fori(1, NQ // 2 - 1) as j:
                exp_quad(2 * j, 0)
                exp_quad(2 * j + 1, 1)
            exp_quad(NQ - 2, 0)
            exp_quad(NQ - 1, 1)
            exp_evacuate(NQ - 1)
            project(1)
            deviation(2)
            copy_xt(2)

            act.wait_ge(f_max, 1)
            act.activation(GG[:, :, :], GG[:, :, :], ACT.Exp).then_inc(f_exp, 1)
            KF = F1 // P

            def silus(e, first):
                for c in range(CH * KF):
                    act.wait_ge(f_up, CH * KF * e + c + 1)
                    if not (first and c < 2):
                        act.wait_ge(f_hid, CH * KF * e + c - 1)
                    act.activation(act_f[:, c % 2, :], banks[2 * (c % 2)], ACT.Silu).then_inc(f_act, 1)

            silus(0, True)
            with act.Fori(1, E1) as e:
                silus(e, False)
            deviation(3)

        @block.vector
        def _(dve):
            chained = [0]

            def link(ins):
                ins.then_inc(dve_chain, 1)
                chained[0] += 1
                dve.wait_ge(dve_chain, chained[0])

            dve.memset(eps_ln[:, :], EPS_LN)
            dve.memset(tails[:, :, :, :], 0.0)
            dve.memset(ident[:, :], 1.0)
            dve.memset(sum_sel[:, :], 0.0).then_inc(consts, 1)
            dve.wait_ge(consts, 1)
            dve.memset(sum_sel[:, D + 1:D + 2], 1.0)
            dve.wait_ge(w_in, 16 * 6)
            link(dve.tensor_scalar(gain_tmp[:, :], gain[:, :], 0.0, 2.0, ALU.is_ge, ALU.mult))
            dve.tensor_scalar(gain_sign[:, :], gain_tmp[:, :], -1.0, None, ALU.add)
            link(dve.reciprocal(gain_inv[:, :], gain[:, :]))

            def take_rests(layer, b, values):
                for n in range(REP - 1):
                    for m in range(2):
                        f = values[:, 2 * b + m, :]
                        dve.wait_ge(part_done, 2 * REP * (B * layer + b) + 2 * n + m + 1)
                        dve.tensor_tensor(f, f, pt[:, m, n, :], ALU.subtract).then_inc(rest_done, 1)

            for b in range(B):
                q, k = proj[:, 2 * b, :], proj[:, 2 * b + 1, :]
                dve.wait_ge(proj_full, 2 * b + 1)
                dve.tensor_scalar(q, causal_ps[0][:, :], b_cols[:, 0:1], gain_sign[:, :],
                                  ALU.add, ALU.mult).then_inc(rest_done, 1)
                dve.wait_ge(proj_full, 2 * b + 2)
                link(dve.tensor_scalar(k, causal_ps[1][:, :], b_cols[:, 1:2], 0.0, ALU.add, ALU.add,
                                       accum_out=k_sum[:, :]))
                link(dve.tensor_scalar(k_mean[:, :], k_sum[:, :], 1.0 / T, None, ALU.mult))
                dve.tensor_scalar(k, k, k_mean[:, :], None, ALU.subtract).then_inc(rest_done, 1)
                take_rests(0, b, proj)
                dve.wait_ge(v_full, b + 1)
                dve.tensor_tensor(Y[:, b, :, :], tail_ps[:, :].rearrange("p (i c) -> p i c", c=P),
                                  b_v[:, :].unsqueeze(1).broadcast_to([P, KT, P]), ALU.add).then_inc(v_sb, 1)
            dve.wait_ge(upto_ready, 2)

            def square(g, par, s):
                rp, width = (par + s) % 2, pieces(s)[1]
                at_least(dve, step_summed, NS * g + s - 1)
                for h0 in (0, 2):
                    dve.wait_ge(drained, NJ * g + RELU_AT[s, h0 + 1] + 1)
                    dve.tensor_tensor(R4[:, rp, h0:h0 + 2, 0:width], R1[:, rp, h0:h0 + 2, 0:width],
                                      R1[:, rp, h0:h0 + 2, 0:width], ALU.mult).then_inc(square_done, 1)
                    dve.wait_ge(square_done, 2 * NS * g + 2 * s + h0 // 2 + 1)
                    for kt, at, _ in pieces(s)[0]:
                        ins = dve.tensor_tensor(R4[:, rp, h0:h0 + 2, at:at + P], R4[:, rp, h0:h0 + 2, at:at + P],
                                                upto[:, :].unsqueeze(1).broadcast_to([P, 2, P]), ALU.mult)
                    ins.then_inc(mask_done, 1)

            def fourth(g, par, s):
                rp, width, h0 = (par + s) % 2, pieces(s)[1], POOL_HEADS[s]
                dve.wait_ge(mask_done, 2 * NS * g + 2 * s + 2)
                dve.tensor_tensor(R4[:, rp, h0:HQ, 0:width], R4[:, rp, h0:HQ, 0:width],
                                  R4[:, rp, h0:HQ, 0:width], ALU.mult).then_inc(fourth_dve, 1)

            def y_of(k, par):
                heads = slice(HQ * D * k, HQ * D * (k + 1)) if isinstance(k, int) else bass.ds(k * (HQ * D), HQ * D)
                return Y[:, par, :, heads].rearrange("p i (h d) -> p i h d", d=D)

            def before(k, par):
                return (k, 0) if par else (k - 1, 1)

            def normalise(k, par):
                got = tail_ps[:, :].rearrange("p (i h w) -> p i h w", i=KT, w=VW)
                g = 2 * k + par
                sums, z, z2, z4, den, w = [nrm[:, n, :].rearrange("p (i h) -> p i h", h=HQ) for n in range(6)]
                dve.wait_ge(turned, g + 1)

                def then(ins):
                    ins.then_inc(dve_chain, 1)
                    step[0] += 1
                    dve.wait_ge(dve_chain, base + per * g + step[0])
                base, per, step = chained[0], 7, [0]
                then(dve.tensor_tensor(sums, got[:, :, :, D + 1], tails[:, par, :, :], ALU.add))
                then(dve.tensor_scalar(z, sums, 2.0 / T, 1e-6, ALU.mult, ALU.add))
                then(dve.tensor_scalar(z, z, gain_inv[:, 0:1], None, ALU.mult))
                then(dve.tensor_tensor(z2, z, z, ALU.mult))
                then(dve.tensor_tensor(z4, z2, z2, ALU.mult))
                then(dve.scalar_tensor_tensor(den, z4, 1e-6, got[:, :, :, D], ALU.mult, ALU.add))
                then(dve.reciprocal(w, den))
                dve.tensor_tensor(y_of(k, par), got[:, :, :, 0:D],
                                  w.unsqueeze(3).broadcast_to([P, KT, HQ, D]), ALU.mult).then_inc(normed, 1)

            def quad(k, par, first=False):
                g = 2 * k + par
                for s in range(NS):
                    if s == NORM_AT and not first:
                        normalise(*before(k, par))
                    square(g, par, s)
                    fourth(g, par, s)

            quad(0, 0, first=True)
            with dve.Fori(0, NQ // 2 - 1) as j:
                quad(j, 1)
                quad(j + 1, 0)
            quad(NQ // 2 - 1, 1)
            normalise(NQ // 2 - 1, 1)
            chained[0] += 7 * NQ

            def residual(layer):
                for n in range(CH):
                    dve.wait_ge(out_full, CH * layer + n + 1)
                    dve.tensor_tensor(Z[:, n * CT:(n + 1) * CT, :], X[:, n * CT:(n + 1) * CT, :],
                                      banks[2 + n % 2].rearrange("p (i d) -> p i d", d=P), ALU.add).then_inc(z_sb, 1)

            def layer_norm(layer):
                for i in range(NT):
                    dve.bn_stats(stats[:, i, :], Z[:, i, :]).then_inc(ln_stat, 1)
                for i in range(NT):
                    dve.wait_ge(ln_stat, NT * layer + i + 1)
                    ins = dve.bn_aggr(mean_var[:, i, :], stats[:, i, :])
                ins.then_inc(ln_var, 1)
                dve.wait_ge(ln_std, layer + 1)
                dve.reciprocal(spread_sb[:, 1, :], spread_sb[:, 0, :]).then_inc(ln_rec, 1)
                dve.wait_ge(ln_rec, layer + 1)
                dve.wait_ge(ln_var, layer + 1)
                for i in range(NT):
                    ins = dve.tensor_scalar(X[:, i, :], Z[:, i, :], mean_var[:, i, 0:1], spread_sb[:, 1, i:i + 1],
                                            ALU.subtract, ALU.mult)
                ins.then_inc(ln_x, 1)

            dve.wait_ge(res_in, 1)
            residual(0)
            dve.wait_ge(z_sb, CH)
            layer_norm(0)

            dve.wait_ge(logits, 1)
            got = banks[0][:, 0:NT * E0].rearrange("p (i e) -> p i e", e=E0)
            link(dve.tensor_reduce(row1[:, :], got, AX.X, ALU.max))
            dve.tensor_tensor(S[:, :, :], got, row1[:, :].unsqueeze(2).broadcast_to([P, NT, E0]),
                              ALU.subtract).then_inc(row_max, 1)
            dve.wait_ge(exps, 1)
            link(dve.tensor_reduce(row2[:, :], S[:, :, :], AX.X, ALU.add))
            link(dve.reciprocal(row3[:, :], row2[:, :]))
            dve.tensor_tensor(S[:, :, :], S[:, :, :], row3[:, :].unsqueeze(2).broadcast_to([P, NT, E0]),
                              ALU.mult).then_inc(probs, 1)
            dve.wait_ge(sc_full, 1)
            link(dve.tensor_copy(SC[:, :, :].rearrange("p h t -> p (h t)"), banks[7][:, 0:2 * P]))
            for c in range(4):
                dve.memset(two_bits[:, c:c + 1], c << (SCORE_BITS - 2))
                dve.memset(cand[:, c:c + 1], c << (SCORE_BITS - 2))
            link(dve.memset(count[:, 0:1], float(CAP)))
            sc_all = SC[:, :, :].rearrange("p h t -> p (h t)")

            def search_round(r, between=None):
                for c in range(1, 4):
                    ins = dve.tensor_scalar(over[:, 2 * P * (c - 1):2 * P * c], sc_all, cand[:, c:c + 1].bitcast(F32), 0.0,
                                            ALU.is_ge, ALU.add, accum_out=count[:, c:c + 1])
                ins.then_inc(counted, 1)
                dve.tensor_scalar(two_bits[:, :], two_bits[:, :], 2, None, ALU.logical_shift_right).then_inc(search, 1)
                if between:
                    between()
                dve.wait_ge(totalled, r + 1)
                dve.scalar_tensor_tensor(reached[:, :], banks[0][:, 0:4], CAP - 0.5, cand[:, :].bitcast(F32),
                                         ALU.is_ge, ALU.mult).then_inc(search, 1)
                dve.wait_ge(search, 4 * r + 2)
                dve.tensor_reduce(thr[:, :].bitcast(F32), reached[:, :], AX.X, ALU.max).then_inc(search, 1)
                dve.wait_ge(search, 4 * r + 3)
                dve.tensor_tensor(cand[:, :], two_bits[:, :], thr[:, 0:1].broadcast_to([P, 4]),
                                  ALU.bitwise_or).then_inc(search, 1)
                dve.wait_ge(search, 4 * r + 4)

            def shared_hidden(n, k):
                dve.wait_ge(sh_act, n * (IS // P) + k + 1)
                dve.tensor_tensor(hid_s[:, k, :], act_s[:, k, :], banks[2 + 2 * k], ALU.mult).then_inc(sh_hid, 1)

            def shared_out(n):
                dve.wait_ge(sh_down, n + 1)
                dve.tensor_tensor(Z[:, bass.ds(n * CT, CT), :], X[:, bass.ds(n * CT, CT), :],
                                  banks[5].rearrange("p (i d) -> p i d", d=P), ALU.add).then_inc(sh_sum, 1)

            search_round(0)
            with dve.Fori(0, CH) as n:
                search_round(3 * n + 1, lambda: shared_hidden(n, 0))
                search_round(3 * n + 2, lambda: shared_hidden(n, 1))
                search_round(3 * n + 3, lambda: shared_out(n))
            with dve.Fori(3 * CH + 1, ROUNDS) as r:
                search_round(r)
            dve.nop().then_inc(found, 1)
            for c, op in ((0, ALU.is_gt), (1, ALU.is_equal)):
                for h in range(2):
                    dve.tensor_scalar(over[:, (2 * c + h) * P:(2 * c + h + 1) * P], SC[:, h, :], thr[:, 0:1].bitcast(F32), 0.0, op,
                                      ALU.add, accum_out=tile_counts[:, c, h:h + 1])
            dve.wait_ge(thr_full, 1)
            link(dve.tensor_copy(thr_t[:, :], banks[1][:, 0:E0]))
            for flag, op in ((above, ALU.is_gt), (equal, ALU.is_equal)):
                dve.tensor_tensor(flag[:, :, :], S[:, :, :], thr_t[:, :].unsqueeze(1).broadcast_to([P, NT, E0]), op
                                  ).then_inc(marked, 1)
            dve.wait_ge(ranked, 1)
            dve.wait_ge(marked, 2)
            big = float(2 * B * T)
            dve.scalar_tensor_tensor(rank_a[:, :], banks[2][:, 0:2 * P], -big,
                                     above[:, :, :].rearrange("p i e -> p (i e)"), ALU.add, ALU.mult)
            link(dve.scalar_tensor_tensor(rank_b[:, :], banks[2][:, 2 * P:4 * P], -big,
                                          equal[:, :, :].rearrange("p i e -> p (i e)"), ALU.add, ALU.mult))
            link(dve.scalar_tensor_tensor(slot[:, :], rank_a[:, :], big, rank_b[:, :], ALU.add, ALU.add))
            link(dve.tensor_scalar(slot_hi[:, :], slot[:, :], 4, None, ALU.logical_shift_right))
            link(dve.tensor_scalar(slot_lo[:, :], slot[:, :], 15, None, ALU.bitwise_and))
            link(dve.tensor_copy(hi_f[:, :], slot_hi[:, :]))
            link(dve.tensor_copy(lo_f[:, :], slot_lo[:, :]))
            dve.wait_ge(masks0, 4)
            for hot_x, val in ((hot_hi, hi_f), (hot_lo, lo_f)):
                link(dve.tensor_tensor(hot_x[:, :, :].rearrange("p i (e s) -> p (i e) s", s=16),
                                       val[:, :].unsqueeze(2).broadcast_to([P, NT * E0, 16]),
                                       iota16[:, :].unsqueeze(1).broadcast_to([P, NT * E0, 16]), ALU.is_equal))
            dve.tensor_tensor(hot_hi[:, :, :], hot_hi[:, :, :], token[:, :].unsqueeze(2).broadcast_to([P, NT, E0 * 16]),
                              ALU.mult).then_inc(hot, 1)
            dve.wait_ge(listed, 1)
            for q in range(2):
                link(dve.tensor_tensor(picked[:, q, :, :], banks[3 + q][:, 0:P].rearrange("p (e b) -> p e b", b=16),
                                       own_e[:, :, :], ALU.mult))
                link(dve.tensor_reduce(lists[:, q, :], picked[:, q, :, :].rearrange("p e b -> p b e"), AX.X, ALU.add))
                for h in range(NH):
                    ins = dve.tensor_tensor(turned_l[:, q, h, :, :], own_hi[:, :, :],
                                            lists[:, q, h * 8:(h + 1) * 8].unsqueeze(1).broadcast_to([P, 16, 8]),
                                            ALU.mult)
            ins.then_inc(list_sb, 1)
            dve.wait_ge(idx_full, 1)
            dve.tensor_copy(idx[:, :, :].rearrange("p (q e) h -> p q h e", q=2),
                            banks[5][:, 0:2 * NH * 8].rearrange("p (q h e) -> p q h e", q=2, e=8)).then_inc(idx_sb, 1)

            def take_tokens(j, k):
                dve.wait_ge(g_turned, 4 * j + k + 1)
                if k >= 2 or not isinstance(j, int) or j > 0:
                    dve.wait_ge(up_full, 16 * j + 4 * (k - 1))
                col = P + 4 * j + k
                w_col = G[:, k, :, col:col + 1] if isinstance(j, int) else G[:, k, :, bass.ds(col, 1)]
                dve.tensor_copy(w_tok[:, k, :].unsqueeze(2), w_col)
                dve.tensor_copy(GT[:, k % 2, :], banks[k % 2][:, 0:CAP]).then_inc(g_sb, 1)

            def hidden(j, k):
                for m in range(I0 // P):
                    dve.wait_ge(gelu_done, 16 * j + 4 * k + m + 1)
                    if m == 0 and (k >= 2 or not isinstance(j, int) or j > 0):
                        dve.wait_ge(down_full, 4 * j + k - 1)
                    dve.tensor_tensor(hid_e[:, k % 2, m, :], act_e[:, m, :], banks[2 + m][:, CAP:2 * CAP],
                                      ALU.mult).then_inc(hid_done, 1)

            def weigh(j, k):
                dve.wait_ge(down_full, 4 * j + k + 1)
                if k >= 2 or not isinstance(j, int) or j > 0:
                    dve.wait_ge(scattered, 16 * NH * (4 * j + k - 1))
                for h in range(NH):
                    ins = dve.tensor_scalar(out_e[:, k % 2, h, :], banks[6 + k % 2][:, h * P:(h + 1) * P],
                                            w_tok[:, k, h:h + 1], None, ALU.mult)
                ins.then_inc(out_sb, 1)

            def four_experts(j):
                take_tokens(j, 0)
                take_tokens(j, 1)
                hidden(j, 0)
                for k in range(1, 4):
                    hidden(j, k)
                    weigh(j, k - 1)
                    if k < 3:
                        take_tokens(j, k + 1)
                weigh(j, 3)

            four_experts(0)
            with dve.Fori(1, E0 // 4) as j:
                four_experts(j)
            dve.wait_ge(z_in, 16)
            layer_norm(1)

            dve.wait_ge(w2_in, 16 * 6)
            dve.memset(KE[64:96, :, :, :], 1.0).then_inc(ones_set, 1)
            for b in range(B):
                for m in range(2):
                    dve.wait_ge(proj_full, 2 * (B + b) + m + 1)
                    dve.tensor_copy(projE[:, 2 * b + m, :], causal_ps[m][:, :]).then_inc(rest_done, 1)
                take_rests(1, b, projE)
                dve.wait_ge(v_full, B + b + 1)
                dve.tensor_copy(Y[:, b, :, :], tail_ps[:, :].rearrange("p (i c) -> p i c", c=P)).then_inc(v_sb, 1)

            def row_max_of(g, par, n):
                hh, c = MAX[n]
                (o0, step, cnt), groups = MAX_JOBS[c]
                w, half = groups[0][2], n % 2
                dve.wait_ge(max_full, len(MAX) * g + n + 1)
                dst = mx[:, par, hh, o0:o0 + step * (cnt - 1) + 1:step]
                dve.tensor_reduce(dst, tail_ps[:, half * BANK:half * BANK + cnt * w].rearrange("p (c w) -> p c w", w=w),
                                  AX.X, ALU.max, negate=True).then_inc(max_done, 1)

            def parts_of_max(g, par):
                dve.wait_ge(max_done, len(MAX) * (g + 1))
                at_least(dve, mx_full, g)
                dve.tensor_copy(mxt[:, :, 0:CT], mx[:, par, :, 0:CT])
                dve.tensor_tensor(mxt[:, :, CT:KT], mx[:, par, :, CT:KT], mx[:, par, :, KT:12], ALU.min
                                  ).then_inc(mx_ready, 1)
                dve.wait_ge(mx_full, g + 1)
                if not isinstance(g, int) or g > 0:
                    dve.wait_ge(m_out, 16 * g)
                src = tail_ps[0:HQ * KT, 0:P]

                def then(n, ins):
                    ins.then_inc(m_chain, 1)
                    dve.wait_ge(m_chain, 4 * g + n)
                then(1, dve.tensor_copy(mparts[:, 0, :], src))
                then(2, dve.tensor_tensor(mrest[:, :], src, mparts[:, 0, :], ALU.subtract))
                then(3, dve.tensor_copy(mparts[:, 1, :], mrest[:, :]))
                then(4, dve.tensor_tensor(mrest[:, :], mrest[:, :], mparts[:, 1, :], ALU.subtract))
                dve.tensor_copy(mparts[:, 2, :], mrest[:, :]).then_inc(m_sb, 1)

            def exp_normalise(k, par):
                g = 2 * k + par
                got = tail_ps[:, :].rearrange("p (i h w) -> p i h w", i=KT, w=VW)
                d3 = den[:, :].rearrange("p (i h) -> p i h", h=HQ)
                dve.wait_ge(e_turned, g + 1)
                dve.reciprocal(d3, got[:, :, :, D]).then_inc(e_chain, 1)
                dve.wait_ge(e_chain, g + 1)
                dve.tensor_tensor(y_of(k, par), got[:, :, :, 0:D],
                                  d3.unsqueeze(3).broadcast_to([P, KT, HQ, D]), ALU.mult).then_inc(e_normed, 1)

            for g in range(2):
                for n in range(len(MAX)):
                    row_max_of(g, g, n)
                parts_of_max(g, g)

            def max_quad(k, par, first=False):
                g = 2 * k + par
                for n in range(len(MAX)):
                    row_max_of(g + 2, par, n)
                parts_of_max(g + 2, par)
                if not first:
                    exp_normalise(*before(k, par))

            max_quad(0, 0, first=True)
            max_quad(0, 1)
            with dve.Fori(1, NQ // 2 - 1) as j:
                max_quad(j, 0)
                max_quad(j, 1)
            for g in range(NQ - 3, NQ):
                exp_normalise(g // 2, g % 2)
            residual(1)
            dve.wait_ge(z_sb, 2 * CH)
            layer_norm(2)

            dve.wait_ge(f_logits, 1)
            got1 = banks[0][:, 0:NT * E1].rearrange("p (i e) -> p i e", e=E1)
            link(dve.tensor_reduce(rowF[:, 0, :], got1, AX.X, ALU.max))
            dve.tensor_tensor(GG[:, :, :], got1, rowF[:, 0, :].unsqueeze(2).broadcast_to([P, NT, E1]),
                              ALU.subtract).then_inc(f_max, 1)
            dve.wait_ge(f_exp, 1)
            link(dve.tensor_reduce(rowF[:, 1, :], GG[:, :, :], AX.X, ALU.add))
            link(dve.reciprocal(rowF[:, 2, :], rowF[:, 1, :]))
            link(dve.tensor_tensor(GG[:, :, :], GG[:, :, :], rowF[:, 2, :].unsqueeze(2).broadcast_to([P, NT, E1]), ALU.mult))
            dve.wait_ge(masks0, 6)
            for i0 in range(0, NT, 4):
                mine = GG[:, i0:i0 + 4, :].unsqueeze(3).broadcast_to([P, 4, E1, E1])
                other = GG[:, i0:i0 + 4, :].unsqueeze(2).broadcast_to([P, 4, E1, E1])
                dve.tensor_tensor(cmp_a[:, i0:i0 + 4, :, :], other, mine, ALU.is_gt)
                link(dve.tensor_tensor(cmp_b[:, i0:i0 + 4, :, :], other, mine, ALU.is_equal))
            low = lower[:, :, :].unsqueeze(1).broadcast_to([P, NT, E1, E1])
            link(dve.tensor_tensor(cmp_b[:, :, :, :], cmp_b[:, :, :, :], low, ALU.mult))
            link(dve.tensor_tensor(cmp_a[:, :, :, :], cmp_a[:, :, :, :], cmp_b[:, :, :, :], ALU.add))
            link(dve.tensor_reduce(rankF[:, :, :], cmp_a[:, :, :, :], AX.X, ALU.add))
            link(dve.scalar_tensor_tensor(GW[:, :, :], rankF[:, :, :], TOP - 0.5, GG[:, :, :], ALU.is_lt, ALU.mult))
            link(dve.tensor_reduce(rowF[:, 0, :], GW[:, :, :], AX.X, ALU.add))
            link(dve.reciprocal(rowF[:, 1, :], rowF[:, 0, :]))
            link(dve.tensor_tensor(WT[:, :, :], GW[:, :, :].rearrange("p i e -> p e i"),
                                   rowF[:, 1, :].unsqueeze(1).broadcast_to([P, E1, NT]), ALU.mult))
            link(dve.tensor_copy(Z[:, :, :], X[:, :, :]))
            dve.nop().then_inc(f_max, 1)
            KF = F1 // P

            def hidden1(e, n, first):
                for m in range(KF):
                    c = KF * n + m
                    dve.wait_ge(f_act, CH * KF * e + c + 1)
                    if m == 0 and not (first and n < 2):
                        dve.wait_ge(f_y, CH * e + n - 1)
                    dve.tensor_tensor(hid_f[:, n % 2, m, :], act_f[:, c % 2, :], banks[2 * (c % 2) + 1],
                                      ALU.mult).then_inc(f_hid, 1)

            def add_up(e, n, first):
                dve.wait_ge(f_y, CH * e + n + 1)
                if not first:
                    dve.wait_ge(f_acc, CH * e + n - 3)
                for i in range(CT):
                    t = n * CT + i
                    w = WT[:, 0, t:t + 1] if isinstance(e, int) else WT[:, bass.ds(e, 1), t:t + 1].rearrange("p o t -> p (o t)")
                    ins = dve.scalar_tensor_tensor(Z[:, t, :], banks[4 + n % 2][:, i * P:(i + 1) * P], w, Z[:, t, :],
                                                   ALU.mult, ALU.add)
                ins.then_inc(f_acc, 1)

            def expert1(e, first):
                hidden1(e, 0, first)
                for n in range(CH):
                    if n + 1 < CH:
                        hidden1(e, n + 1, first)
                    add_up(e, n, first)

            expert1(0, True)
            with dve.Fori(1, E1) as e:
                expert1(e, False)
            dve.wait_ge(f_acc, CH * E1)
            layer_norm(3)

        @block.gpsimd
        def _(pool):
            pool.wait_ge(consts, 1)
            pool.affine_select(out=ident[:, :], in_=ident[:, :], compare_op=ALU.is_equal, fill=0.0, base=0,
                               pattern=[[-1, P]], channel_multiplier=1).then_inc(consts, 1)
            pool.memset(upto[:, :], 1.0).then_inc(upto_ready, 1)
            pool.wait_ge(upto_ready, 1)
            pool.affine_select(out=upto[:, :], in_=upto[:, :], compare_op=ALU.is_ge, fill=0.0, base=0,
                               pattern=[[1, P]], channel_multiplier=-1).then_inc(upto_ready, 1)

            pool.memset(VS[:, :, :, :], 0.0).then_inc(upto_ready, 1)
            pool.wait_ge(upto_ready, 3)
            pool.memset(VS[:, :, :, :].rearrange("p a i (h w) -> p (a i h) w", w=VW)[:, :, D:D + 1], 1.0
                        ).then_inc(upto_ready, 1)

            def take_v(k, par):
                heads = slice(HQ * D * k, HQ * D * (k + 1)) if isinstance(k, int) else bass.ds(k * (HQ * D), HQ * D)
                pool.tensor_copy(VS[:, par, :, :].rearrange("p i (h w) -> p i h w", w=VW)[:, :, :, 0:D],
                                 Y[:, par, :, heads].rearrange("p i (h d) -> p i h d", d=D)).then_inc(v_ready, 1)

            def quad(g, par, after=None):
                for s in range(NS):
                    if s == 3 and after is not None:
                        at_least(pool, step_summed, NS * g)
                        take_v(after, 1 - par)
                    rp, width = (par + s) % 2, pieces(s)[1]
                    for h0, h1 in ((0, 2), (2, POOL_HEADS[s])):
                        if h0 < h1:
                            pool.wait_ge(mask_done, 2 * NS * g + 2 * s + h0 // 2 + 1)
                            ins = pool.tensor_tensor(R4[:, rp, h0:h1, 0:width], R4[:, rp, h0:h1, 0:width],
                                                     R4[:, rp, h0:h1, 0:width], ALU.mult)
                    ins.then_inc(fourth_pool, 1)

            pool.wait_ge(x_in, 16)
            pool.wait_ge(w_in, 16 * 6)
            pool.tensor_tensor(X[:, :, :], X[:, :, :], YT[:, 0, 0:P].unsqueeze(1).broadcast_to([P, NT, P]),
                               ALU.add).then_inc(res_in, 1)
            pool.wait_ge(upto_ready, 4)
            pool.wait_ge(v_sb, 1)
            take_v(0, 0)
            pool.wait_ge(v_sb, B)
            quad(0, 0, after=0)
            quad(1, 1, after=1)
            with pool.Fori(1, NQ // 2 - 1) as j:
                quad(2 * j, 0, after=j)
                quad(2 * j + 1, 1, after=j + 1)
            quad(NQ - 2, 0, after=NQ // 2 - 1)
            quad(NQ - 1, 1)

            pool.wait_ge(normed, NQ)

            def link(n, ins):
                ins.then_inc(pool_chain, 1)
                pool.wait_ge(pool_chain, n)
            pool.iota(iota_i[:, :], pattern=[[0, P // E0], [1, E0]], base=0, channel_multiplier=0)
            link(1, pool.memset(same_e[:, :], 0.0))
            for o in range(-(P // E0) + 1, P // E0):
                link(o + 8 + 1, pool.affine_select(out=same_e[:, :], in_=same_e[:, :], compare_op=ALU.not_equal, fill=1.0,
                                                   base=o * E0, pattern=[[-1, P]], channel_multiplier=1))
            link(17, pool.memset(own_e[:, :, :], 1.0))
            pool.affine_select(out=before_e[:, :], in_=same_e[:, :], compare_op=ALU.is_gt, fill=0.0, base=0,
                               pattern=[[1, P]], channel_multiplier=-1).then_inc(masks0, 1)
            link(18, pool.memset(rank_a[:, 0:P], 1.0))
            pool.affine_select(out=before_t[:, :], in_=rank_a[:, 0:P], compare_op=ALU.is_gt, fill=0.0, base=0,
                               pattern=[[1, P]], channel_multiplier=-1).then_inc(masks0, 1)
            link(19, pool.affine_select(out=own_e[:, :, :], in_=own_e[:, :, :], compare_op=ALU.is_ge, fill=0.0, base=0,
                                        pattern=[[-16, 8], [0, 16]], channel_multiplier=1))
            link(20, pool.affine_select(out=own_e[:, :, :], in_=own_e[:, :, :], compare_op=ALU.is_ge, fill=0.0, base=15,
                                        pattern=[[16, 8], [0, 16]], channel_multiplier=-1))
            link(21, pool.tensor_copy(is_e[:, :], own_e[:, :, 0]))
            link(22, pool.memset(own_hi[:, :, :], 0.0))
            for e in range(8):
                link(23 + e, pool.affine_select(out=own_hi[:, :, :], in_=own_hi[:, :, :], compare_op=ALU.not_equal,
                                                fill=1.0, base=-16 * e, pattern=[[-1, 16], [0, 8]],
                                                channel_multiplier=1))
            link(31, pool.tensor_copy(iota16[:, :], iota_i[:, 0:16]))
            link(32, pool.iota(iota_i[:, 0:NT], pattern=[[P, NT]], base=0, channel_multiplier=1))
            pool.tensor_copy(token[:, :], iota_i[:, 0:NT]).then_inc(masks0, 1)
            pool.wait_ge(masks0, 3)
            pool.nop().then_inc(masks0, 1)

            def carry_waits():
                pool.tensor_tensor(carrier[:, :], eps_ln[:, :], eps_ln[:, :], ALU.add)

            def gather(e, k):
                src = idx[:, e, :] if isinstance(e, int) else idx[:, bass.ds(e, 1), :].rearrange("p o h -> p (o h)")
                pool.tensor_copy(idx_in[:, k, :], src).then_inc(idx_ready, 1)
                return 1

            def fetch(k):
                for h in range(NH):
                    pool.indirect_dma_start(out=G[:, k, h, :], out_offset=None, in_=xs_rows,
                                            in_offset=bass.IndirectOffsetOnAxis(ap=idx_in[:, k, h:h + 1].bitcast(U32), axis=0)
                                            ).then_inc(gathered[k], 16)

            def scatter(j, k):
                e = 4 * j + k
                src = idx[:, e, :] if isinstance(e, int) else idx[:, bass.ds(e, 1), :].rearrange("p o h -> p (o h)")
                pool.tensor_copy(idx_out[:, k, :], src).then_inc(idx_ready, 1)
                pool.wait_ge(idx_ready, 4 + (8 * j if not isinstance(j, int) or j < 3 else 24) + scat_at(j, k))
                pool.wait_ge(out_sb, e + 1)
                if not (isinstance(e, int) and e == 0):
                    pool.wait_ge(scattered, 16 * NH * e)
                carry_waits()
                for h in range(NH):
                    pool.indirect_dma_start(out=moe_rows, in_=out_e[:, k % 2, h, :], in_offset=None,
                                            out_offset=bass.IndirectOffsetOnAxis(ap=idx_out[:, k, h:h + 1].bitcast(U32), axis=0),
                                            compute_op=ALU.add).then_inc(scattered, 16)

            ORDER = [("g", 0), ("g", 1), ("s", 0), ("g", 2), ("s", 1), ("g", 3), ("s", 2), ("s", 3)]

            def scat_at(j, k):
                order = ORDER if not isinstance(j, int) or j < 3 else [o for o in ORDER if o[0] == "s"]
                return order.index(("s", k)) + 1

            pool.wait_ge(idx_sb, 1)
            pool.wait_ge(xs_out, 16 * 2)
            for k in range(4):
                gather(k, k)
            pool.wait_ge(idx_ready, 4)
            for k in range(4):
                fetch(k)
            pool.wait_ge(sh_out, 16 * CH)

            def four_experts(j):
                for n, (kind, k) in enumerate(ORDER):
                    if kind == "g":
                        pool.wait_ge(g_sb, 4 * j + k + 1)
                        gather(4 * j + 4 + k, k)
                        pool.wait_ge(idx_ready, 4 + 8 * j + n + 1)
                        carry_waits()
                        fetch(k)
                    else:
                        scatter(j, k)

            four_experts(0)
            with pool.Fori(1, E0 // 4 - 1) as j:
                four_experts(j)
            for k in range(4):
                scatter(E0 // 4 - 1, k)

            pool.wait_ge(w2_in, 16 * 6)
            pool.tensor_copy(identb[:, :], ident[:, :])
            link(33, pool.memset(mask_f[:, :], 0.0))
            pool.affine_select(out=mask[:, :], in_=mask_f[:, :], compare_op=ALU.is_ge, fill=NEG, base=0,
                               pattern=[[1, P]], channel_multiplier=-1).then_inc(masks0, 1)
            for par in range(2):
                pool.wait_ge(v_sb, B + par + 1)
                take_v(0, par)
            with pool.Fori(0, NQ // 2 - 1) as j:
                for par in range(2):
                    pool.wait_ge(exp_summed, NS * (2 * j + par + 1))
                    take_v(j + 1, par)
            pool.wait_ge(e_normed, NQ)
            link(34, pool.memset(lower[:, :, :], 1.0))
            pool.affine_select(out=lower[:, :, :], in_=lower[:, :, :], compare_op=ALU.is_gt, fill=0.0, base=0,
                               pattern=[[1, E1], [-1, E1]], channel_multiplier=0).then_inc(masks0, 1)


_INS = {
    "x": ("L0_attn_x", lambda a: a.reshape(B * T, P)),
    "xT": ("L0_attn_x", lambda a: a.reshape(B * T, P).T),
    "w_attn": ("L0_attn_W_attn", lambda a: a),
    "b_attn": ("L0_attn_b_attn", lambda a: a),
    "b_cols": ("L0_attn_b_attn", lambda a: a.reshape(3, P).T),
    "w_proj": ("L0_attn_W_proj", lambda a: a),
    "b_proj": ("L0_attn_b_proj", lambda a: a),
    "gain": ("L0_attn_score_gain", lambda a: a.reshape(1)),
    "gate_t": ("L0_ffn_gate_w", lambda a: a.T),
    "wg_t": ("L0_ffn_Wg", lambda a: a.transpose(0, 2, 1)),
    "wu_t": ("L0_ffn_Wu", lambda a: a.transpose(0, 2, 1)),
    "wd_t": ("L0_ffn_Wd", lambda a: a.transpose(0, 2, 1)),
    "sg_t": ("L0_ffn_Sg", lambda a: a.T),
    "su_t": ("L0_ffn_Su", lambda a: a.T),
    "sd_t": ("L0_ffn_Sd", lambda a: a.T),
    "w_dq": ("L1_attn_W_dq", lambda a: a),
    "w_uq": ("L1_attn_W_uq", lambda a: a),
    "w_dkv": ("L1_attn_W_dkv", lambda a: a),
    "w_uk": ("L1_attn_W_uk", lambda a: a),
    "w_uv": ("L1_attn_W_uv", lambda a: a),
    "w_o": ("L1_attn_W_o", lambda a: a),
    "gate1": ("L1_ffn_Wg", lambda a: a),
    "w1": ("L1_ffn_W1", lambda a: a),
    "w3": ("L1_ffn_W3", lambda a: a),
    "w2": ("L1_ffn_W2", lambda a: a),
}


def kernel(**inputs):
    import numpy as _np
    import concourse.bacc as _bacc
    from concourse.bass_utils import run_bass_kernel_spmd as _run

    nc = _bacc.Bacc("TRN2", target_bir_lowering=False, num_devices=1)
    arrays, aps = {}, {}
    for name, (source, lay) in _INS.items():
        arr = _np.ascontiguousarray(lay(_np.asarray(inputs[source])))
        arrays[f"in_{name}"] = arr
        aps[name] = nc.dram_tensor(f"in_{name}", arr.shape, mybir.dt.from_np(arr.dtype), kind="ExternalInput").ap()
    out = nc.dram_tensor("out_x", (B * T, P), F32, kind="ExternalOutput").ap()
    build(nc, aps, out)
    r = _run(nc, [arrays], core_ids=[0])
    return r.results[0]["out_x"].reshape(B, T, P)
```

```python
from contextlib import ExitStack

import concourse.bass as bass
from concourse import mybir

F32 = mybir.dt.float32
BF16 = mybir.dt.bfloat16
F16 = mybir.dt.float16
I32 = mybir.dt.int32
U32 = mybir.dt.uint32
ALU = mybir.AluOpType
ACT = mybir.ActivationFunctionType
AX = mybir.AxisListType

P = 128
B = 2
T = 1024
NT = B * T // P
KT = T // P
H = 16
D = P // H
HQ = 4
NQ = B * H // HQ
BANK = 512
REP = 3
ROWS = REP * REP * D
VW = 32
EPS_LN = 1e-5

STEPS = [(0,)] + [(kt, KT - kt) for kt in range(1, KT // 2)] + [(KT // 2,)]
NS = len(STEPS)
POOL_HEADS = [3, 2, 3, 2, 2]


def pieces(s):
    out, at = [], 0
    for kt in STEPS[s]:
        out.append((kt, at, T - kt * P))
        at += T - kt * P
    return out, at


def cut(lo, hi, edges):
    out, at = [], lo
    while at < hi:
        nxt = min(hi, ((at - edges) // BANK + 1) * BANK + edges)
        out.append((at, nxt))
        at = nxt
    return out


def score_cuts(s):
    return [(kt, a, b, kt * P + a - at) for kt, at, n in pieces(s)[0] for a, b in cut(at, at + n, 0)]


def value_cuts(s):
    return [(kt, at + qa - kt * P, qa, qb) for kt, at, n in pieces(s)[0] for qa, qb in cut(kt * P, T, 0)]


def spread(main, extra):
    out, done = [], 0
    for n, item in enumerate(main):
        out.append(item)
        upto = len(extra) * (n + 1) // len(main)
        out += extra[done:upto]
        done = upto
    return out + extra[done:]


TAIL = [(i, hh) for i in range(KT - 1) for hh in range(HQ)]
TAIL_AT = [len(TAIL) * s // NS for s in range(NS + 1)]


def step_jobs(s):
    return spread([("c", hh) for hh in range(HQ)], [("u", n) for n in range(TAIL_AT[s], TAIL_AT[s + 1])])


JOBS = [(s, kind, n) for s in range(NS) for kind, n in step_jobs(s)]
NJ = len(JOBS)
STEP_AT = [[job[0] for job in JOBS].index(s) for s in range(NS)] + [NJ]
RELU_AT = {(s, n): j for j, (s, kind, n) in enumerate(JOBS) if kind == "c"}
NORM_AT = 2
TAIL_JOB = [j for j in range(NJ) if JOBS[j][1] == "u"]
TURN_AT, HELD, EVAC_AT = STEP_AT[2] + (2 - STEP_AT[2]) % 3, 6, STEP_AT[1] + 4
SLOT = [n % 3 if n < TURN_AT else (n - TURN_AT) % 2 if n < TURN_AT + HELD else (n - TURN_AT - HELD + 2) % 3
        for n in range(NJ)]
PREV = [max(m for m in range(-NJ, n) if SLOT[m % NJ] == SLOT[n]) for n in range(NJ)]


E0 = 16
I0 = 4 * P
CAP = 2 * B * T // E0
NH = CAP // P
IS = 2 * P
EB = P // E0
XW = P + E0
E1 = 8
TOP = 2
F1 = 2 * P
DC = 32
MROWS = ROWS + REP
NEG = -1e30
CH = B * T // BANK
CT = BANK // P
STACK_DMAS = REP + 1
SCORE_BITS = 30
ROUNDS = SCORE_BITS // 2

MAX_JOBS = [((0, CT * 2, 2), [(0, 0, P), (4, BANK, P)]), ((1, CT * 2, 2), [(1, 0, 2 * P), (5, BANK, 2 * P)]),
            ((2, 1, 1), [(2, 0, 3 * P)]), ((10, 1, 1), [(6, BANK, 3 * P)]), ((3, 1, 1), [(3, 0, BANK)]),
            ((4, 1, 1), [(4, 0, BANK)]), ((5, 1, 1), [(5, 0, BANK)]), ((6, 1, 1), [(6, 0, BANK)]),
            ((7, 1, 1), [(7, 0, BANK)]), ((11, 1, 1), [(7, BANK, BANK)])]
MAX = [(hh, n) for hh in range(HQ) for n in range(len(MAX_JOBS))]
MAX_AT = [0, 0, 11, 23, 35, len(MAX)]

FIRST_TURN = 8


def build(nc, a, out):
    with ExitStack() as whole:
        def sem(name):
            return whole.enter_context(nc.semaphore(name))

        def dram(name, shape, dt):
            return nc.dram_tensor(name, shape, dt, kind="Internal").ap()

        def sb(name, shape, dt, scope=whole):
            return scope.enter_context(nc.sbuf_tensor(name, shape, dt))

        q_parts = dram("q_parts", [NQ, REP, D, HQ, T], BF16)
        k_parts = dram("k_parts", [NQ, REP, D, HQ, T], BF16)

        xs_rows = dram("xs_rows", [B * T, XW], F32)
        moe_rows = dram("moe_rows", [B * T, P], F32)
        m_rows = dram("m_rows", [NQ, REP, HQ * T], BF16)

        causal_ps = [whole.enter_context(nc.psum_tensor(f"causal_ps{i}", [P, T], F32)) for i in range(2)]
        tail_ps = whole.enter_context(nc.psum_tensor("tail_ps", [P, T], F32))
        acc_ps = whole.enter_context(nc.psum_tensor("acc_ps", [P, T], F32))

        slots = [*causal_ps, tail_ps]
        banks = [t[:, h * BANK:(h + 1) * BANK] for t in (causal_ps[0], causal_ps[1], tail_ps, acc_ps)
                 for h in range(2)]

        X = sb("X", [P, NT, P], F32)
        XT = sb("XT", [P, NT * P], F32)
        Y = sb("Y", [P, B, KT, P], F32)
        ident = sb("ident", [P, P], F32)
        Z = sb("Z", [P, NT, P], F32)
        stats = sb("stats", [P, NT, 6], F32)
        mean_var = sb("mean_var", [P, NT, 2], F32)
        spread_sb = sb("spread_sb", [P, 2, NT], F32)
        eps_ln = sb("eps_ln", [P, 1], F32)
        w_proj = sb("w_proj", [P, P], F32)
        YT = sb("YT", [P, 2, BANK], F32)
        pt = sb("pt", [P, 2, REP, T], BF16)
        VS = sb("VS", [P, 2, KT, HQ * VW], F32)

        A = ExitStack()
        w_attn = sb("w_attn", [P, 3 * P], F32, A)
        b_cols = sb("b_cols", [P, 2], F32, A)
        b_v = sb("b_v", [P, P], F32, A)
        gain = sb("gain", [P, 1], F32, A)
        gain_sign = sb("gain_sign", [P, 1], F32, A)
        gain_inv = sb("gain_inv", [P, 1], F32, A)
        gain_tmp = sb("gain_tmp", [P, 1], F32, A)
        k_sum = sb("k_sum", [P, 1], F32, A)
        k_mean = sb("k_mean", [P, 1], F32, A)
        upto = sb("upto", [P, P], F32, A)
        sum_sel = sb("sum_sel", [P, VW], F32, A)
        QS = sb("QS", [P, 2, HQ, T], BF16, A)
        KS = sb("KS", [P, 2, HQ, T], BF16, A)
        R1 = sb("R1", [P, 2, HQ, T], F32, A)
        R4 = sb("R4", [P, 2, HQ, T], F32, A)
        tails = sb("tails", [P, 2, KT, HQ], F32, A)
        junk = sb("junk", [P, 3, T], BF16, A)
        Ysb = sb("Ysb", [P, T], F32, A)
        nrm = sb("nrm", [P, 6, KT * HQ], F32, A)
        proj = R1[:, :, :, :].rearrange("p a h t -> p (a h t)").rearrange("p (m t) -> p m t", t=T)

        xT_in = [sem(f"xT_in{b}") for b in range(B)]
        x_in = sem("x_in")
        w_in = sem("w_in")
        consts = sem("consts")
        dve_chain = sem("dve_chain")
        pool_chain = sem("pool_chain")
        proj_full = sem("proj_full")
        part_done = sem("part_done")
        rest_done = sem("rest_done")
        part_out = [[sem(f"part_out{m}{n}") for n in range(REP)] for m in range(2)]
        v_full = sem("v_full")
        v_sb = sem("v_sb")
        v_ready = sem("v_ready")
        stack_in = [sem(f"stack_in{i}") for i in range(2)]
        filled = sem("filled")
        drained = sem("drained")
        square_done = sem("square_done")
        mask_done = sem("mask_done")
        fourth_pool = sem("fourth_pool")
        fourth_dve = sem("fourth_dve")
        step_summed = sem("step_summed")
        relu_summed = sem("relu_summed")
        acc_out = sem("acc_out")
        turned = sem("turned")
        normed = sem("normed")
        finish = sem("finish")
        first_full = sem("first_full")
        first_max = sem("first_max")
        hot_hi_ready = sem("hot_hi_ready")
        hot_lo_ready = sem("hot_lo_ready")
        upto_ready = sem("upto_ready")

        A.close()

        M = ExitStack()
        gate_t = sb("gate_t", [P, E0], F32, M)
        sg_t = sb("sg_t", [P, IS], F32, M)
        su_t = sb("su_t", [P, IS], F32, M)
        sd_t = sb("sd_t", [P, IS // P, P], F32, M)
        act_s = sb("act_s", [P, 2, BANK], F32, M)
        hid_s = sb("hid_s", [P, IS // P, BANK], F32, M)
        S = sb("S", [P, NT, E0], F32, M)
        row1 = sb("row1", [P, NT], F32, M)
        row2 = sb("row2", [P, NT], F32, M)
        row3 = sb("row3", [P, NT], F32, M)
        SC = sb("SC", [P, 2, P], F32, M)
        thr = sb("thr", [P, 1], I32, M)
        two_bits = sb("two_bits", [P, 4], I32, M)
        cand = sb("cand", [P, 4], I32, M)
        reached = sb("reached", [P, 4], F32, M)
        over = sb("over", [P, 6 * P], BF16, M)
        count = sb("count", [P, 4], F32, M)
        tile_counts = sb("tile_counts", [P, 2, 2], F32, M)
        same_e = sb("same_e", [P, P], F32, M)
        before_e = sb("before_e", [P, P], F32, M)
        before_t = sb("before_t", [P, P], BF16, M)
        thr_t = sb("thr_t", [P, E0], F32, M)
        above = sb("above", [P, NT, E0], BF16, M)
        equal = sb("equal", [P, NT, E0], BF16, M)
        rank_a = sb("rank_a", [P, NT * E0], F32, M)
        rank_b = sb("rank_b", [P, NT * E0], F32, M)
        slot = sb("slot", [P, NT * E0], I32, M)
        slot_hi = sb("slot_hi", [P, NT * E0], I32, M)
        slot_lo = sb("slot_lo", [P, NT * E0], I32, M)
        hi_f = sb("hi_f", [P, NT * E0], F16, M)
        lo_f = sb("lo_f", [P, NT * E0], F16, M)
        iota16 = sb("iota16", [P, 16], F16, M)
        iota_i = sb("iota_i", [P, P], I32, M)
        token = sb("token", [P, NT], F32, M)
        hot_hi = sb("hot_hi", [P, NT, E0 * 16], F16, M)
        hot_lo = sb("hot_lo", [P, NT, E0 * 16], F16, M)
        own_e = sb("own_e", [P, 8, 16], F32, M)
        own_hi = sb("own_hi", [P, 16, 8], F32, M)
        is_e = sb("is_e", [P, 8], F32, M)
        picked = sb("picked", [P, 2, 8, 16], F32, M)
        lists = sb("lists", [P, 2, 16], F32, M)
        turned_l = sb("turned_l", [P, 2, 2, 16, 8], F32, M)
        idx = sb("idx", [P, E0, NH], I32, M)
        carrier = sb("carrier", [P, 1], F32, M)
        idx_in = sb("idx_in", [P, 4, NH], I32, M)
        idx_out = sb("idx_out", [P, 4, NH], I32, M)
        G = sb("G", [P, 4, NH, XW], F32, M)
        w_tok = sb("w_tok", [P, 4, NH], F32, M)
        GT = sb("GT", [P, 2, CAP], F32, M)
        wg = sb("wg", [P, 4, I0], F32, M)
        wu = sb("wu", [P, 4, I0], F32, M)
        wd = sb("wd", [P, 4, I0], F32, M)
        act_e = sb("act_e", [P, 4, CAP], F32, M)
        hid_e = sb("hid_e", [P, 2, 4, CAP], F32, M)
        out_e = sb("out_e", [P, 2, NH, P], F32, M)
        M.close()

        N = ExitStack()
        w_down = sb("w_down", [P, 2 * DC], F32, N)
        w_up = sb("w_up", [2 * DC, 2, P], F32, N)
        latent = sb("latent", [2 * DC, B * T], F32, N)
        QM = sb("QM", [P, 2, HQ, T], BF16, N)
        KM = sb("KM", [P, 2, HQ, T], BF16, N)
        QE = sb("QE", [P, 2, HQ, T], BF16, N)
        KE = sb("KE", [P, 2, HQ, T], BF16, N)
        EX = sb("EX", [P, 2, HQ, T], F32, N)
        Esb = sb("Esb", [P, T], F32, N)
        projE = EX[:, :, :, :].rearrange("p a h t -> p (a h t)").rearrange("p (m t) -> p m t", t=T)
        mx = sb("mx", [P, 2, HQ, 12], F32, N)
        mxt = sb("mxt", [P, HQ, KT], F32, N)
        mparts = sb("mparts", [HQ * KT, REP, P], BF16, N)
        mrest = sb("mrest", [HQ * KT, P], F32, N)
        mask = sb("mask", [P, P], BF16, N)
        identb = sb("identb", [P, P], BF16, N)
        mask_f = sb("mask_f", [P, P], F32, N)
        den = sb("den", [P, KT * HQ], F32, N)
        N.close()

        F = ExitStack()
        gate1 = sb("gate1", [P, E1], F32, F)
        GG = sb("GG", [P, NT, E1], F32, F)
        rowF = sb("rowF", [P, 3, NT], F32, F)
        cmp_a = sb("cmp_a", [P, NT, E1, E1], F32, F)
        cmp_b = sb("cmp_b", [P, NT, E1, E1], F32, F)
        lower = sb("lower", [P, E1, E1], F32, F)
        rankF = sb("rankF", [P, NT, E1], F32, F)
        GW = sb("GW", [P, NT, E1], F32, F)
        WT = sb("WT", [P, E1, NT], F32, F)
        w1 = sb("w1", [P, 2, F1], F32, F)
        w3 = sb("w3", [P, 2, F1], F32, F)
        w2 = sb("w2", [P, 2, F1 // P, P], F32, F)
        act_f = sb("act_f", [P, 3, BANK], F32, F)
        hid_f = sb("hid_f", [P, 2, F1 // P, BANK], F32, F)
        F.close()

        ln_var = sem("ln_var")
        ln_std = sem("ln_std")
        ln_rec = sem("ln_rec")
        ln_stat = sem("ln_stat")
        ln_x = sem("ln_x")
        res_in = sem("res_in")
        yt_full = sem("yt_full")
        yt_sb = sem("yt_sb")
        out_full = sem("out_full")
        z_sb = sem("z_sb")
        xt_full = sem("xt_full")
        xt_sb = sem("xt_sb")
        moe_w_in = sem("moe_w_in")
        sh_up = sem("sh_up")
        sh_act = sem("sh_act")
        sh_hid = sem("sh_hid")
        sh_down = sem("sh_down")
        sh_sum = sem("sh_sum")
        sh_out = sem("sh_out")
        logits = sem("logits")
        row_max = sem("row_max")
        exps = sem("exps")
        probs = sem("probs")
        xs_out = sem("xs_out")
        sc_full = sem("sc_full")
        counted = sem("counted")
        totalled = sem("totalled")
        search = sem("search")
        found = sem("found")
        thr_full = sem("thr_full")
        marked = sem("marked")
        ranked = sem("ranked")
        token_hot = sem("token_hot")
        listed = sem("listed")
        list_sb = sem("list_sb")
        idx_full = sem("idx_full")
        idx_sb = sem("idx_sb")
        masks_ready = sem("masks_ready")
        gathered = [sem(f"gathered{k}") for k in range(4)]
        weights = [sem(f"weights{k}") for k in range(4)]
        g_turned = sem("g_turned")
        g_sb = sem("g_sb")
        up_full = sem("up_full")
        gelu_done = sem("gelu_done")
        hid_done = sem("hid_done")
        down_full = sem("down_full")
        out_sb = sem("out_sb")
        idx_ready = sem("idx_ready")
        scattered = sem("scattered")
        z_in = [sem(f"z_in{n}") for n in range(CH)]
        w2_in = sem("w2_in")
        lat_full = sem("lat_full")
        lat_sb = sem("lat_sb")
        max_in = [sem(f"max_in{i}") for i in range(2)]
        exp_in = [sem(f"exp_in{i}") for i in range(2)]
        ones_set = sem("ones_set")
        max_full = sem("max_full")
        max_done = sem("max_done")
        mx_ready = sem("mx_ready")
        mx_full = sem("mx_full")
        m_sb = sem("m_sb")
        m_chain = sem("m_chain")
        m_out = sem("m_out")
        exp_full = sem("exp_full")
        exp_done = sem("exp_done")
        exp_summed = sem("exp_summed")
        e_out = sem("e_out")
        e_turned = sem("e_turned")
        e_normed = sem("e_normed")
        e_chain = sem("e_chain")
        f_gate_in = sem("f_gate_in")
        f_logits = sem("f_logits")
        f_max = sem("f_max")
        f_exp = sem("f_exp")
        f_win = [sem(f"f_win{i}") for i in range(2)]
        f_up = sem("f_up")
        f_act = sem("f_act")
        f_hid = sem("f_hid")
        f_y = sem("f_y")
        f_acc = sem("f_acc")
        block = whole.enter_context(nc.Block())

        def at_least(eng, s, value):
            if not isinstance(value, int) or value > 0:
                eng.wait_ge(s, value)

        def maxima(par, n, scores, reduce, op, **how):
            hh, c = MAX[n]
            (o0, step, cnt), groups = MAX_JOBS[c]
            w = groups[0][2]
            return reduce(mx[:, par, hh, o0:o0 + step * (cnt - 1) + 1:step],
                          scores[:, 0:cnt * w].rearrange("p (c w) -> p c w", w=w), AX.X, op, **how)

        @block.sync
        def _(sp):
            sp.dma_start(w_attn[:, 0:2 * P], a["w_qk"]).then_inc(w_in, 16)
            sp.dma_start(w_attn[:, 2 * P:3 * P], a["w_v"]).then_inc(w_in, 16)
            sp.dma_start(XT[:, 0:T], a["xT"][:, 0:T]).then_inc(xT_in[0], 16)
            sp.dma_start(b_cols[:, :], a["b_cols"]).then_inc(w_in, 16)
            sp.dma_start(b_v[:, :], a["b_attn"][2 * P:3 * P].unsqueeze(0).broadcast_to([P, P])).then_inc(w_in, 16)
            sp.dma_start(w_proj[:, :], a["w_proj"]).then_inc(w_in, 16)
            sp.dma_start(YT[:, 0, 0:P], a["b_proj"].unsqueeze(0).broadcast_to([P, P])).then_inc(w_in, 16)
            sp.dma_start(gain[:, :], a["gain"].broadcast_to([P, 1])).then_inc(w_in, 16)
            sp.dma_start(XT[:, T:2 * T], a["xT"][:, T:2 * T]).then_inc(xT_in[1], 16)
            sp.dma_start(X[:, :, :], a["x"].rearrange("(i p) c -> p i c", p=P)).then_inc(x_in, 16)

            def store_parts(layer, b):
                for n in range(REP):
                    for m, parts in enumerate((q_parts, k_parts)):
                        sp.wait_ge(part_done, 2 * REP * (B * layer + b) + 2 * n + m + 1)
                        quads = slice(b * (NQ // B), (b + 1) * (NQ // B))
                        sp.dma_start(parts[quads, n].rearrange("k d h t -> k (d h) t"), pt[:, m, n, :]
                                     ).then_inc(part_out[m][n], 16)

            def parts_stored(layer, b):
                for m in range(2):
                    for n in range(REP):
                        sp.wait_ge(part_out[m][n], 16 * (B * layer + b + 1))

            def load_stack(q_stack, k_stack, g, done):
                q, k = [quad_of(parts, g).rearrange("r d h t -> r d (h t)") for parts in (q_parts, k_parts)]
                for m in range(REP):
                    sp.dma_start(q_stack[m * REP * D:(m + 1) * REP * D, :, :].rearrange("p h t -> p (h t)"),
                                 q[m].unsqueeze(0).broadcast_to([REP, D, HQ * T])).then_inc(done, 16)
                sp.dma_start(k_stack[0:ROWS, :, :].rearrange("p h t -> p (h t)"),
                             k.rearrange("r d x -> (r d) x").unsqueeze(0).broadcast_to([REP, REP * D, HQ * T])
                             ).then_inc(done, 16)

            def quad_of(dram_ap, g):
                if isinstance(g, int):
                    return dram_ap[g]
                if len(dram_ap.shape) == 3:
                    return dram_ap[bass.ds(g, 1), :, :].rearrange("o a b -> (o a) b")
                return dram_ap[bass.ds(g, 1), :, :, :, :].rearrange("o r d h t -> (o r) d h t")

            def load_quad(k, par):
                g = par * (NQ // B) + k
                load_stack(QS[:, par, :, :], KS[:, par, :, :], g, stack_in[par])

            for b in range(B):
                store_parts(0, b)
                parts_stored(0, b)
                load_quad(0, b)
            with sp.Fori(0, NQ // 2 - 1) as j:
                sp.wait_ge(step_summed, (2 * j + 1) * NS)
                load_quad(j + 1, 0)
                sp.wait_ge(step_summed, (2 * j + 2) * NS)
                load_quad(j + 1, 1)

            sp.wait_ge(normed, NQ)
            for dst, src in ((gate_t[:, :], a["gate_t"]), (sg_t[:, :], a["sg_t"]), (su_t[:, :], a["su_t"]),
                             (sd_t[:, :, :], a["sd_t"].rearrange("(k p) d -> p k d", p=P))):
                sp.dma_start(dst, src).then_inc(moe_w_in, 16)

            def load_expert(e, k):
                for dst, name in ((wg, "wg_t"), (wu, "wu_t")):
                    sp.dma_start(dst[:, k, :], one_of(a[name], e)).then_inc(weights[k], 16)
                sp.dma_start(wd[:, k, :].rearrange("p (m d) -> p m d", d=P),
                             one_of(a["wd_t"], e).rearrange("(m p) d -> p m d", p=P)).then_inc(weights[k], 16)

            def one_of(ap, e):
                return ap[e] if isinstance(e, int) else ap[bass.ds(e, 1), :, :].rearrange("o a b -> (o a) b")

            for k in range(4):
                load_expert(k, k)
            for n in range(CH):
                sp.wait_ge(sh_sum, n + 1)
                sp.dma_start(moe_rows[n * BANK:(n + 1) * BANK, :].rearrange("(i p) d -> p i d", p=P),
                             Z[:, n * CT:(n + 1) * CT, :]).then_inc(sh_out, 16)
            sp.wait_ge(probs, 1)
            xs = xs_rows.rearrange("(i p) w -> p i w", p=P)
            sp.dma_start(xs[:, :, 0:P], X[:, :, :]).then_inc(xs_out, 16)
            sp.dma_start(xs[:, :, P:XW], S[:, :, :]).then_inc(xs_out, 16)
            with sp.Fori(0, E0 // 4 - 1) as j:
                for k in range(4):
                    sp.wait_ge(down_full, 4 * j + k + 1)
                    load_expert(4 * j + 4 + k, k)
            sp.wait_ge(scattered, 16 * NH * E0)
            for n in range(CH):
                sp.dma_start(Z[:, n * CT:(n + 1) * CT, :],
                             moe_rows[n * BANK:(n + 1) * BANK, :].rearrange("(i p) d -> p i d", p=P)).then_inc(z_in[n], 16)

            for dst, src in ((w_down[:, 0:DC], a["w_dq"]), (w_down[:, DC:2 * DC], a["w_dkv"]),
                             (w_up[0:DC, 0, :], a["w_uq"]), (w_up[DC:2 * DC, 0, :], a["w_uk"]),
                             (w_up[DC:2 * DC, 1, :], a["w_uv"]), (w_proj[:, :], a["w_o"])):
                sp.dma_start(dst, src).then_inc(w2_in, 16)
            def load_max(k, par):
                g = par * (NQ // B) + k
                load_stack(QM[:, par, :, :], KM[:, par, :, :], g, max_in[par])

            def store_max(g):
                sp.wait_ge(m_sb, g + 1)
                sp.dma_start(quad_of(m_rows, g).rearrange("r (h t) -> h r t", t=P), mparts[:, :, :]).then_inc(m_out, 16)

            def load_exp(k, par):
                sp.wait_ge(m_out, 16 * (2 * k + par + 1))
                g = par * (NQ // B) + k
                load_stack(QE[:, par, :, :], KE[:, par, :, :], g, exp_in[par])
                sp.dma_start(QE[ROWS:MROWS, par, :, :].rearrange("r h t -> r (h t)"), quad_of(m_rows, 2 * k + par)
                             ).then_inc(exp_in[par], 16)

            for b in range(B):
                store_parts(1, b)
                parts_stored(1, b)
                load_max(0, b)
            sp.wait_ge(ones_set, 1)
            for par in range(2):
                sp.wait_ge(first_full, len(MAX) * (par + 1))
                load_max(1, par)
                store_max(par)
                load_exp(0, par)
            with sp.Fori(0, NQ // 2 - 2) as j:
                for par in range(2):
                    sp.wait_ge(max_full, len(MAX) * (2 * j + 1 + par))
                    load_max(j + 2, par)
                    store_max(2 * j + 2 + par)
                    sp.wait_ge(exp_summed, NS * (2 * j + 1 + par))
                    load_exp(j + 1, par)
            for par in range(2):
                store_max(NQ - 2 + par)
                sp.wait_ge(exp_summed, NS * (NQ - 3 + par))
                load_exp(NQ // 2 - 1, par)

            sp.wait_ge(e_normed, NQ)
            sp.dma_start(gate1[:, :], a["gate1"]).then_inc(f_gate_in, 16)

            def load_ffn(e, k):
                for dst, name in ((w1, "w1"), (w3, "w3")):
                    sp.dma_start(dst[:, k, :], one_of(a[name], e)).then_inc(f_win[k], 16)
                sp.dma_start(w2[:, k, :, :], one_of(a["w2"], e).rearrange("(m p) d -> p m d", p=P)
                             ).then_inc(f_win[k], 16)

            load_ffn(0, 0)
            load_ffn(1, 1)
            with sp.Fori(0, E1 // 2 - 1) as j:
                for k in range(2):
                    sp.wait_ge(f_y, CH * (2 * j + k + 1))
                    load_ffn(2 * j + 2 + k, k)
            for n in range(CH):
                sp.wait_ge(ln_x, 3 * CH + n + 1)
                sp.dma_start(out[n * BANK:(n + 1) * BANK, :].rearrange("(i p) d -> p i d", p=P),
                             X[:, n * CT:(n + 1) * CT, :]).then_inc(finish, 16)
            sp.wait_ge(finish, 16 * CH)

        @block.tensor
        def _(pe):
            pe.wait_ge(w_in, 16 * 7)
            for m in range(2 * B):
                b = m // 2
                pe.wait_ge(xT_in[b], 16)
                if m > 1:
                    pe.wait_ge(rest_done, m - 1)
                for n in range(T // BANK):
                    mm = pe.matmul(causal_ps[m % 2][:, n * BANK:(n + 1) * BANK],
                                   w_attn[:, (m % 2) * P:(m % 2 + 1) * P],
                                   XT[:, b * T + n * BANK:b * T + (n + 1) * BANK], start=True, stop=True)
                mm.then_inc(proj_full, 1)
                if m % 2:
                    at_least(pe, v_sb, b)
                    for i in range(KT):
                        mm = pe.matmul(tail_ps[:, i * P:(i + 1) * P], XT[:, b * T + i * P:b * T + (i + 1) * P],
                                       w_attn[:, 2 * P:3 * P], start=True, stop=True)
                    mm.then_inc(v_full, 1)
            pe.wait_ge(rest_done, 2 * REP * (B - 1) + 2)
            pe.wait_ge(v_sb, B)
            pe.wait_ge(consts, 2)

            def fill(g, par, j):
                s, kind, n = JOBS[j]
                at_least(pe, drained, NJ * g + PREV[j] + 1)
                if j == TURN_AT + HELD:
                    at_least(pe, normed, g)
                (causal if kind == "c" else tail)(slots[SLOT[j]], par, s, n).then_inc(filled, 1)

            def causal(slot, par, s, hh):
                for kt, c0, c1, q0 in score_cuts(s):
                    mm = pe.matmul(slot[:, c0:c1], KS[0:ROWS, par, hh, kt * P:(kt + 1) * P],
                                   QS[0:ROWS, par, hh, q0:q0 + c1 - c0], start=True, stop=True)
                return mm

            def tail(slot, par, s, n):
                i, hh = TAIL[n]
                w = T - (i + 1) * P
                for c0, c1 in cut(0, w, 0):
                    mm = pe.matmul(slot[:, c0:c1], QS[0:ROWS, par, hh, i * P:(i + 1) * P],
                                   KS[0:ROWS, par, hh, (i + 1) * P + c0:(i + 1) * P + c1], start=True, stop=True)
                return mm

            def sums(g, par, s, powered):
                rp, cuts = (par + s) % 2, value_cuts(s)

                def group(k):
                    kt, c0, qa, qb = cuts[k]
                    if k == 0 and powered:
                        pe.wait_ge(fourth_pool, NS * g + s + 1)
                        pe.wait_ge(fourth_dve, NS * g + s + 1)
                        if s == 0:
                            pe.wait_ge(v_ready, g + 1)
                    if k == 0 and not powered:
                        pe.wait_ge(drained, NJ * g + RELU_AT[s, HQ - 1] + 1)
                        if s == 0:
                            at_least(pe, acc_out, g)
                    for hh in range(HQ):
                        src, w = (R4, VS[:, par, kt, hh * VW:(hh + 1) * VW]) if powered else (R1, sum_sel[:, :])
                        last = powered and kt == STEPS[-2 if qb <= BANK else -1][0]
                        mm = pe.matmul(acc_ps[hh * VW:(hh + 1) * VW, qa:qb], w,
                                       src[:, rp, hh, c0:c0 + qb - qa],
                                       start=(kt == 0 and not powered), stop=last, tile_position=(0, hh * VW))
                    if k == len(cuts) - 1:
                        mm.then_inc(step_summed if powered else relu_summed, 1)
                return [lambda k=k: group(k) for k in range(len(cuts))]

            def turn(g, last=False):
                pe.wait_ge(acc_out, g + 1)
                pe.wait_ge(drained, NJ * (g + 1) + (PREV[TURN_AT + HELD] + 1 if not last else 0))
                for i in range(KT):
                    mm = pe.transpose(tail_ps[:, i * P:(i + 1) * P], Ysb[:, i * P:(i + 1) * P], ident[:, :])
                mm.then_inc(turned, 1)

            def quad(g, k, par, first=False):
                pe.wait_ge(stack_in[par], 16 * STACK_DMAS * (k + 1))
                for s in range(NS):
                    early = [] if first and s < 2 else (
                        sums(g, par, s - 2, True) if s >= 2 else sums(g - 1, 1 - par, NS - 2 + s, True))
                    late = [] if s == 1 or (first and s == 0) else (
                        sums(g, par, s - 1, False) if s else sums(g - 1, 1 - par, NS - 1, False))
                    if s == 1:
                        late = sums(g, par, 0, False)
                    jobs = []
                    for j in range(STEP_AT[s], STEP_AT[s + 1]):
                        if j == TURN_AT and not first:
                            jobs.append(lambda: turn(g - 1))
                        jobs.append(lambda j=j: fill(g, par, j))
                    at = EVAC_AT - STEP_AT[s] + 2 if s == 1 else 4
                    for job in jobs[:2] + spread(jobs[2:4], early) + jobs[4:at] + spread(jobs[max(at, 4):], late):
                        job()

            quad(0, 0, 0, first=True)
            with pe.Fori(0, NQ // 2 - 1) as j:
                quad(2 * j + 1, j, 1)
                quad(2 * j + 2, j + 1, 0)
            quad(NQ - 1, NQ // 2 - 1, 1)
            for job in (sums(NQ - 1, 1, NS - 1, False) + sums(NQ - 1, 1, NS - 2, True)
                        + sums(NQ - 1, 1, NS - 1, True)):
                job()
            turn(NQ - 1, last=True)

            def project(layer):
                pe.wait_ge(e_normed if layer else normed, NQ)
                for n in range(CH + 1):
                    if n < CH:
                        at_least(pe, yt_sb, CH * layer + n - 1)
                        for i in range(CT):
                            t = n * CT + i
                            mm = pe.transpose(banks[n % 2][:, i * P:(i + 1) * P],
                                              Y[:, t // KT, t % KT, :],
                                              ident[:, :])
                        mm.then_inc(yt_full, 1)
                    if n:
                        pe.wait_ge(yt_sb, CH * layer + n)
                        at_least(pe, z_sb, CH * layer + n - 2 if n > 2 else 0)
                        for i in range(CT):
                            mm = pe.matmul(banks[2 + (n - 1) % 2][:, i * P:(i + 1) * P],
                                           YT[:, (n - 1) % 2, i * P:(i + 1) * P], w_proj[:, :], start=True, stop=True)
                        mm.then_inc(out_full, 1)

            def turn_x(layer, use):
                for n in range(CH + 1):
                    if n < CH:
                        pe.wait_ge(ln_x, CH * layer + n + 1)
                        for i in range(CT):
                            mm = pe.transpose(banks[4 + n][:, i * P:(i + 1) * P], X[:, n * CT + i, :], ident[:, :])
                        mm.then_inc(xt_full, 1)
                    if n > 0:
                        pe.wait_ge(xt_sb, CH * layer + n)
                        use(n - 1)

            def route(n, gate, experts, done):
                for i in range(n * CT, (n + 1) * CT):
                    mm = pe.matmul(banks[0][:, i * experts:(i + 1) * experts], XT[:, i * P:(i + 1) * P], gate[:, :],
                                   start=True, stop=True)
                mm.then_inc(done, 1)

            project(0)
            pe.wait_ge(moe_w_in, 16 * 4)
            turn_x(0, lambda n: route(n, gate_t, E0, logits))

            pe.wait_ge(probs, 1)
            for h in range(2):
                mm = pe.transpose(banks[7][:, h * P:(h + 1) * P], S[:, 8 * h:8 * (h + 1), :], ident[:, :])
            mm.then_inc(sc_full, 1)
            pe.wait_ge(masks_ready, 3)

            def total(r):
                pe.wait_ge(counted, r + 1)
                pe.matmul(banks[0][:, 0:4], same_e[:, :], count[:, :], start=True, stop=True).then_inc(totalled, 1)

            with pe.Fori(0, CH) as n:
                for k in range(IS // P):
                    total(3 * n + k)
                    for w, o in ((sg_t, 1), (su_t, 2)):
                        mm = pe.matmul(banks[o + 2 * k], w[:, k * P:(k + 1) * P], XT[:, bass.ds(n * BANK, BANK)],
                                       start=True, stop=True)
                    mm.then_inc(sh_up, 1)
                total(3 * n + 2)
                pe.wait_ge(sh_hid, (n + 1) * (IS // P))
                for i in range(CT):
                    for k in range(IS // P):
                        mm = pe.matmul(banks[5][:, i * P:(i + 1) * P], hid_s[:, k, i * P:(i + 1) * P],
                                       sd_t[:, k, :], start=(k == 0), stop=(k == IS // P - 1))
                mm.then_inc(sh_down, 1)
            with pe.Fori(3 * CH, ROUNDS) as r:
                total(r)
            pe.wait_ge(found, 1)
            pe.transpose(banks[1][:, 0:P], thr[:, 0:1].bitcast(F32).broadcast_to([P, P]), ident[:, :]
                         ).then_inc(thr_full, 1)
            pe.wait_ge(marked, 2)
            for c, flag in ((0, above), (1, equal)):
                pe.matmul(banks[2][:, c * 2 * P:(c + 1) * 2 * P], before_t[:, :],
                          flag[:, :, :].rearrange("p i e -> p (i e)"), start=True, stop=False, skip_group_check=True)
                for h in range(2):
                    more = [(tile_counts[:, c, h:h + 1], before_e)]
                    if h:
                        more.append((tile_counts[:, c, 0:1], same_e))
                    if c:
                        more += [(tile_counts[:, 0, 0:1], same_e), (tile_counts[:, 0, 1:2], same_e)]
                    for n, (cnt, w) in enumerate(more):
                        mm = pe.matmul(banks[2][:, c * 2 * P + h * P:c * 2 * P + (h + 1) * P],
                                       cnt.broadcast_to([P, P]), w[:, :], start=False,
                                       stop=(h == 1 and n == len(more) - 1), skip_group_check=True)
            mm.then_inc(ranked, 1)
            for i in range(NT):
                pe.wait_ge(token_hot, i + 1)
                if i % (NT // 2) == 0:
                    pe.wait_ge(hot_lo_ready, i // (NT // 2) + 1)
                for q in range(2):
                    mm = pe.matmul(banks[3 + q][:, 0:P], hot_hi[:, i, q * P:(q + 1) * P], hot_lo[:, i, q * P:(q + 1) * P],
                                   start=(i == 0), stop=(i == NT - 1))
            mm.then_inc(listed, 1)
            pe.wait_ge(list_sb, 1)
            for q in range(2):
                for h in range(NH):
                    mm = pe.matmul(banks[5][:, (q * NH + h) * 8:(q * NH + h + 1) * 8],
                                   turned_l[:, q, h, :, :].rearrange("p a b -> p (a b)"), is_e[:, :],
                                   start=True, stop=True)
            mm.then_inc(idx_full, 1)
            pe.wait_ge(idx_sb, 1)

            def turn_tokens(j, k):
                pe.wait_ge(gathered[k], 16 * NH * (j + 1))
                if k >= 2:
                    at_least(pe, g_sb, 4 * j + k - 1)
                elif not isinstance(j, int) or j > 0:
                    pe.wait_ge(g_sb, 4 * j + k - 1)
                for h in range(NH):
                    mm = pe.transpose(banks[k % 2][:, h * P:(h + 1) * P], G[:, k, h, 0:P], ident[:, :])
                mm.then_inc(g_turned, 1)

            def expert_up(j, k):
                pe.wait_ge(weights[k], 16 * 3 * (j + 1))
                pe.wait_ge(g_sb, 4 * j + k + 1)
                for m in range(I0 // P):
                    if isinstance(j, int) and j == 0:
                        at_least(pe, hid_done, 4 * k + m - 3)
                    else:
                        pe.wait_ge(hid_done, 16 * j + 4 * k + m - 3)
                    for w, c in ((wg, 0), (wu, 1)):
                        mm = pe.matmul(banks[2 + m][:, c * CAP:(c + 1) * CAP], w[:, k, m * P:(m + 1) * P],
                                       GT[:, k % 2, :], start=True, stop=True)
                    mm.then_inc(up_full, 1)

            def expert_down(j, k):
                pe.wait_ge(hid_done, 16 * j + 4 * k + 4)
                if k >= 2 or not isinstance(j, int) or j > 0:
                    pe.wait_ge(out_sb, 4 * j + k - 1)
                for h in range(NH):
                    for m in range(I0 // P):
                        mm = pe.matmul(banks[6 + k % 2][:, h * P:(h + 1) * P], hid_e[:, k % 2, m, h * P:(h + 1) * P],
                                       wd[:, k, m * P:(m + 1) * P], start=(m == 0), stop=(m == I0 // P - 1))
                mm.then_inc(down_full, 1)

            def four_experts(j, first=False, last=False):
                for k in range(4):
                    expert_up(j, k)
                    if k < 3:
                        turn_tokens(j, k + 1)
                    elif not last:
                        turn_tokens(j + 1, 0)
                    if k > 0:
                        expert_down(j, k - 1)
                    elif not first:
                        expert_down(j - 1, 3)

            turn_tokens(0, 0)
            four_experts(0, first=True)
            with pe.Fori(1, E0 // 4 - 1) as j:
                four_experts(j)
            four_experts(E0 // 4 - 1, last=True)
            expert_down(E0 // 4 - 1, 3)

            pe.wait_ge(w2_in, 16 * 6)
            turn_x(1, lambda n: pe.matmul(banks[n][0:2 * DC, :], w_down[:, :], XT[:, n * BANK:(n + 1) * BANK],
                                          start=True, stop=True).then_inc(lat_full, 1))
            pe.wait_ge(lat_sb, CH)
            for m in range(2 * B):
                b, r0 = m // 2, DC * (m % 2)
                if m > 1:
                    pe.wait_ge(rest_done, 2 * REP * B + m - 1)
                for n in range(T // BANK):
                    mm = pe.matmul(causal_ps[m % 2][:, n * BANK:(n + 1) * BANK], w_up[r0:r0 + DC, 0, :],
                                   latent[r0:r0 + DC, b * T + n * BANK:b * T + (n + 1) * BANK], start=True, stop=True)
                mm.then_inc(proj_full, 1)
                if m % 2:
                    at_least(pe, v_sb, B + b if b else 0)
                    for i in range(KT):
                        mm = pe.matmul(tail_ps[:, i * P:(i + 1) * P], latent[DC:2 * DC, b * T + i * P:b * T + (i + 1) * P],
                                       w_up[DC:2 * DC, 1, :], start=True, stop=True)
                    mm.then_inc(v_full, 1)
            pe.wait_ge(rest_done, 2 * REP * B + 2 * (REP - 1) * (B - 1) + 2)
            pe.wait_ge(v_sb, 2 * B)

            def row_scores(slot, par, n):
                hh, c = MAX[n]
                at = 0
                for i, k0, w in MAX_JOBS[c][1]:
                    diag = k0 + w == (i + 1) * P
                    mm = pe.matmul(slot[:, at:at + w], QM[0:ROWS, par, hh, i * P:(i + 1) * P],
                                   KM[0:ROWS, par, hh, k0:k0 + w], start=True, stop=not diag, skip_group_check=True)
                    if diag:
                        mm = pe.matmul(slot[:, at + w - P:at + w], mask[:, :], identb[:, :],
                                       start=False, stop=True, skip_group_check=True)
                    at += w
                return mm

            def max_job(g, par, n):
                at_least(pe, max_done, len(MAX) * (g - 2) + n - 1)
                if n < 2:
                    at_least(pe, m_sb, g)
                    at_least(pe, e_normed, g - 2)
                row_scores(tail_ps[:, n % 2 * BANK:(n % 2 + 1) * BANK], par, n).then_inc(max_full, 1)

            def first_job(g, i):
                i += len(MAX) * g
                at_least(pe, first_max, i - 5)
                row_scores(banks[i % 6], g, i % len(MAX)).then_inc(first_full, 1)
                if i == len(MAX) + FIRST_TURN - 1:
                    turn_max(0, acc_ps)

            def turn_max(g, slot=tail_ps):
                pe.wait_ge(mx_ready, g + 1)
                pe.transpose(slot[0:HQ * KT, 0:P], mxt[:, :, :], ident[:, :]).then_inc(mx_full, 1)

            def exp_scores(g, par, s, hh):
                cuts = score_cuts(s)

                def one(n):
                    kt, c0, c1, q0 = cuts[n]
                    if n == 0:
                        at_least(pe, exp_done, HQ * NS * g + HQ * s + hh - 1)
                    mm = pe.matmul(causal_ps[hh % 2][:, c0:c1], KE[0:MROWS, par, hh, kt * P:(kt + 1) * P],
                                   QE[0:MROWS, par, hh, q0:q0 + c1 - c0], start=True, stop=q0 != kt * P,
                                   skip_group_check=True)
                    if q0 == kt * P:
                        mm = pe.matmul(causal_ps[hh % 2][:, c0:c0 + P], identb[:, :], mask[:, :],
                                       start=False, stop=True, skip_group_check=True)
                    if n == len(cuts) - 1:
                        mm.then_inc(exp_full, 1)
                return [(c1 - c0, lambda n=n: one(n)) for n, (_, c0, c1, _) in enumerate(cuts)]

            def exp_sums(g, par, s):
                rp, cuts = (par + s) % 2, value_cuts(s)

                def group(k):
                    kt, c0, qa, qb = cuts[k]
                    if k == 0:
                        pe.wait_ge(exp_done, HQ * NS * g + HQ * (s + 1))
                        if s == 0:
                            at_least(pe, e_out, g)
                            pe.wait_ge(v_ready, NQ + g + 1)
                    for hh in range(HQ):
                        mm = pe.matmul(acc_ps[hh * VW:(hh + 1) * VW, qa:qb], VS[:, par, kt, hh * VW:(hh + 1) * VW],
                                       EX[:, rp, hh, c0:c0 + qb - qa], start=(kt == 0),
                                       stop=(kt == STEPS[-2 if qb <= BANK else -1][0]), tile_position=(0, hh * VW))
                    if k == len(cuts) - 1:
                        mm.then_inc(exp_summed, 1)
                return [(2 * (qb - qa), lambda k=k: group(k)) for k, (_, _, qa, qb) in enumerate(cuts)]

            def turn_exp(g):
                pe.wait_ge(e_out, g + 1)
                for i in range(KT):
                    mm = pe.transpose(tail_ps[:, i * P:(i + 1) * P], Esb[:, i * P:(i + 1) * P], ident[:, :])
                mm.then_inc(e_turned, 1)

            def run_all(jobs):
                for _, job in jobs:
                    job()

            def among(jobs, extra):
                out, done, passed, total = [], 0, 0, sum(w for w, _ in jobs)
                for w, job in jobs:
                    while done < len(extra) and passed + w / 2 >= total * (done + 0.5) / len(extra):
                        out.append(extra[done])
                        done += 1
                    out.append((w, job))
                    passed += w
                return out + extra[done:]

            def max_part(g, par, s):
                return [(0, lambda n=n: max_job(g, par, n)) for n in range(MAX_AT[s], MAX_AT[s + 1])]

            pe.wait_ge(masks_ready, 5)
            for g in range(2):
                pe.wait_ge(max_in[g], 16 * STACK_DMAS)
                for i in range(len(MAX)):
                    first_job(g, i)
            pe.wait_ge(first_max, 2 * len(MAX))

            def exp_quad(g, k, par, with_max, first=False, turn_maxima=True):
                pe.wait_ge(exp_in[par], 16 * (STACK_DMAS + 1) * (k + 1))
                if with_max:
                    pe.wait_ge(max_in[par], 16 * STACK_DMAS * (k + 2))
                for hh in range(2):
                    run_all(exp_scores(g, par, 0, hh))
                if first:
                    turn_max(1, acc_ps)
                    pe.wait_ge(m_sb, 2)
                else:
                    if turn_maxima:
                        turn_max(g + 1)
                    run_all(exp_sums(g - 1, 1 - par, NS - 1))
                run_all(exp_scores(g, par, 0, 2))
                if not first:
                    pe.wait_ge(m_sb, g + 2 if turn_maxima else NQ)
                    at_least(pe, e_normed, g - 1)
                    turn_exp(g - 1)
                run_all(exp_scores(g, par, 0, 3))
                for s in range(1, NS):
                    jobs = [cut for hh in range(HQ) for cut in exp_scores(g, par, s, hh)]
                    jobs = spread(jobs, exp_sums(g, par, s - 1))
                    run_all(among(jobs, max_part(g + 2, par, s)) if with_max else jobs)

            exp_quad(0, 0, 0, True, first=True)
            exp_quad(1, 0, 1, True)
            with pe.Fori(1, NQ // 2 - 1) as j:
                exp_quad(2 * j, j, 0, True)
                exp_quad(2 * j + 1, j, 1, True)
            exp_quad(NQ - 2, NQ // 2 - 1, 0, False)
            exp_quad(NQ - 1, NQ // 2 - 1, 1, False, turn_maxima=False)
            run_all(exp_sums(NQ - 1, 1, NS - 1))
            pe.wait_ge(e_normed, NQ - 1)
            turn_exp(NQ - 1)
            project(1)
            pe.wait_ge(f_gate_in, 16)
            turn_x(2, lambda n: route(n, gate1, E1, f_logits))

            pe.wait_ge(f_max, 1)

            KF = F1 // P

            def ffn_up(e, k, n, first):
                for m in range(KF):
                    c = CH * KF * e + KF * n + m
                    ring = (KF * n + m) % 2
                    if not (first and n == 0):
                        pe.wait_ge(f_hid, c - 1)
                    for w, o in ((w1, 0), (w3, 1)):
                        mm = pe.matmul(banks[2 * ring + o], w[:, k, m * P:(m + 1) * P],
                                       XT[:, n * BANK:(n + 1) * BANK], start=True, stop=True)
                    mm.then_inc(f_up, 1)

            def ffn_down(e, k, n, first):
                pe.wait_ge(f_hid, CH * KF * e + KF * (n + 1))
                if not (first and n < 2):
                    pe.wait_ge(f_acc, CH * e + n - 1)
                for i in range(CT):
                    for m in range(KF):
                        mm = pe.matmul(banks[4 + n % 2][:, i * P:(i + 1) * P], hid_f[:, n % 2, m, i * P:(i + 1) * P],
                                       w2[:, k, m, :], start=(m == 0), stop=(m == KF - 1))
                mm.then_inc(f_y, 1)

            def ffn_two(e, kk, first):
                for k in range(2):
                    pe.wait_ge(f_win[k], 16 * 3 * (kk + 1))
                    first_k = first and k == 0
                    ffn_up(e + k, k, 0, first_k)
                    for n in range(CH):
                        if n + 1 < CH:
                            ffn_up(e + k, k, n + 1, False)
                        ffn_down(e + k, k, n, first_k)

            ffn_two(0, 0, True)
            with pe.Fori(1, E1 // 2) as j:
                ffn_two(2 * j, j, False)

        @block.scalar
        def _(act):
            def rests(layer, b, n, m):
                return 2 * REP * b + 2 * n + m + 1 if layer == 0 else 2 * REP * B + 2 * (REP - 1) * b + 2 * (n - 1) + m + 1

            def cut_parts(layer, values):
                for b in range(B):
                    for n in range(REP):
                        for m in range(2):
                            if layer and n == 0:
                                act.wait_ge(proj_full, 2 * (B + b) + m + 1)
                            else:
                                act.wait_ge(rest_done, rests(layer, b, n, m))
                            at_least(act, part_out[m][n], 16 * (B * layer + b))
                            src = causal_ps[m][:, :] if layer and n == 0 else values[:, 2 * b + m, :]
                            act.activation(pt[:, m, n, :], src, ACT.Copy).then_inc(part_done, 1)

            cut_parts(0, proj)

            def drain(g, par, j):
                s, kind, n = JOBS[j]
                if j == 0:
                    at_least(act, normed, g - 1)
                if (kind, n) == ("c", 0):
                    at_least(act, relu_summed, NS * g + s - 1)
                    at_least(act, square_done, 2 * (NS * g + s - 1))
                if kind == "u":
                    at_least(act, drained, NJ * g + (TAIL_JOB[n - 3] + 1 if n >= 3 else 0))
                act.wait_ge(filled, NJ * g + j + 1)
                (keep if kind == "c" else add_up)(slots[SLOT[j]], par, s, n).then_inc(drained, 1)

            def keep(slot, par, s, hh):
                rp, width = (par + s) % 2, pieces(s)[1]
                return act.activation(R1[:, rp, hh, 0:width], slot[:, 0:width], ACT.Relu)

            def add_up(slot, par, s, n):
                i, hh = TAIL[n]
                return act.activation(junk[:, n % 3, 0:T - (i + 1) * P], slot[:, 0:T - (i + 1) * P], ACT.Relu,
                                      accum_out=tails[:, par, i, hh:hh + 1])

            def evacuate(g):
                act.wait_ge(step_summed, NS * (g + 1))
                at_least(act, turned, g)
                act.activation(Ysb[:, :], acc_ps[:, :], ACT.Copy).then_inc(acc_out, 1)

            def quad(g, par, first=False):
                for j in range(NJ):
                    if j == EVAC_AT and not first:
                        evacuate(g - 1)
                    drain(g, par, j)

            quad(0, 0, first=True)
            quad(1, 1)
            with act.Fori(1, NQ // 2) as j:
                quad(2 * j, 0)
                quad(2 * j + 1, 1)
            evacuate(NQ - 1)

            def project(layer):
                for n in range(CH):
                    act.wait_ge(yt_full, CH * layer + n + 1)
                    at_least(act, out_full, CH * layer + n - 1 if n > 1 else 0)
                    act.activation(YT[:, n % 2, :], banks[n % 2], ACT.Copy).then_inc(yt_sb, 1)

            def deviation(layer, n):
                act.wait_ge(ln_var, CH * layer + n + 1)
                act.activation(spread_sb[:, 0, n * CT:(n + 1) * CT], mean_var[:, n * CT:(n + 1) * CT, 1], ACT.Sqrt,
                               bias=eps_ln[:, 0:1]).then_inc(ln_std, 1)

            def copy_xt(layer, n):
                act.wait_ge(xt_full, CH * layer + n + 1)
                act.activation(XT[:, n * BANK:(n + 1) * BANK], banks[4 + n], ACT.Copy).then_inc(xt_sb, 1)

            def normed_xt(layer):
                for n in range(CH + 1):
                    if n < CH:
                        deviation(layer, n)
                    if n > 0:
                        copy_xt(layer, n - 1)

            project(0)
            normed_xt(0)

            act.wait_ge(row_max, 1)
            act.activation(S[:, :, :], S[:, :, :], ACT.Exp).then_inc(exps, 1)
            with act.Fori(0, CH) as n:
                for k in range(IS // P):
                    act.wait_ge(sh_up, n * (IS // P) + k + 1)
                    act.activation(act_s[:, k, :], banks[1 + 2 * k], ACT.Gelu).then_inc(sh_act, 1)

            act.wait_ge(masks_ready, 4)
            for i in range(NT):
                if i % (NT // 2) == 0:
                    act.wait_ge(hot_hi_ready, i // (NT // 2) + 1)
                act.activation(hot_hi[:, i, :], hot_hi[:, i, :], ACT.Copy, scale=token[:, i:i + 1]).then_inc(token_hot, 1)

            def gelu_expert(j, k):
                for m in range(I0 // P):
                    act.wait_ge(up_full, 16 * j + 4 * k + m + 1)
                    if k > 0 or not isinstance(j, int) or j > 0:
                        act.wait_ge(hid_done, 16 * j + 4 * k + m - 3)
                    act.activation(act_e[:, m, :], banks[2 + m][:, 0:CAP], ACT.Gelu).then_inc(gelu_done, 1)

            for k in range(4):
                gelu_expert(0, k)
            with act.Fori(1, E0 // 4) as j:
                for k in range(4):
                    gelu_expert(j, k)
            normed_xt(1)

            for n in range(CH):
                act.wait_ge(lat_full, n + 1)
                act.activation(latent[:, n * BANK:(n + 1) * BANK], banks[n][0:2 * DC, :], ACT.Copy).then_inc(lat_sb, 1)
            cut_parts(1, projE)

            def exps_of(g, par, s, hh):
                rp, width = (par + s) % 2, pieces(s)[1]
                act.wait_ge(exp_full, HQ * NS * g + HQ * s + hh + 1)
                if hh == 0:
                    at_least(act, exp_summed, NS * g + s - 1)
                act.activation(EX[:, rp, hh, 0:width], causal_ps[hh % 2][:, 0:width], ACT.Exp,
                               scale=float(D) ** -0.5).then_inc(exp_done, 1)

            def exp_evacuate(g):
                act.wait_ge(exp_summed, NS * (g + 1))
                at_least(act, e_turned, g)
                act.activation(Esb[:, :], acc_ps[:, :], ACT.Copy).then_inc(e_out, 1)

            def exp_quad(g, par, first=False):
                for s in range(NS):
                    for hh in range(HQ):
                        exps_of(g, par, s, hh)
                        if (s, hh) == (0, 1) and not first:
                            exp_evacuate(g - 1)

            exp_quad(0, 0, first=True)
            exp_quad(1, 1)
            with act.Fori(1, NQ // 2 - 1) as j:
                exp_quad(2 * j, 0)
                exp_quad(2 * j + 1, 1)
            exp_quad(NQ - 2, 0)
            exp_quad(NQ - 1, 1)
            exp_evacuate(NQ - 1)
            project(1)
            normed_xt(2)

            act.wait_ge(f_max, 1)
            act.activation(GG[:, :, :], GG[:, :, :], ACT.Exp).then_inc(f_exp, 1)
            KF = F1 // P

            def silus(e, first):
                for c in range(CH * KF):
                    act.wait_ge(f_up, CH * KF * e + c + 1)
                    if not (first and c < 2):
                        act.wait_ge(f_hid, CH * KF * e + c - 1)
                    act.activation(act_f[:, c % 2, :], banks[2 * (c % 2)], ACT.Silu).then_inc(f_act, 1)

            silus(0, True)
            with act.Fori(1, E1) as e:
                silus(e, False)
            for n in range(CH):
                deviation(3, n)

        @block.vector
        def _(dve):
            chained = [0]

            def link(ins):
                ins.then_inc(dve_chain, 1)
                chained[0] += 1
                dve.wait_ge(dve_chain, chained[0])

            dve.memset(eps_ln[:, :], EPS_LN)
            dve.memset(tails[:, :, :, :], 0.0)
            dve.memset(ident[:, :], 1.0)
            dve.memset(sum_sel[:, :], 0.0).then_inc(consts, 1)
            dve.wait_ge(consts, 1)
            dve.memset(sum_sel[:, D + 1:D + 2], 1.0)
            dve.wait_ge(w_in, 16 * 7)
            link(dve.tensor_scalar(gain_tmp[:, :], gain[:, :], 0.0, 2.0, ALU.is_ge, ALU.mult))
            dve.tensor_scalar(gain_sign[:, :], gain_tmp[:, :], -1.0, None, ALU.add)
            link(dve.reciprocal(gain_inv[:, :], gain[:, :]))

            def take_rests(layer, b, rests, values=None):
                for n in range(REP - 1):
                    for m in range(2):
                        rest = rests[:, 2 * b + m, :]
                        dve.wait_ge(part_done, 2 * REP * (B * layer + b) + 2 * n + m + 1)
                        dve.tensor_tensor(rest, values[m][:, :] if values and n == 0 else rest, pt[:, m, n, :],
                                          ALU.subtract).then_inc(rest_done, 1)

            for b in range(B):
                q, k = proj[:, 2 * b, :], proj[:, 2 * b + 1, :]
                dve.wait_ge(proj_full, 2 * b + 1)
                dve.tensor_scalar(q, causal_ps[0][:, :], b_cols[:, 0:1], gain_sign[:, :],
                                  ALU.add, ALU.mult).then_inc(rest_done, 1)
                dve.wait_ge(proj_full, 2 * b + 2)
                link(dve.tensor_scalar(k, causal_ps[1][:, :], b_cols[:, 1:2], 0.0, ALU.add, ALU.add,
                                       accum_out=k_sum[:, :]))
                link(dve.tensor_scalar(k_mean[:, :], k_sum[:, :], 1.0 / T, None, ALU.mult))
                dve.tensor_scalar(k, k, k_mean[:, :], None, ALU.subtract).then_inc(rest_done, 1)
                take_rests(0, b, proj)
                dve.wait_ge(v_full, b + 1)
                dve.tensor_tensor(Y[:, b, :, :], tail_ps[:, :].rearrange("p (i c) -> p i c", c=P),
                                  b_v[:, :].unsqueeze(1).broadcast_to([P, KT, P]), ALU.add).then_inc(v_sb, 1)
            dve.wait_ge(upto_ready, 2)

            def square(g, par, s):
                rp, width = (par + s) % 2, pieces(s)[1]
                at_least(dve, step_summed, NS * g + s - 1)
                for h0 in (0, 2):
                    dve.wait_ge(drained, NJ * g + RELU_AT[s, h0 + 1] + 1)
                    dve.tensor_tensor(R4[:, rp, h0:h0 + 2, 0:width], R1[:, rp, h0:h0 + 2, 0:width],
                                      R1[:, rp, h0:h0 + 2, 0:width], ALU.mult).then_inc(square_done, 1)
                    dve.wait_ge(square_done, 2 * NS * g + 2 * s + h0 // 2 + 1)
                    for kt, at, _ in pieces(s)[0]:
                        ins = dve.tensor_tensor(R4[:, rp, h0:h0 + 2, at:at + P], R4[:, rp, h0:h0 + 2, at:at + P],
                                                upto[:, :].unsqueeze(1).broadcast_to([P, 2, P]), ALU.mult)
                    ins.then_inc(mask_done, 1)

            def fourth(g, par, s):
                rp, width, h0 = (par + s) % 2, pieces(s)[1], POOL_HEADS[s]
                dve.wait_ge(mask_done, 2 * NS * g + 2 * s + 2)
                dve.tensor_tensor(R4[:, rp, h0:HQ, 0:width], R4[:, rp, h0:HQ, 0:width],
                                  R4[:, rp, h0:HQ, 0:width], ALU.mult).then_inc(fourth_dve, 1)

            def y_of(k, par):
                heads = slice(HQ * D * k, HQ * D * (k + 1)) if isinstance(k, int) else bass.ds(k * (HQ * D), HQ * D)
                return Y[:, par, :, heads].rearrange("p i (h d) -> p i h d", d=D)

            def before(k, par):
                return (k, 0) if par else (k - 1, 1)

            def normalise(k, par):
                got = tail_ps[:, :].rearrange("p (i h w) -> p i h w", i=KT, w=VW)
                g = 2 * k + par
                sums, z, z2, z4, den, w = [nrm[:, n, :].rearrange("p (i h) -> p i h", h=HQ) for n in range(6)]
                dve.wait_ge(turned, g + 1)

                def then(ins):
                    ins.then_inc(dve_chain, 1)
                    step[0] += 1
                    dve.wait_ge(dve_chain, base + per * g + step[0])
                base, per, step = chained[0], 7, [0]
                then(dve.tensor_tensor(sums, got[:, :, :, D + 1], tails[:, par, :, :], ALU.add))
                then(dve.tensor_scalar(z, sums, 2.0 / T, 1e-6, ALU.mult, ALU.add))
                then(dve.tensor_scalar(z, z, gain_inv[:, 0:1], None, ALU.mult))
                then(dve.tensor_tensor(z2, z, z, ALU.mult))
                then(dve.tensor_tensor(z4, z2, z2, ALU.mult))
                then(dve.scalar_tensor_tensor(den, z4, 1e-6, got[:, :, :, D], ALU.mult, ALU.add))
                then(dve.reciprocal(w, den))
                dve.tensor_tensor(y_of(k, par), got[:, :, :, 0:D],
                                  w.unsqueeze(3).broadcast_to([P, KT, HQ, D]), ALU.mult).then_inc(normed, 1)

            def quad(k, par, first=False):
                g = 2 * k + par
                for s in range(NS):
                    if s == NORM_AT and not first:
                        normalise(*before(k, par))
                    square(g, par, s)
                    fourth(g, par, s)

            quad(0, 0, first=True)
            with dve.Fori(0, NQ // 2 - 1) as j:
                quad(j, 1)
                quad(j + 1, 0)
            quad(NQ // 2 - 1, 1)
            normalise(NQ // 2 - 1, 1)
            chained[0] += 7 * NQ

            def residual(layer, n):
                dve.wait_ge(out_full, CH * layer + n + 1)
                dve.tensor_tensor(Z[:, n * CT:(n + 1) * CT, :], X[:, n * CT:(n + 1) * CT, :],
                                  banks[2 + n % 2].rearrange("p (i d) -> p i d", d=P), ALU.add).then_inc(z_sb, 1)
                dve.wait_ge(z_sb, CH * layer + n + 1)

            def moments(layer, n):
                for i in range(n * CT, (n + 1) * CT):
                    dve.bn_stats(stats[:, i, :], Z[:, i, :]).then_inc(ln_stat, 1)
                for i in range(n * CT, (n + 1) * CT):
                    dve.wait_ge(ln_stat, NT * layer + i + 1)
                    ins = dve.bn_aggr(mean_var[:, i, :], stats[:, i, :])
                ins.then_inc(ln_var, 1)

            def standardise(layer, n):
                dve.wait_ge(ln_std, CH * layer + n + 1)
                dve.reciprocal(spread_sb[:, 1, n * CT:(n + 1) * CT], spread_sb[:, 0, n * CT:(n + 1) * CT]).then_inc(ln_rec, 1)
                dve.wait_ge(ln_rec, CH * layer + n + 1)
                for i in range(n * CT, (n + 1) * CT):
                    ins = dve.tensor_scalar(X[:, i, :], Z[:, i, :], mean_var[:, i, 0:1], spread_sb[:, 1, i:i + 1],
                                            ALU.subtract, ALU.mult)
                ins.then_inc(ln_x, 1)

            def layer_norm(layer, ready):
                for n in range(CH + 1):
                    if n < CH:
                        ready(n)
                        moments(layer, n)
                    if n > 0:
                        standardise(layer, n - 1)

            dve.wait_ge(res_in, 1)
            layer_norm(0, lambda n: residual(0, n))

            dve.wait_ge(logits, CH)
            got = banks[0][:, 0:NT * E0].rearrange("p (i e) -> p i e", e=E0)
            link(dve.tensor_reduce(row1[:, :], got, AX.X, ALU.max))
            dve.tensor_tensor(S[:, :, :], got, row1[:, :].unsqueeze(2).broadcast_to([P, NT, E0]),
                              ALU.subtract).then_inc(row_max, 1)
            dve.wait_ge(exps, 1)
            link(dve.tensor_reduce(row2[:, :], S[:, :, :], AX.X, ALU.add))
            link(dve.reciprocal(row3[:, :], row2[:, :]))
            dve.tensor_tensor(S[:, :, :], S[:, :, :], row3[:, :].unsqueeze(2).broadcast_to([P, NT, E0]),
                              ALU.mult).then_inc(probs, 1)
            dve.wait_ge(sc_full, 1)
            link(dve.tensor_copy(SC[:, :, :].rearrange("p h t -> p (h t)"), banks[7][:, 0:2 * P]))
            for c in range(4):
                dve.memset(two_bits[:, c:c + 1], c << (SCORE_BITS - 2))
                dve.memset(cand[:, c:c + 1], c << (SCORE_BITS - 2))
            link(dve.memset(count[:, 0:1], float(CAP)))
            sc_all = SC[:, :, :].rearrange("p h t -> p (h t)")

            def search_round(r, between=None):
                for c in range(1, 4):
                    ins = dve.tensor_scalar(over[:, 2 * P * (c - 1):2 * P * c], sc_all, cand[:, c:c + 1].bitcast(F32), 0.0,
                                            ALU.is_ge, ALU.add, accum_out=count[:, c:c + 1])
                ins.then_inc(counted, 1)
                dve.tensor_scalar(two_bits[:, :], two_bits[:, :], 2, None, ALU.logical_shift_right).then_inc(search, 1)
                if between:
                    between()
                dve.wait_ge(totalled, r + 1)
                dve.scalar_tensor_tensor(reached[:, :], banks[0][:, 0:4], CAP - 0.5, cand[:, :].bitcast(F32),
                                         ALU.is_ge, ALU.mult).then_inc(search, 1)
                dve.wait_ge(search, 4 * r + 2)
                dve.tensor_reduce(thr[:, :].bitcast(F32), reached[:, :], AX.X, ALU.max).then_inc(search, 1)
                dve.wait_ge(search, 4 * r + 3)
                dve.tensor_tensor(cand[:, :], two_bits[:, :], thr[:, 0:1].broadcast_to([P, 4]),
                                  ALU.bitwise_or).then_inc(search, 1)
                dve.wait_ge(search, 4 * r + 4)

            def shared_hidden(n, k):
                dve.wait_ge(sh_act, n * (IS // P) + k + 1)
                dve.tensor_tensor(hid_s[:, k, :], act_s[:, k, :], banks[2 + 2 * k], ALU.mult).then_inc(sh_hid, 1)

            def shared_out(n):
                dve.wait_ge(sh_down, n + 1)
                dve.tensor_tensor(Z[:, bass.ds(n * CT, CT), :], X[:, bass.ds(n * CT, CT), :],
                                  banks[5].rearrange("p (i d) -> p i d", d=P), ALU.add).then_inc(sh_sum, 1)

            search_round(0)
            with dve.Fori(0, CH) as n:
                search_round(3 * n + 1, lambda: shared_hidden(n, 0))
                search_round(3 * n + 2, lambda: shared_hidden(n, 1))
                search_round(3 * n + 3, lambda: shared_out(n))
            with dve.Fori(3 * CH + 1, ROUNDS) as r:
                search_round(r)
            dve.nop().then_inc(found, 1)
            for c, op in ((0, ALU.is_gt), (1, ALU.is_equal)):
                for h in range(2):
                    dve.tensor_scalar(over[:, (2 * c + h) * P:(2 * c + h + 1) * P], SC[:, h, :], thr[:, 0:1].bitcast(F32), 0.0, op,
                                      ALU.add, accum_out=tile_counts[:, c, h:h + 1])
            dve.wait_ge(thr_full, 1)
            link(dve.tensor_copy(thr_t[:, :], banks[1][:, 0:E0]))
            for flag, op in ((above, ALU.is_gt), (equal, ALU.is_equal)):
                dve.tensor_tensor(flag[:, :, :], S[:, :, :], thr_t[:, :].unsqueeze(1).broadcast_to([P, NT, E0]), op
                                  ).then_inc(marked, 1)
            dve.wait_ge(ranked, 1)
            dve.wait_ge(marked, 2)
            big = float(2 * B * T)
            dve.scalar_tensor_tensor(rank_a[:, :], banks[2][:, 0:2 * P], -big,
                                     above[:, :, :].rearrange("p i e -> p (i e)"), ALU.add, ALU.mult)
            link(dve.scalar_tensor_tensor(rank_b[:, :], banks[2][:, 2 * P:4 * P], -big,
                                          equal[:, :, :].rearrange("p i e -> p (i e)"), ALU.add, ALU.mult))
            link(dve.scalar_tensor_tensor(slot[:, :], rank_a[:, :], big, rank_b[:, :], ALU.add, ALU.add))
            dve.tensor_scalar(slot_hi[:, :], slot[:, :], 4, None, ALU.logical_shift_right)
            link(dve.tensor_scalar(slot_lo[:, :], slot[:, :], 15, None, ALU.bitwise_and))
            dve.tensor_copy(lo_f[:, :], slot_lo[:, :])
            link(dve.tensor_copy(hi_f[:, :], slot_hi[:, :]))
            dve.wait_ge(masks_ready, 4)
            half = NT // 2 * E0
            for h in range(2):
                for hot_x, digit, ready in ((hot_hi, hi_f, hot_hi_ready), (hot_lo, lo_f, hot_lo_ready)):
                    dve.tensor_tensor(hot_x[:, :, :].rearrange("p i (e s) -> p (i e) s", s=16)[:, h * half:(h + 1) * half, :],
                                      digit[:, h * half:(h + 1) * half].unsqueeze(2).broadcast_to([P, half, 16]),
                                      iota16[:, :].unsqueeze(1).broadcast_to([P, half, 16]), ALU.is_equal
                                      ).then_inc(ready, 1)
            dve.wait_ge(listed, 1)
            for q in range(2):
                link(dve.tensor_tensor(picked[:, q, :, :], banks[3 + q][:, 0:P].rearrange("p (e b) -> p e b", b=16),
                                       own_e[:, :, :], ALU.mult))
                link(dve.tensor_reduce(lists[:, q, :], picked[:, q, :, :].rearrange("p e b -> p b e"), AX.X, ALU.add))
                for h in range(NH):
                    ins = dve.tensor_tensor(turned_l[:, q, h, :, :], own_hi[:, :, :],
                                            lists[:, q, h * 8:(h + 1) * 8].unsqueeze(1).broadcast_to([P, 16, 8]),
                                            ALU.mult)
            ins.then_inc(list_sb, 1)
            dve.wait_ge(idx_full, 1)
            dve.tensor_copy(idx[:, :, :].rearrange("p (q e) h -> p q h e", q=2),
                            banks[5][:, 0:2 * NH * 8].rearrange("p (q h e) -> p q h e", q=2, e=8)).then_inc(idx_sb, 1)

            def take_tokens(j, k):
                dve.wait_ge(g_turned, 4 * j + k + 1)
                if k >= 2 or not isinstance(j, int) or j > 0:
                    dve.wait_ge(up_full, 16 * j + 4 * (k - 1))
                col = P + 4 * j + k
                w_col = G[:, k, :, col:col + 1] if isinstance(j, int) else G[:, k, :, bass.ds(col, 1)]
                dve.tensor_copy(w_tok[:, k, :].unsqueeze(2), w_col)
                dve.tensor_copy(GT[:, k % 2, :], banks[k % 2][:, 0:CAP]).then_inc(g_sb, 1)

            def hidden(j, k):
                for m in range(I0 // P):
                    dve.wait_ge(gelu_done, 16 * j + 4 * k + m + 1)
                    if m == 0 and (k >= 2 or not isinstance(j, int) or j > 0):
                        dve.wait_ge(down_full, 4 * j + k - 1)
                    dve.tensor_tensor(hid_e[:, k % 2, m, :], act_e[:, m, :], banks[2 + m][:, CAP:2 * CAP],
                                      ALU.mult).then_inc(hid_done, 1)

            def weigh(j, k):
                dve.wait_ge(down_full, 4 * j + k + 1)
                if k >= 2 or not isinstance(j, int) or j > 0:
                    dve.wait_ge(scattered, 16 * NH * (4 * j + k - 1))
                for h in range(NH):
                    ins = dve.tensor_scalar(out_e[:, k % 2, h, :], banks[6 + k % 2][:, h * P:(h + 1) * P],
                                            w_tok[:, k, h:h + 1], None, ALU.mult)
                ins.then_inc(out_sb, 1)

            def four_experts(j, first=False, last=False):
                for k in range(4):
                    hidden(j, k)
                    if k < 3:
                        take_tokens(j, k + 1)
                    elif not last:
                        take_tokens(j + 1, 0)
                    if k > 0:
                        weigh(j, k - 1)
                    elif not first:
                        weigh(j - 1, 3)

            take_tokens(0, 0)
            four_experts(0, first=True)
            with dve.Fori(1, E0 // 4 - 1) as j:
                four_experts(j)
            four_experts(E0 // 4 - 1, last=True)
            weigh(E0 // 4 - 1, 3)
            layer_norm(1, lambda n: dve.wait_ge(z_in[n], 16))

            dve.wait_ge(w2_in, 16 * 6)
            for b in range(B):
                take_rests(1, b, projE, causal_ps)
                dve.wait_ge(v_full, B + b + 1)
                dve.tensor_copy(Y[:, b, :, :], tail_ps[:, :].rearrange("p (i c) -> p i c", c=P)).then_inc(v_sb, 1)

            def row_max_of(g, par, n):
                half = n % 2
                dve.wait_ge(max_full, len(MAX) * (g - 2) + n + 1)
                maxima(par, n, tail_ps[:, half * BANK:(half + 1) * BANK], dve.tensor_reduce, ALU.max, negate=True
                       ).then_inc(max_done, 1)

            def parts_of_max(g, par):
                if isinstance(g, int) and g < 2:
                    dve.wait_ge(first_max, len(MAX) * (g + 1))
                else:
                    dve.wait_ge(max_done, len(MAX) * (g - 1))
                at_least(dve, mx_full, g)
                dve.tensor_copy(mxt[:, :, 0:CT], mx[:, par, :, 0:CT])
                dve.tensor_tensor(mxt[:, :, CT:KT], mx[:, par, :, CT:KT], mx[:, par, :, KT:12], ALU.min
                                  ).then_inc(mx_ready, 1)
                dve.wait_ge(mx_full, g + 1)
                if not isinstance(g, int) or g > 0:
                    dve.wait_ge(m_out, 16 * g)
                src = (acc_ps if isinstance(g, int) and g < 2 else tail_ps)[0:HQ * KT, 0:P]

                def then(n, ins):
                    ins.then_inc(m_chain, 1)
                    dve.wait_ge(m_chain, 4 * g + n)
                then(1, dve.tensor_copy(mparts[:, 0, :], src))
                then(2, dve.tensor_tensor(mrest[:, :], src, mparts[:, 0, :], ALU.subtract))
                then(3, dve.tensor_copy(mparts[:, 1, :], mrest[:, :]))
                then(4, dve.tensor_tensor(mrest[:, :], mrest[:, :], mparts[:, 1, :], ALU.subtract))
                dve.tensor_copy(mparts[:, 2, :], mrest[:, :]).then_inc(m_sb, 1)

            def exp_normalise(k, par):
                g = 2 * k + par
                got = tail_ps[:, :].rearrange("p (i h w) -> p i h w", i=KT, w=VW)
                d3 = den[:, :].rearrange("p (i h) -> p i h", h=HQ)
                dve.wait_ge(e_turned, g + 1)
                dve.reciprocal(d3, got[:, :, :, D]).then_inc(e_chain, 1)
                dve.wait_ge(e_chain, g + 1)
                dve.tensor_tensor(y_of(k, par), got[:, :, :, 0:D],
                                  d3.unsqueeze(3).broadcast_to([P, KT, HQ, D]), ALU.mult).then_inc(e_normed, 1)

            for i in range(2 * len(MAX)):
                g, n = divmod(i, len(MAX))
                dve.wait_ge(first_full, i + 1)
                maxima(g, n, banks[i % 6], dve.tensor_reduce, ALU.max, negate=True).then_inc(first_max, 1)
                if i == len(MAX) + FIRST_TURN - 1:
                    parts_of_max(0, 0)
            parts_of_max(1, 1)

            def max_quad(k, par, first=False):
                g = 2 * k + par
                if not first:
                    parts_of_max(g + 1, 1 - par)
                    exp_normalise(*before(k, par))
                for n in range(len(MAX)):
                    row_max_of(g + 2, par, n)

            max_quad(0, 0, first=True)
            max_quad(0, 1)
            with dve.Fori(1, NQ // 2 - 1) as j:
                max_quad(j, 0)
                max_quad(j, 1)
            parts_of_max(NQ - 1, 1)
            for g in range(NQ - 3, NQ):
                exp_normalise(g // 2, g % 2)
            layer_norm(2, lambda n: residual(1, n))

            dve.wait_ge(f_logits, CH)
            got1 = banks[0][:, 0:NT * E1].rearrange("p (i e) -> p i e", e=E1)
            link(dve.tensor_reduce(rowF[:, 0, :], got1, AX.X, ALU.max))
            dve.tensor_tensor(GG[:, :, :], got1, rowF[:, 0, :].unsqueeze(2).broadcast_to([P, NT, E1]),
                              ALU.subtract).then_inc(f_max, 1)
            dve.wait_ge(f_exp, 1)
            link(dve.tensor_reduce(rowF[:, 1, :], GG[:, :, :], AX.X, ALU.add))
            link(dve.reciprocal(rowF[:, 2, :], rowF[:, 1, :]))
            link(dve.tensor_tensor(GG[:, :, :], GG[:, :, :], rowF[:, 2, :].unsqueeze(2).broadcast_to([P, NT, E1]), ALU.mult))
            KF = F1 // P

            def hidden1(e, n, first):
                for m in range(KF):
                    c = KF * n + m
                    dve.wait_ge(f_act, CH * KF * e + c + 1)
                    if m == 0 and not (first and n < 2):
                        dve.wait_ge(f_y, CH * e + n - 1)
                    dve.tensor_tensor(hid_f[:, n % 2, m, :], act_f[:, c % 2, :], banks[2 * (c % 2) + 1],
                                      ALU.mult).then_inc(f_hid, 1)

            dve.wait_ge(masks_ready, 6)
            mine = GG[:, :, :].unsqueeze(3).broadcast_to([P, NT, E1, E1])
            other = GG[:, :, :].unsqueeze(2).broadcast_to([P, NT, E1, E1])
            dve.tensor_tensor(cmp_a[:, :, :, :], other, mine, ALU.is_gt)
            link(dve.tensor_tensor(cmp_b[:, :, :, :], other, mine, ALU.is_equal))
            hidden1(0, 0, True)
            low = lower[:, :, :].unsqueeze(1).broadcast_to([P, NT, E1, E1])
            link(dve.tensor_tensor(cmp_b[:, :, :, :], cmp_b[:, :, :, :], low, ALU.mult))
            link(dve.tensor_tensor(cmp_a[:, :, :, :], cmp_a[:, :, :, :], cmp_b[:, :, :, :], ALU.add))
            link(dve.tensor_reduce(rankF[:, :, :], cmp_a[:, :, :, :], AX.X, ALU.add))
            link(dve.scalar_tensor_tensor(GW[:, :, :], rankF[:, :, :], TOP - 0.5, GG[:, :, :], ALU.is_lt, ALU.mult))
            link(dve.tensor_reduce(rowF[:, 0, :], GW[:, :, :], AX.X, ALU.add))
            link(dve.reciprocal(rowF[:, 1, :], rowF[:, 0, :]))
            link(dve.tensor_tensor(WT[:, :, :], GW[:, :, :].rearrange("p i e -> p e i"),
                                   rowF[:, 1, :].unsqueeze(1).broadcast_to([P, E1, NT]), ALU.mult))
            def add_up(e, n, first):
                dve.wait_ge(f_y, CH * e + n + 1)
                if not first:
                    dve.wait_ge(f_acc, CH * e + n - 3)
                for i in range(CT):
                    t = n * CT + i
                    w = WT[:, e, t:t + 1] if isinstance(e, int) else WT[:, bass.ds(e, 1), t:t + 1].rearrange("p o t -> p (o t)")
                    before_it = X if first else Z
                    ins = dve.scalar_tensor_tensor(Z[:, t, :], banks[4 + n % 2][:, i * P:(i + 1) * P], w, before_it[:, t, :],
                                                   ALU.mult, ALU.add)
                ins.then_inc(f_acc, 1)

            def expert1(e, first=False, last=False):
                if not first:
                    hidden1(e, 0, first)
                for n in range(CH):
                    if n + 1 < CH:
                        hidden1(e, n + 1, first)
                    add_up(e, n, first)
                    if last:
                        dve.wait_ge(f_acc, CH * e + n + 1)
                        moments(3, n)

            expert1(0, first=True)
            with dve.Fori(1, E1 - 1) as e:
                expert1(e)
            expert1(E1 - 1, last=True)
            for n in range(CH):
                standardise(3, n)

        @block.gpsimd
        def _(pool):
            pool.wait_ge(consts, 1)
            pool.affine_select(out=ident[:, :], in_=ident[:, :], compare_op=ALU.is_equal, fill=0.0, base=0,
                               pattern=[[-1, P]], channel_multiplier=1).then_inc(consts, 1)
            pool.memset(upto[:, :], 1.0).then_inc(upto_ready, 1)
            pool.wait_ge(upto_ready, 1)
            pool.affine_select(out=upto[:, :], in_=upto[:, :], compare_op=ALU.is_ge, fill=0.0, base=0,
                               pattern=[[1, P]], channel_multiplier=-1).then_inc(upto_ready, 1)

            pool.memset(VS[:, :, :, :], 0.0).then_inc(upto_ready, 1)
            pool.wait_ge(upto_ready, 3)
            pool.memset(VS[:, :, :, :].rearrange("p a i (h w) -> p (a i h) w", w=VW)[:, :, D:D + 1], 1.0
                        ).then_inc(upto_ready, 1)

            def take_v(k, par):
                heads = slice(HQ * D * k, HQ * D * (k + 1)) if isinstance(k, int) else bass.ds(k * (HQ * D), HQ * D)
                pool.tensor_copy(VS[:, par, :, :].rearrange("p i (h w) -> p i h w", w=VW)[:, :, :, 0:D],
                                 Y[:, par, :, heads].rearrange("p i (h d) -> p i h d", d=D)).then_inc(v_ready, 1)

            def quad(g, par, after=None):
                for s in range(NS):
                    if s == 3 and after is not None:
                        at_least(pool, step_summed, NS * g)
                        take_v(after, 1 - par)
                    rp, width = (par + s) % 2, pieces(s)[1]
                    for h0, h1 in ((0, 2), (2, POOL_HEADS[s])):
                        if h0 < h1:
                            pool.wait_ge(mask_done, 2 * NS * g + 2 * s + h0 // 2 + 1)
                            ins = pool.tensor_tensor(R4[:, rp, h0:h1, 0:width], R4[:, rp, h0:h1, 0:width],
                                                     R4[:, rp, h0:h1, 0:width], ALU.mult)
                    ins.then_inc(fourth_pool, 1)

            pool.wait_ge(x_in, 16)
            pool.wait_ge(w_in, 16 * 7)
            pool.tensor_tensor(X[:, :, :], X[:, :, :], YT[:, 0, 0:P].unsqueeze(1).broadcast_to([P, NT, P]),
                               ALU.add).then_inc(res_in, 1)
            pool.wait_ge(upto_ready, 4)
            pool.wait_ge(v_sb, 1)
            take_v(0, 0)
            pool.wait_ge(v_sb, B)
            quad(0, 0, after=0)
            quad(1, 1, after=1)
            with pool.Fori(1, NQ // 2 - 1) as j:
                quad(2 * j, 0, after=j)
                quad(2 * j + 1, 1, after=j + 1)
            quad(NQ - 2, 0, after=NQ // 2 - 1)
            quad(NQ - 1, 1)

            pool.wait_ge(normed, NQ)

            def link(n, ins):
                ins.then_inc(pool_chain, 1)
                pool.wait_ge(pool_chain, n)
            pool.iota(iota_i[:, :], pattern=[[0, P // E0], [1, E0]], base=0, channel_multiplier=0)
            link(1, pool.memset(same_e[:, :], 0.0))
            for o in range(-(P // E0) + 1, P // E0):
                link(o + 8 + 1, pool.affine_select(out=same_e[:, :], in_=same_e[:, :], compare_op=ALU.not_equal, fill=1.0,
                                                   base=o * E0, pattern=[[-1, P]], channel_multiplier=1))
            link(17, pool.memset(own_e[:, :, :], 1.0))
            pool.affine_select(out=before_e[:, :], in_=same_e[:, :], compare_op=ALU.is_gt, fill=0.0, base=0,
                               pattern=[[1, P]], channel_multiplier=-1).then_inc(masks_ready, 1)
            link(18, pool.memset(rank_a[:, 0:P], 1.0))
            pool.affine_select(out=before_t[:, :], in_=rank_a[:, 0:P], compare_op=ALU.is_gt, fill=0.0, base=0,
                               pattern=[[1, P]], channel_multiplier=-1).then_inc(masks_ready, 1)
            link(19, pool.affine_select(out=own_e[:, :, :], in_=own_e[:, :, :], compare_op=ALU.is_ge, fill=0.0, base=0,
                                        pattern=[[-16, 8], [0, 16]], channel_multiplier=1))
            link(20, pool.affine_select(out=own_e[:, :, :], in_=own_e[:, :, :], compare_op=ALU.is_ge, fill=0.0, base=15,
                                        pattern=[[16, 8], [0, 16]], channel_multiplier=-1))
            link(21, pool.tensor_copy(is_e[:, :], own_e[:, :, 0]))
            link(22, pool.memset(own_hi[:, :, :], 0.0))
            for e in range(8):
                link(23 + e, pool.affine_select(out=own_hi[:, :, :], in_=own_hi[:, :, :], compare_op=ALU.not_equal,
                                                fill=1.0, base=-16 * e, pattern=[[-1, 16], [0, 8]],
                                                channel_multiplier=1))
            link(31, pool.tensor_copy(iota16[:, :], iota_i[:, 0:16]))
            link(32, pool.iota(iota_i[:, 0:NT], pattern=[[P, NT]], base=0, channel_multiplier=1))
            pool.tensor_copy(token[:, :], iota_i[:, 0:NT]).then_inc(masks_ready, 1)
            pool.wait_ge(masks_ready, 3)
            pool.nop().then_inc(masks_ready, 1)

            def carry_waits():
                pool.tensor_tensor(carrier[:, :], eps_ln[:, :], eps_ln[:, :], ALU.add)

            def gather(e, k):
                src = idx[:, e, :] if isinstance(e, int) else idx[:, bass.ds(e, 1), :].rearrange("p o h -> p (o h)")
                pool.tensor_copy(idx_in[:, k, :], src).then_inc(idx_ready, 1)

            def fetch(k):
                for h in range(NH):
                    pool.indirect_dma_start(out=G[:, k, h, :], out_offset=None, in_=xs_rows,
                                            in_offset=bass.IndirectOffsetOnAxis(ap=idx_in[:, k, h:h + 1].bitcast(U32), axis=0)
                                            ).then_inc(gathered[k], 16)

            def scatter(j, k):
                e = 4 * j + k
                src = idx[:, e, :] if isinstance(e, int) else idx[:, bass.ds(e, 1), :].rearrange("p o h -> p (o h)")
                pool.tensor_copy(idx_out[:, k, :], src).then_inc(idx_ready, 1)
                pool.wait_ge(idx_ready, 4 + (8 * j if not isinstance(j, int) or j < 3 else 24) + scat_at(j, k))
                pool.wait_ge(out_sb, e + 1)
                if not (isinstance(e, int) and e == 0):
                    pool.wait_ge(scattered, 16 * NH * e)
                carry_waits()
                for h in range(NH):
                    pool.indirect_dma_start(out=moe_rows, in_=out_e[:, k % 2, h, :], in_offset=None,
                                            out_offset=bass.IndirectOffsetOnAxis(ap=idx_out[:, k, h:h + 1].bitcast(U32), axis=0),
                                            compute_op=ALU.add).then_inc(scattered, 16)

            ORDER = [("g", 0), ("g", 1), ("s", 0), ("g", 2), ("s", 1), ("g", 3), ("s", 2), ("s", 3)]

            def scat_at(j, k):
                order = ORDER if not isinstance(j, int) or j < 3 else [o for o in ORDER if o[0] == "s"]
                return order.index(("s", k)) + 1

            pool.wait_ge(idx_sb, 1)
            pool.wait_ge(xs_out, 16 * 2)
            for k in range(4):
                gather(k, k)
            pool.wait_ge(idx_ready, 4)
            for k in range(4):
                fetch(k)
            pool.wait_ge(sh_out, 16 * CH)

            def four_experts(j):
                for n, (kind, k) in enumerate(ORDER):
                    if kind == "g":
                        pool.wait_ge(g_sb, 4 * j + k + 1)
                        gather(4 * j + 4 + k, k)
                        pool.wait_ge(idx_ready, 4 + 8 * j + n + 1)
                        carry_waits()
                        fetch(k)
                    else:
                        scatter(j, k)

            four_experts(0)
            with pool.Fori(1, E0 // 4 - 1) as j:
                four_experts(j)
            for k in range(4):
                scatter(E0 // 4 - 1, k)

            pool.wait_ge(w2_in, 16 * 6)
            pool.tensor_copy(identb[:, :], ident[:, :])
            link(33, pool.memset(mask_f[:, :], 0.0))
            pool.affine_select(out=mask[:, :], in_=mask_f[:, :], compare_op=ALU.is_ge, fill=NEG, base=0,
                               pattern=[[1, P]], channel_multiplier=-1).then_inc(masks_ready, 1)
            pool.wait_ge(masks_ready, 5)
            pool.memset(KE[64:96, :, :, :], 1.0).then_inc(ones_set, 1)
            pool.wait_ge(ones_set, 1)
            for par in range(2):
                pool.wait_ge(v_sb, B + par + 1)
                take_v(0, par)
            with pool.Fori(0, NQ // 2 - 1) as j:
                for par in range(2):
                    pool.wait_ge(exp_summed, NS * (2 * j + par + 1))
                    take_v(j + 1, par)
            pool.wait_ge(e_normed, NQ)
            link(34, pool.memset(lower[:, :, :], 1.0))
            pool.affine_select(out=lower[:, :, :], in_=lower[:, :, :], compare_op=ALU.is_gt, fill=0.0, base=0,
                               pattern=[[1, E1], [-1, E1]], channel_multiplier=0).then_inc(masks_ready, 1)


def _column_major(a):
    return a.reshape(a.shape[0], -1, HQ, D).transpose(0, 1, 3, 2).reshape(a.shape[0], -1)


_INS = {
    "x": ("L0_attn_x", lambda a: a.reshape(B * T, P)),
    "xT": ("L0_attn_x", lambda a: a.reshape(B * T, P).T),
    "w_qk": ("L0_attn_W_attn", lambda a: _column_major(a[:, 0:2 * P])),
    "w_v": ("L0_attn_W_attn", lambda a: a[:, 2 * P:3 * P]),
    "b_attn": ("L0_attn_b_attn", lambda a: a),
    "b_cols": ("L0_attn_b_attn", lambda a: _column_major(a[None, 0:2 * P]).reshape(2, P).T),
    "w_proj": ("L0_attn_W_proj", lambda a: a),
    "b_proj": ("L0_attn_b_proj", lambda a: a),
    "gain": ("L0_attn_score_gain", lambda a: a.reshape(1)),
    "gate_t": ("L0_ffn_gate_w", lambda a: a.T),
    "wg_t": ("L0_ffn_Wg", lambda a: a.transpose(0, 2, 1)),
    "wu_t": ("L0_ffn_Wu", lambda a: a.transpose(0, 2, 1)),
    "wd_t": ("L0_ffn_Wd", lambda a: a.transpose(0, 2, 1)),
    "sg_t": ("L0_ffn_Sg", lambda a: a.T),
    "su_t": ("L0_ffn_Su", lambda a: a.T),
    "sd_t": ("L0_ffn_Sd", lambda a: a.T),
    "w_dq": ("L1_attn_W_dq", lambda a: a),
    "w_uq": ("L1_attn_W_uq", lambda a: _column_major(a)),
    "w_dkv": ("L1_attn_W_dkv", lambda a: a),
    "w_uk": ("L1_attn_W_uk", lambda a: _column_major(a)),
    "w_uv": ("L1_attn_W_uv", lambda a: a),
    "w_o": ("L1_attn_W_o", lambda a: a),
    "gate1": ("L1_ffn_Wg", lambda a: a),
    "w1": ("L1_ffn_W1", lambda a: a),
    "w3": ("L1_ffn_W3", lambda a: a),
    "w2": ("L1_ffn_W2", lambda a: a),
}


def kernel(**inputs):
    import numpy as _np
    import concourse.bacc as _bacc
    from concourse.bass_utils import run_bass_kernel_spmd as _run

    nc = _bacc.Bacc("TRN2", target_bir_lowering=False, num_devices=1)
    arrays, aps = {}, {}
    for name, (source, lay) in _INS.items():
        arr = _np.ascontiguousarray(lay(_np.asarray(inputs[source])))
        arrays[f"in_{name}"] = arr
        aps[name] = nc.dram_tensor(f"in_{name}", arr.shape, mybir.dt.from_np(arr.dtype), kind="ExternalInput").ap()
    out = nc.dram_tensor("out_x", (B * T, P), F32, kind="ExternalOutput").ap()
    build(nc, aps, out)
    r = _run(nc, [arrays], core_ids=[0])
    return r.results[0]["out_x"].reshape(B, T, P)
```
